# Optimizing a Trainium2 kernel written in Bass

```python
import numpy as np
import jax
import jax.numpy as jnp

def _softmax(x, axis=-1):
    return jax.nn.softmax(x, axis=axis)

def _gelu(x):
    return jax.nn.gelu(x, approximate=True)

def _silu(x):
    return jax.nn.silu(x)

def _sigmoid(x):
    return jax.nn.sigmoid(x)

def _layernorm(x, axis=-1, eps=1e-05):
    m = jnp.mean(x, axis=axis, keepdims=True)
    v = jnp.var(x, axis=axis, keepdims=True)
    return (x - m) / jnp.sqrt(v + eps)

def _scatter_add(tgt, idx, src, axis=0):
    return tgt.at[idx].add(src)

def _segment_sum(src, seg, n):
    return jax.ops.segment_sum(src, seg, n)
kernel_name = 'mk_adaln_d1_jaxref_r8_cdbb3a'

def setup_inputs(seed: int=0):
    np.random.seed(seed)
    _w = jnp.asarray

    def _L0_attn_setup():
        import jax, jax.numpy as jnp
        import numpy as np
        B, S, HID, QK, H = (2, 256, 256, 256, 16)
        DK, DV = (QK // H, HID // H)
        EPS = 1e-05
        key = jax.random.key(seed)
        ks = jax.random.split(key, 8)
        sd = 1.0 / np.sqrt(HID)
        inp = {'x': jax.random.normal(ks[0], (B, S, HID), jnp.float32), 'wq': jax.random.normal(ks[1], (HID, QK), jnp.float32) * sd, 'bq': jnp.zeros((QK,), jnp.float32), 'wk': jax.random.normal(ks[2], (HID, QK), jnp.float32) * sd, 'bk': jnp.zeros((QK,), jnp.float32), 'wv': jax.random.normal(ks[3], (HID, HID), jnp.float32) * sd, 'bv': jnp.zeros((HID,), jnp.float32), 'wg': jax.random.normal(ks[4], (HID, HID), jnp.float32) * sd, 'bg': jnp.zeros((HID,), jnp.float32), 'wo': jax.random.normal(ks[5], (HID, HID), jnp.float32) * sd, 'bo': jnp.zeros((HID,), jnp.float32), 'gn_w': jnp.ones((HID,), jnp.float32), 'gn_b': jnp.zeros((HID,), jnp.float32), 'gamma': 1.0 - jnp.exp(jnp.linspace(-np.log(32.0), -np.log(512.0), H)).astype(jnp.float32)}
        return inp
    _L0_attn_in = _L0_attn_setup()

    def _L0_ffn_setup():
        import jax, jax.numpy as jnp
        import numpy as np
        NUM_EXPERTS = 8
        TOP_K = 2
        EMB = 256
        MLP = 512
        B, S = (4, 128)
        key = jax.random.key(seed)
        ks = jax.random.split(key, 5)
        scale_x = 1.0
        return {'x': jax.random.normal(ks[0], (B, S, EMB), dtype=jnp.float32), 'gate_kernel': jax.random.normal(ks[1], (EMB, NUM_EXPERTS), dtype=jnp.float32) / np.sqrt(EMB), 'w0_kernel': jax.random.normal(ks[2], (NUM_EXPERTS, EMB, MLP), dtype=jnp.float32) / np.sqrt(EMB), 'w1_kernel': jax.random.normal(ks[3], (NUM_EXPERTS, EMB, MLP), dtype=jnp.float32) / np.sqrt(EMB), 'wo_kernel': jax.random.normal(ks[4], (NUM_EXPERTS, MLP, EMB), dtype=jnp.float32) / np.sqrt(MLP)}
    _L0_ffn_in = _L0_ffn_setup()
    _L0_c = _w((lambda *s: np.random.randn(*s).astype(np.float32) * 0.05)(4, 256))
    _L0_wmod = _w((lambda *s: np.random.randn(*s).astype(np.float32) * 0.05)(256, 6 * 256) * 256 ** (-0.5))
    _d = {'L0_attn_x': _L0_attn_in['x'], 'L0_attn_wq': _L0_attn_in['wq'], 'L0_attn_bq': _L0_attn_in['bq'], 'L0_attn_wk': _L0_attn_in['wk'], 'L0_attn_bk': _L0_attn_in['bk'], 'L0_attn_wv': _L0_attn_in['wv'], 'L0_attn_bv': _L0_attn_in['bv'], 'L0_attn_wg': _L0_attn_in['wg'], 'L0_attn_bg': _L0_attn_in['bg'], 'L0_attn_wo': _L0_attn_in['wo'], 'L0_attn_bo': _L0_attn_in['bo'], 'L0_attn_gn_w': _L0_attn_in['gn_w'], 'L0_attn_gn_b': _L0_attn_in['gn_b'], 'L0_attn_gamma': _L0_attn_in['gamma'], 'L0_ffn_gate_kernel': _L0_ffn_in['gate_kernel'], 'L0_ffn_w0_kernel': _L0_ffn_in['w0_kernel'], 'L0_ffn_w1_kernel': _L0_ffn_in['w1_kernel'], 'L0_ffn_wo_kernel': _L0_ffn_in['wo_kernel'], 'L0_c': _L0_c, 'L0_wmod': _L0_wmod}
    _x0 = _d['L0_attn_x']
    _d['L0_attn_x'] = jax.random.normal(jax.random.fold_in(jax.random.key(seed), 1), (4, 512, 256), dtype=_x0.dtype)
    del _x0
    return _d

def reference(L0_attn_x, L0_attn_wq, L0_attn_bq, L0_attn_wk, L0_attn_bk, L0_attn_wv, L0_attn_bv, L0_attn_wg, L0_attn_bg, L0_attn_wo, L0_attn_bo, L0_attn_gn_w, L0_attn_gn_b, L0_attn_gamma, L0_ffn_gate_kernel, L0_ffn_w0_kernel, L0_ffn_w1_kernel, L0_ffn_wo_kernel, L0_c, L0_wmod):

    def _L0_attn_ref(x, wq, bq, wk, bk, wv, bv, wg, bg, wo, bo, gn_w, gn_b, gamma):
        import jax, jax.numpy as jnp
        import numpy as np
        B, S, HID, QK, H = (2, 256, 256, 256, 16)
        DK, DV = (QK // H, HID // H)
        EPS = 1e-05
        b, s, hid = x.shape
        h = gamma.shape[0]
        dk = wq.shape[1] // h
        dv = hid // h
        q = (x @ wq + bq).reshape(b, s, h, dk).transpose(0, 2, 1, 3)
        k = (x @ wk + bk).reshape(b, s, h, dk).transpose(0, 2, 1, 3)
        v = (x @ wv + bv).reshape(b, s, h, dv).transpose(0, 2, 1, 3)
        idx = jnp.arange(s)
        diff = idx[:, None] - idx[None, :]
        expn = jnp.maximum(diff, 0).astype(x.dtype)
        dmask = jnp.where(diff >= 0, gamma[:, None, None] ** expn, 0.0)
        scores = jnp.einsum('bhnd,bhmd->bhnm', q, k) * dmask
        ret = jnp.einsum('bhnm,bhmv->bhnv', scores, v)
        mean = ret.mean(axis=(2, 3), keepdims=True)
        var = ((ret - mean) ** 2).mean(axis=(2, 3), keepdims=True)
        norm = (ret - mean) * jax.lax.rsqrt(var + EPS)
        norm = norm * gn_w.reshape(h, dv)[None, :, None, :] + gn_b.reshape(h, dv)[None, :, None, :]
        ro = norm.transpose(0, 2, 1, 3).reshape(b, s, hid)
        gate = jax.nn.silu(x @ wg + bg)
        out = gate * ro @ wo + bo
        return out

    def _L0_ffn_ref(x, gate_kernel, w0_kernel, w1_kernel, wo_kernel):
        import jax, jax.numpy as jnp
        import numpy as np
        NUM_EXPERTS = 8
        TOP_K = 2
        EMB = 256
        MLP = 512
        B, S = (4, 128)
        gate_logits = jnp.einsum('bsd,de->bse', x, gate_kernel)
        top_k_weights, top_k_indices = jax.lax.top_k(gate_logits, TOP_K)
        top_k_weights = jax.nn.softmax(top_k_weights.astype(jnp.float32), axis=-1).astype(x.dtype)
        one_hot = jax.nn.one_hot(top_k_indices, NUM_EXPERTS, dtype=x.dtype)
        combine = jnp.einsum('bsk,bske->bse', top_k_weights, one_hot)
        h0 = jnp.einsum('bsd,edm->bsem', x, w0_kernel)
        h1 = jnp.einsum('bsd,edm->bsem', x, w1_kernel)
        inter = jax.nn.silu(h0) * h1
        out = jnp.einsum('bse,bsem,emd->bsd', combine, inter, wo_kernel)
        return out
    x = L0_attn_x
    mod = (_silu(L0_c) @ L0_wmod).reshape(L0_c.shape[0], 6, 1, -1)
    sa, ca, ga, sb, cb, gb = (mod[:, 0], mod[:, 1], mod[:, 2], mod[:, 3], mod[:, 4], mod[:, 5])
    ga = (2 * (ga >= 0) - 1) * jnp.maximum(jnp.abs(ga), 0.25)
    gb = (2 * (gb >= 0) - 1) * jnp.maximum(jnp.abs(gb), 0.25)
    h = _layernorm(x, axis=-1) * (1 + ca) + sa
    x = x + ga * _L0_attn_ref(h, L0_attn_wq, L0_attn_bq, L0_attn_wk, L0_attn_bk, L0_attn_wv, L0_attn_bv, L0_attn_wg, L0_attn_bg, L0_attn_wo, L0_attn_bo, L0_attn_gn_w, L0_attn_gn_b, L0_attn_gamma)
    h = _layernorm(x, axis=-1) * (1 + cb) + sb
    x = x + gb * _L0_ffn_ref(h, L0_ffn_gate_kernel, L0_ffn_w0_kernel, L0_ffn_w1_kernel, L0_ffn_wo_kernel)
    return x

_drawn_inputs = setup_inputs


def setup_inputs(seed=0):
    import zlib

    import numpy as np

    out = dict(_drawn_inputs(seed))
    spreads = {'L0_attn_bq': (0.0, 0.45),
     'L0_attn_bk': (0.0, 0.39),
     'L0_attn_bv': (0.0, 0.381),
     'L0_attn_bg': (0.0, 0.438),
     'L0_attn_bo': (0.0, 0.286),
     'L0_attn_gn_w': (1.0, 0.2),
     'L0_attn_gn_b': (0.0, 0.416)}
    factors = {}
    for name, (base, spread) in spreads.items():
        noise = np.random.default_rng([zlib.crc32(name.encode()), seed]).standard_normal(out[name].shape)
        drawn = base * np.exp(spread * noise) if base else spread * noise
        out[name] = jnp.asarray(drawn.astype(out[name].dtype))
    for name, factor in factors.items():
        out[name] = (out[name] * factor).astype(out[name].dtype)
    return out
```

```python
from contextlib import ExitStack

import concourse.bass as bass
from concourse import mybir

F32 = mybir.dt.float32
I32 = mybir.dt.int32
U32 = mybir.dt.uint32
ALU = mybir.AluOpType
ACT = mybir.ActivationFunctionType
AX = mybir.AxisListType

P = 128
B, S, D = 4, 512, 256
H, DH = 16, 16
FT = D // P
HPT = H // FT
NC = S // P
NTOK = B * S
E, F = 8, 512
KF = F // P
TOPK = 2
EPS = 1e-5
COMB, TOK, BAT, ROW = D, D + E, D + E + 1, D + E + 2
META = ROW - D
REGION = NTOK + P
PAD_ROW = E * REGION
N_TILES = (NTOK * TOPK + E * (P - 1)) // P
WE = FT * F * 2 + KF * D

FRONT = [("hT0", "act"), ("hT1", "act"), ("q0", "act"), ("q1", "act"), ("k0", "act"), ("k1", "act"),
         ("g0", "act"), ("g1", "act"), ("v01", "dve"), ("v23", "dve"), ("kd01", "dve"), ("kd2", "dve")]
TAIL = [("st0", "dve"), ("st1", "dve"), ("st2", "dve"), ("gn", "dve"), ("wo01", "dve"), ("wo23", "dve"),
        ("h2T0", "act"), ("h2T1", "act"), ("logits", "dve"), ("rank", "dve")]
CREDIT = 2


class Ring:

    def __init__(self, items, banks, full, drained):
        self.names = [n for n, _ in items]
        self.who = [w for _, w in items]
        self.banks, self.full, self.drained = banks, full, drained

    def bank(self, name):
        return self.banks[self.names.index(name) % 2]

    def filled(self, b, name):
        return b * len(self.names) + (self.names.index(name) + 1)

    def drains(self, b, name):
        i = self.names.index(name)
        w = self.who[i]
        return self.drained[w], b * self.who.count(w) + (CREDIT + self.who[:i + 1].count(w))

    def free(self, b, name):
        i = self.names.index(name)
        if i >= 2:
            return self.drains(b, self.names[i - 2])
        w = self.who[i - 2]
        return self.drained[w], b * self.who.count(w) + (CREDIT - (1 - i))


def adaln_block(nc, x, wq, bq, wk, bk, wv, bv, wg, bg, wo, bo, gn_w, gn_b, gamma,
                gate_k, w0, w1, wo_e, c, wmod, out):
    ctx = ExitStack()
    with ctx:
        def sb(name, shape, dt=F32):
            return ctx.enter_context(nc.sbuf_tensor(name, shape, dt))

        def sem(name):
            return ctx.enter_context(nc.semaphore(name))

        ctx.enter_context(nc.allow_non_contiguous_dma(reason="small vectors"))

        routed = nc.dram_tensor("routed", [PAD_ROW + P, ROW], F32, kind="Internal").ap()
        gb_dram = nc.dram_tensor("gb_dram", [B, D], F32, kind="Internal").ap()

        xs = sb("xs", [P, B * NC, D])
        wq_s, wk_s, wv_s, wg_s, wo_s = (sb(n, [P, FT, D]) for n in ("wq_s", "wk_s", "wv_s", "wg_s", "wo_s"))
        gate_s = sb("gate_s", [P, FT, E])
        we = sb("we", [P, E, WE])
        wmod_s = we[:, E - 1, :].rearrange("p (k n) -> p k n", k=FT)
        siluT = sb("siluT", [P, FT, B])
        bq_s, bk_s, bg_s, bgh_s, gnw_s, gnb_s, gcol = (
            sb(n, [P, FT]) for n in ("bq_s", "bk_s", "bg_s", "bgh_s", "gnw_s", "gnb_s", "gcol"))
        bv_bc, bo_bc = sb("bv_bc", [P, D]), sb("bo_bc", [P, D])
        gam_bc = sb("gam_bc", [P, H])
        ident, tri, ones, blk, blkavg = (sb(n, [P, P]) for n in ("ident", "tri", "ones", "blk", "blkavg"))
        hmask = sb("hmask", [P, HPT])
        mhalf = sb("mhalf", [P, NC])
        erow_i, erow = sb("erow_i", [P, E], I32), sb("erow", [P, E])
        ebase_i, ebase = sb("ebase_i", [P, E], I32), sb("ebase", [P, E])
        tokid = sb("tokid", [P, B * NC], I32)
        batid = sb("batid", [P, B * NC], I32)
        tmpl = sb("tmpl", [P, ROW])
        saT, ca1T = sb("saT", [P, FT, B]), sb("ca1T", [P, FT, B])
        gsc = sb("gsc", [P, B, 3 * D])
        dmask = sb("dmask", [P, H, P])
        qdec = sb("qdec", [P, FT, P + 1])
        kdec = sb("kdec", [P, H])
        st1, mv1, ve1, rs1 = sb("st1", [P, NC, 6]), sb("mv1", [P, NC, 2]), sb("ve1", [P, NC]), sb("rs1", [P, NC])
        xn = sb("xn", [P, NC, D])
        hT = sb("hT", [P, FT, S])
        qT, kT, qd = sb("qT", [P, FT, S]), sb("kT", [P, FT, S]), sb("qd", [P, FT, S])
        qx = sb("qx", [P, FT, HPT * P])
        vx = sb("vx", [P, NC, 2 * D])
        kd = xn
        z = sb("z", [P, FT, S])
        sm = sb("sm", [P, 4, 4 * P])
        th, ro = sm[:, 0:2, :], sm[:, 2:4, :]
        bog = sm[:, 2, 0:D]
        stt = xn[:, NC - 1, :].rearrange("p (k n) -> p k n", k=FT)
        state = sb("state", [P, FT, P])
        gst, gmv, gav, gd, gd2, gve, grs, gA, gt, gB = (
            sb("gst", [P, FT, 6]), sb("gmv", [P, FT, 2]), sb("gav", [P, FT, 2]), sb("gd", [P, FT]),
            sb("gd2", [P, FT]), sb("gve", [P, FT]), sb("grs", [P, FT]), sb("gA", [P, FT]),
            sb("gt", [P, FT]), sb("gB", [P, FT]))
        xt = [qd[:, u, :].rearrange("p (t d) -> p t d", t=2) for u in range(2)]
        st2, mv2, ve2, rs2 = sb("st2", [P, NC, 6]), sb("mv2", [P, NC, 2]), sb("ve2", [P, NC]), sb("rs2", [P, NC])
        h2 = sb("h2", [P, NC, ROW])
        h2T = hT
        modrow = sm[0:B, 0:2, :].rearrange("b a n -> b (a n)")
        msgn = sm[0:B, 2, :].rearrange("b (m d) -> b m d", m=2)
        mmag = sm[0:B, 3, :].rearrange("b (m d) -> b m d", m=2)
        zeros = h2[:, 0, 0:P]
        c_s, c_t = kT[0:B, 0, 0:D], kT[0:B, 1, 0:D]
        sel = qx[0:B, 0, 0:B * P].rearrange("b (c p) -> b c p", c=B)
        lg, mx, ix = sb("lg", [P, NC, E]), sb("mx", [P, NC, 8]), sb("ix", [P, NC, 8], U32)
        ixf, oh, msk, cmb = (sb("ixf", [P, NC, 2]), sb("oh", [P, 2, NC, E]), sb("msk", [P, NC, E]),
                             sb("cmb", [P, 2, NC, E]))
        vd, vt, pk = sb("vd", [P, NC]), sb("vt", [P, NC]), sb("pk", [P, 2, NC])
        carry = sb("carry", [P, NC + 1, E])
        pos, posk, posf = sb("pos", [P, NC, E]), sb("posk", [P, 2, NC, E]), sb("posf", [P, 2, NC])
        idx = sb("idx", [P, 2, NC], I32)
        cnt, cnti, tls, stc, enc, bas = (sb("cnt", [E, 1]), sb("cnti", [E, 1], I32), sb("tls", [E, 1]),
                                         sb("stc", [E, 1]), sb("enc", [E, 1]), sb("bas", [E, 1]))
        ecol_i, ecol, tile_i, tile_f = (sb("ecol_i", [E, 1], I32), sb("ecol", [E, 1]),
                                        sb("tile_i", [E, N_TILES], I32), sb("tile_f", [E, N_TILES]))
        ge, ine, row0 = (z[0:E, 0, 64 * u:64 * u + N_TILES] for u in range(3))
        tab = z[0:E, 1, 0:2 * N_TILES].rearrange("e (a n) -> e a n", a=2)
        tabi = sb("tabi", [1, 2, N_TILES], I32)
        padr, padi = sb("padr", [1, E]), sb("padi", [1, E], I32)
        rows = [h2[:, 0, :], h2[:, 1, :]]
        rT = [xn[:, 2 * u, :].rearrange("p (k n) -> p k n", k=FT) for u in range(2)]
        eth = [sm[:, u, :] for u in range(2)]
        ein = [sm[:, 2 + u, :] for u in range(2)]
        eit = [qx[:, u, 0:F].rearrange("p (k n) -> p k n", k=KF) for u in range(2)]
        ey = [hT[:, u, 0:D] for u in range(2)]
        gbr = [hT[:, u, D:2 * D] for u in range(2)]
        meta = [sb(f"meta{u}", [P, META]) for u in range(4)]

        ps = [ctx.enter_context(nc.psum_tensor(f"ps{i}", [P, 512], F32)) for i in range(8)]
        ret = [ps[0], ps[1]]
        sc = [ps[2], ps[3]]
        front = Ring(FRONT, [ps[4], ps[5]], sem("front_full"), {"act": sem("front_act"), "dve": sem("front_dve")})
        tail = Ring(TAIL, [ps[6], ps[7]], sem("tail_full"), {"act": sem("tail_act"), "dve": sem("tail_dve")})

        def sems(names):
            return [sem(n) for n in names.split()]

        c_in, x_in, wmod_in, small_in, w_in, wo_in, we_in = sems("c_in x_in wmod_in small_in w_in wo_in we_in")
        const_zero, const_ready, tmpl_ready, dve_const = sems("const_zero const_ready tmpl_ready dve_const")
        setup_chain, front_chain, chunk_chain, tail_chain, table_chain = sems(
            "setup_chain front_chain chunk_chain tail_chain table_chain")
        tanh_c, silu_ready, setup_pe, modT_ready, modrow_ready, gsc_ready, setup_done = sems(
            "tanh_c silu_ready setup_pe modT_ready modrow_ready gsc_ready setup_done")
        gb_out, tmpl_out = sems("gb_out tmpl_out")
        var1, rstd1, xn_ready, qd_ready, qx_ready, z_ready = sems("var1 rstd1 xn_ready qd_ready qx_ready z_ready")
        scored, masked, pv_done, state_up = sems("scored masked pv_done state_up")
        gn_stat, gn_full, gn_dev, grstd, gn_ab, ro_ready, prod_ready = sems(
            "gn_stat gn_full gn_dev grstd gn_ab ro_ready prod_ready")
        x2_ready, x2_out, var2, rstd2, h2_ready, row_ready = sems("x2_ready x2_out var2 rstd2 h2_ready row_ready")
        vd_ready, vt_ready, msk_ready, idx_ready, scattered, h2_free = sems(
            "vd_ready vt_ready msk_ready idx_ready scattered h2_free")
        pad_ready, pad_out, tls_ready, table_pe, tab_ready = sems("pad_ready pad_out tls_ready table_pe tab_ready")
        row_in, gbr_in = sems("row_in0 row_in1"), sems("gbr_in0 gbr_in1")
        rt_full, rt_dve, row_used, up0_full, up1_full, th_done, in_done, it_full, it_act, dn_full, y_done = sems(
            "rt_full rt_dve row_used up0_full up1_full th_done in_done it_full it_act dn_full y_done")
        added, added_ok, pool_passed, dve_passed = sems("added added_ok pool_passed dve_passed")
        SMALL, CONSTS = 16 * 10, 13
        N_FRONT_CHAIN, N_TAIL_CHAIN = 14, 46
        BC_BANKS = [ps[6], ps[7], ps[0], ps[1]]
        BC_HALVES = [ps[4][:, 0:D], ps[4][:, D:2 * D], ps[5][:, 0:D], ps[5][:, D:2 * D]]

        def row_loads(i, s):
            if isinstance(i, int):
                return i // 2 + 1
            return loop_loads[0] + s // 2 + 1

        def gbr_value(i, s):
            return gbr_in[s % 2], 16 * row_loads(i, s)

        loop_loads = [None]

        def run_steps(eng, step):
            lead = 2
            loops = (N_TILES - 1 - lead) // 4
            for i in range(lead):
                step(i, i)
            with eng.Fori(0, loops) as j:
                loop_loads[0] = 2 * j
                for s in range(lead, lead + 4):
                    step(4 * j + s, s)
            for i in range(lead + 4 * loops, N_TILES + 2):
                step(i, i)

        def heads(ap, pairs):
            base = [list(d) for d in ap.ap]
            return bass.AP(ap.tensor, ap.offset, [base[0], [4 * DH, pairs], [3 * DH, 2], [1, DH]])

        x_v = x.rearrange("b (t p) d -> b p t d", p=P)
        out_v = out[0:NTOK, :].rearrange("(b t p) d -> b p t d", p=P, t=NC)
        wk_v = lambda w: w.rearrange("(k p) n -> p k n", p=P)
        col = lambda v: v.rearrange("(k p) -> p k", p=P)
        wmod_v = wk_v(wmod)
        we_v = [(0, w0, FT, F), (FT * F, w1, FT, F), (2 * FT * F, wo_e, KF, D)]
        w0e = lambda e, k: we[:, e, k * F:(k + 1) * F]

        def wait(eng, pair):
            eng.wait_ge(pair[0], pair[1])

        def settle(eng, pairs, passed):
            for s, v in pairs:
                eng.wait_ge(s, v)
            eng.sem_inc(passed, 1)

        def grp(b, n):
            return b * (4 * NC) + n

        block = ctx.enter_context(nc.Block())

        @block.sync
        def _(sp):
            def load_x(b):
                if b:
                    sp.wait_ge(x_in, 16 * b)
                sp.dma_start(xs[:, b * NC:(b + 1) * NC, :], x_v[b]).then_inc(x_in, 16)

            def load_expert(e):
                for o, w, k, n in we_v:
                    sp.dma_start(we[:, e, o:o + k * n].rearrange("p (k n) -> p k n", k=k),
                                 w[e].rearrange("(k p) n -> p k n", p=P)).then_inc(we_in, 16)

            sp.dma_start(c_s, c).then_inc(c_in, 16)
            load_x(0)
            sp.dma_start(wmod_s, wmod_v).then_inc(wmod_in, 16)
            for s, d in ((wq_s, wq), (wk_s, wk), (wg_s, wg), (wv_s, wv)):
                sp.dma_start(s[:, :, :], wk_v(d)).then_inc(w_in, 16)
            load_x(1)
            sp.dma_start(wo_s[:, :, :], wk_v(wo)).then_inc(wo_in, 16)
            sp.dma_start(gate_s[:, :, :], wk_v(gate_k)).then_inc(wo_in, 16)
            load_x(2)
            load_expert(0)
            load_x(3)
            for e in range(1, E - 1):
                load_expert(e)
            sp.wait_ge(setup_pe, 3)
            load_expert(E - 1)
            sp.wait_ge(tmpl_ready, 1)
            sp.dma_start(routed[PAD_ROW:PAD_ROW + P, :], tmpl[:, :]).then_inc(tmpl_out, 16)
            with sp.Fori(0, B) as b:
                sp.wait_ge(x2_ready, 2 * b + 2)
                sp.dma_start(out_v[bass.ds(b, 1)].rearrange("b p t d -> p (b t) d"),
                             xs[:, bass.ds(b * NC, NC), :]).then_inc(x2_out, 16)
            sp.wait_ge(pad_ready, 1)
            for e in range(E):
                r = sp.value_load(padi[0:1, e:e + 1], min_val=0, max_val=PAD_ROW - P)
                sp.dma_start(routed[bass.ds(r, P), :], tmpl[:, :]).then_inc(pad_out, 16)
            sp.wait_ge(tab_ready, 2)
            sp.wait_ge(tmpl_out, 16)
            sp.wait_ge(pad_out, 16 * E)
            sp.wait_ge(scattered, 16 * TOPK * NC * B)

            def load_rows(i, s, n):
                r = sp.value_load(tabi[0:1, 0, bass.ds(i, 1)], min_val=0, max_val=PAD_ROW)
                sp.wait_ge(row_used, i + 1)
                sp.dma_start(rows[s % 2], routed[bass.ds(r, P), :]).then_inc(row_in[s % 2], 16)

            with sp.Fori(0, N_TILES // 4) as j:
                for s in range(4):
                    load_rows(4 * j + s, s, 2 * j + s // 2)
            for i in range(N_TILES // 4 * 4, N_TILES):
                load_rows(i, i, i // 2)
            sp.wait_ge(x2_out, 16 * B)
            sp.wait_ge(gb_out, 16)
            sp.wait_ge(added, 16 * N_TILES)

        @block.gpsimd
        def _(pool):
            g = nc.gpsimd
            for t, value in ((ident[:, :], 0.0), (tri[:, :], 1.0), (blk[:, :], 1.0), (hmask[:, :], 1.0),
                             (sel, 0.0), (tmpl[:, :], 0.0)):
                last = g.memset(t, value)
            last.then_inc(const_zero, 1)
            pool.wait_ge(const_zero, 1)
            g.affine_select(out=ident[:, :], in_=ident[:, :], compare_op=ALU.not_equal, fill=1.0, base=0,
                            pattern=[[-1, P]], channel_multiplier=1).then_inc(const_ready, 1)
            g.affine_select(out=sel, in_=sel, compare_op=ALU.not_equal, fill=1.0, base=0,
                            pattern=[[-1, B], [0, P]], channel_multiplier=1).then_inc(const_ready, 1)
            g.affine_select(out=tri[:, :], in_=tri[:, :], compare_op=ALU.is_gt, fill=0.0, base=0,
                            pattern=[[1, P]], channel_multiplier=-1).then_inc(const_ready, 1)
            blk3 = blk[:, :].rearrange("p (h d) -> p h d", d=DH)
            g.affine_select(out=blk3, in_=blk3, compare_op=ALU.is_ge, fill=0.0, base=0,
                            pattern=[[-DH, HPT], [0, DH]], channel_multiplier=1).then_inc(const_ready, 1)
            g.affine_select(out=hmask[:, :], in_=hmask[:, :], compare_op=ALU.is_ge, fill=0.0, base=0,
                            pattern=[[-DH, HPT]], channel_multiplier=1).then_inc(const_ready, 1)
            pool.wait_ge(const_ready, 5)
            g.affine_select(out=blk3, in_=blk3, compare_op=ALU.is_ge, fill=0.0, base=DH - 1,
                            pattern=[[DH, HPT], [0, DH]], channel_multiplier=-1).then_inc(const_ready, 1)
            g.affine_select(out=hmask[:, :], in_=hmask[:, :], compare_op=ALU.is_ge, fill=0.0, base=DH - 1,
                            pattern=[[DH, HPT]], channel_multiplier=-1).then_inc(const_ready, 1)
            g.iota(erow_i[:, :], [[1, E]], base=0, channel_multiplier=0).then_inc(const_ready, 1)
            g.iota(ebase_i[:, :], [[REGION, E]], base=0, channel_multiplier=0).then_inc(const_ready, 1)
            g.iota(tokid[:, :], [[P, B * NC]], base=0, channel_multiplier=1).then_inc(const_ready, 1)
            g.iota(batid[:, :].rearrange("p (b t) -> p b t", b=B), [[1, B], [0, NC]], base=0,
                   channel_multiplier=0).then_inc(const_ready, 1)
            g.iota(ecol_i[:, :], [[0, 1]], base=0, channel_multiplier=1).then_inc(const_ready, 1)
            g.iota(tile_i[:, :], [[1, N_TILES]], base=0, channel_multiplier=0).then_inc(const_ready, 1)
            g.iota(tmpl[:, TOK:TOK + 1].bitcast(I32), [[0, 1]], base=NTOK, channel_multiplier=1).then_inc(tmpl_ready, 1)

            def rstd(b, ready, done, ve, rs, n, per=1):
                pool.wait_ge(ready, b + 1)
                g.tensor_tensor(rs[:, :], ve[:, :], mhalf[:, 0:n], ALU.pow).then_inc(done, 1)

            def expand_q(b, c):
                for ft in range(FT):
                    if c == 0:
                        wait(pool, front.drains(b, f"q{ft}"))
                    pool.wait_ge(scored, grp(b, 4 + 4 * (c - 1) + 2 * ft + 2))
                    q = qT[:, ft, c * P:(c + 1) * P].unsqueeze(1).broadcast_to([P, HPT, P])
                    m = hmask[:, :].unsqueeze(2).broadcast_to([P, HPT, P])
                    g.tensor_tensor(qx[:, ft, :].rearrange("p (h n) -> p h n", h=HPT), q, m,
                                    ALU.mult).then_inc(qx_ready, 1)

            def pool_batch(b):
                rstd(b, var1, rstd1, ve1, rs1, NC)
                for c in range(NC):
                    expand_q(b, c)
                wait(pool, tail.drains(b, "gn"))
                g.tensor_tensor(grs[:, :], gve[:, :], mhalf[:, 0:FT], ALU.pow).then_inc(grstd, 1)
                rstd(b, var2, rstd2, ve2, rs2, NC)
                settle(pool, [(idx_ready, b + 1), (row_ready, b + 1)], pool_passed)
                for t in range(NC):
                    for k in range(TOPK):
                        g.indirect_dma_start(routed, bass.IndirectOffsetOnAxis(ap=idx[:, k, t:t + 1], axis=0),
                                             h2[:, t, :], None).then_inc(scattered, 16)
                pool.wait_ge(scattered, 16 * (TOPK * NC) * b + 16 * (TOPK * NC))
                pool.sem_inc(h2_free, 1)

            pool.wait_ge(dve_const, 2)
            pool.wait_ge(gsc_ready, 1 + 2 * B)
            pool.sem_inc(h2_free, 1)
            with pool.Fori(0, B) as b:
                pool_batch(b)

            def fetch_gb(i, s, n):
                settle(pool, [(row_used, i + 3), (y_done, i + 1)], pool_passed)
                g.indirect_dma_start(gbr[s % 2], None, gb_dram, bass.IndirectOffsetOnAxis(
                    ap=meta[s % 4][:, BAT - D:BAT - D + 1].bitcast(I32), axis=0)).then_inc(gbr_in[s % 2], 16)

            def add_rows(i, s, first=False, last=False):
                if not last:
                    fetch_gb(i + 1, s + 1, None)
                if not first:
                    pool.wait_ge(added, 16 * i)
                    pool.sem_inc(added_ok, 1)
                settle(pool, [(y_done, i + 3)], pool_passed)
                g.indirect_dma_start(out, bass.IndirectOffsetOnAxis(
                    ap=meta[s % 4][:, TOK - D:TOK - D + 1].bitcast(I32), axis=0), ey[s % 2], None,
                    compute_op=ALU.add).then_inc(added, 16)

            pool.sem_inc(added_ok, 4)
            pool.wait_ge(gb_out, 16)
            pool.wait_ge(x2_out, 16 * B)
            fetch_gb(0, 0, None)
            add_rows(0, 0, first=True)
            with pool.Fori(0, (N_TILES - 3) // 4) as j:
                for s in range(1, 5):
                    add_rows(4 * j + s, s)
            for i in range(N_TILES - 2, N_TILES):
                add_rows(i, i, last=i == N_TILES - 1)

        @block.scalar
        def _(act):
            a = nc.scalar
            for s, v in ((bq_s, bq), (bk_s, bk), (bg_s, bg), (gnw_s, gn_w), (gnb_s, gn_b)):
                act.dma_start(s[:, :], col(v)).then_inc(small_in, 16)
            act.dma_start(bv_bc[:, :], bv.partition_broadcast(P)).then_inc(small_in, 16)
            act.dma_start(bo_bc[:, :], bo.partition_broadcast(P)).then_inc(small_in, 16)
            act.dma_start(gam_bc[:, :], gamma.partition_broadcast(P)).then_inc(small_in, 16)
            for ft in range(FT):
                act.dma_start(gcol[:, ft:ft + 1], gamma[ft * HPT:(ft + 1) * HPT].unsqueeze(1).unsqueeze(2)
                              .broadcast_to([HPT, DH, 1])).then_inc(small_in, 16)
            act.wait_ge(c_in, 16)
            a.activation(c_t, c_s, ACT.Tanh, scale=0.5).then_inc(tanh_c, 1)
            act.wait_ge(small_in, SMALL)
            a.mul(bgh_s[:, :], bg_s[:, :], 0.5).then_inc(gsc_ready, 1)
            act.wait_ge(modrow_ready, 1)
            act.dma_start(gb_dram, modrow[:, 3 * D:4 * D]).then_inc(gb_out, 16)
            act.wait_ge(setup_pe, 3 + B)
            for b in range(B):
                a.copy(gsc[:, b, 0:512], BC_BANKS[b][:, :]).then_inc(gsc_ready, 1)
                a.copy(gsc[:, b, 512:3 * D], BC_HALVES[b]).then_inc(gsc_ready, 1)
            act.sem_inc(ro_ready, 2)
            act.wait_ge(gsc_ready, 1 + 2 * B)
            act.wait_ge(modT_ready, 2)

            def front_act(b):
                for ft in range(FT):
                    act.wait_ge(front.full, front.filled(b, f"hT{ft}"))
                    a.activation(hT[:, ft, :], front.bank(f"hT{ft}")[:, :], ACT.Identity,
                                 scale=ca1T[:, ft, bass.ds(b, 1)], bias=saT[:, ft, bass.ds(b, 1)])\
                        .then_inc(front.drained["act"], 1)
                for n, dst, bias in (("q", qT, bq_s), ("k", kT, bk_s)):
                    for ft in range(FT):
                        act.wait_ge(front.full, front.filled(b, f"{n}{ft}"))
                        a.activation(dst[:, ft, :], front.bank(f"{n}{ft}")[:, :], ACT.Identity,
                                     bias=bias[:, ft:ft + 1]).then_inc(front.drained["act"], 1)
                for ft in range(FT):
                    act.wait_ge(front.full, front.filled(b, f"g{ft}"))
                    a.activation(z[:, ft, :],
                                 front.bank(f"g{ft}")[:, :], ACT.Identity,
                                 bias=bg_s[:, ft:ft + 1]).then_inc(z_ready, 1)
                    a.activation(th[:, ft, :], front.bank(f"g{ft}")[:, :], ACT.Tanh, scale=0.5,
                                 bias=bgh_s[:, ft:ft + 1]).then_inc(front.drained["act"], 1)

            def tail_act(b):
                act.wait_ge(gn_ab, b + 1)
                for ft in range(FT):
                    a.activation(ro[:, ft, :], ret[ft][:, :], ACT.Identity, scale=gA[:, ft:ft + 1],
                                 bias=gB[:, ft:ft + 1]).then_inc(ro_ready, 1)
                for ft in range(FT):
                    act.wait_ge(tail.full, tail.filled(b, f"h2T{ft}"))
                    a.copy(h2T[:, ft, :], tail.bank(f"h2T{ft}")[:, :]).then_inc(tail.drained["act"], 1)
                act.wait_ge(vd_ready, b + 1)
                a.activation(vt[:, :], vd[:, :], ACT.Tanh, scale=0.5).then_inc(vt_ready, 1)

            act.sem_inc(tail.drained["act"], CREDIT)
            act.sem_inc(front.drained["act"], CREDIT)
            with act.Fori(0, B) as b:
                front_act(b)
                tail_act(b)

            act.sem_inc(it_act, 1)

            def turn_back(i, s):
                act.wait_ge(it_full, i + 3)
                act.wait_ge(dn_full, i + 1)
                a.copy(eit[s % 2], ps[5][:, :].rearrange("p (k n) -> p k n", k=KF)).then_inc(it_act, 1)

            def tanh_part(i, s):
                act.wait_ge(up0_full, i + 1)
                act.wait_ge(in_done, 2 * i + 2)
                a.activation(eth[s % 2], ps[2 * (s % 2)][:, :], ACT.Tanh, scale=0.5).then_inc(th_done, 1)

            def act_step(i, s):
                if not (isinstance(i, int) and not 0 <= i - 1 < N_TILES):
                    turn_back(i - 1, s - 1)
                if not (isinstance(i, int) and i >= N_TILES):
                    tanh_part(i, s)

            run_steps(act, act_step)

        @block.vector
        def _(dve):
            v = nc.vector

            class Chain:

                def __init__(self, s, per):
                    self.s, self.per, self.k = s, per, 0

                def start(self, b):
                    self.b, self.k = b, 0

                def inc(self, ins):
                    ins.then_inc(self.s, 1)
                    self.k += 1

                def value(self):
                    return self.s, self.b * self.per + self.k

                def wait(self):
                    dve.wait_ge(*self.value())

                def link(self, ins):
                    self.inc(ins)
                    self.wait()

                def end(self):
                    assert self.k == self.per, (self.s, self.k)

            setup, fr, ch, tl, tb = (Chain(setup_chain, 0), Chain(front_chain, N_FRONT_CHAIN),
                                     Chain(chunk_chain, 0), Chain(tail_chain, N_TAIL_CHAIN), Chain(table_chain, 0))
            setup.start(0)
            v.memset(ones[:, :], 1.0).then_inc(dve_const, 1)
            setup.inc(v.memset(zeros, 0.0))
            v.memset(mhalf[:, :], -0.5).then_inc(dve_const, 1)
            setup.inc(v.memset(vx[:, :, :], 0.0))
            setup.inc(v.memset(carry[:, 0, :], 0.0))
            setup.inc(v.memset(h2[:, :, COMB:ROW], 0.0))
            dve.wait_ge(tanh_c, 1)
            setup.link(v.scalar_tensor_tensor(out=c_t, in0=c_t, scalar=1.0, in1=c_s,
                                              op0=ALU.add, op1=ALU.mult))
            v.tensor_scalar(c_t, c_t, 0.5, None, ALU.mult).then_inc(silu_ready, 1)
            dve.wait_ge(setup_pe, 1)
            v.tensor_copy(siluT[:, :, :], ps[4][:, 0:FT * B].rearrange("p (k b) -> p k b", k=FT))\
                .then_inc(silu_ready, 1)
            dve.wait_ge(setup_pe, 2)
            modT = ps[5][:, 0:2 * FT * B].rearrange("p (k b) -> p k b", b=B)
            v.tensor_copy(saT[:, :, :], modT[:, 0:FT, :]).then_inc(modT_ready, 1)
            v.tensor_scalar(ca1T[:, :, :], modT[:, FT:2 * FT, :], 1.0, None, ALU.add).then_inc(modT_ready, 1)
            dve.wait_ge(setup_pe, 3)
            setup.inc(v.tensor_copy(modrow[:, 0:512], ps[2][0:B, :]))
            setup.link(v.tensor_copy(modrow[:, 512:1024], ps[3][0:B, :]))
            gab = modrow.rearrange("b (m d) -> b m d", m=4)[:, 0:4:3, :]
            cb = modrow[:, 2 * D:3 * D]
            setup.inc(v.tensor_scalar(msgn, gab, 0.0, 2.0, ALU.is_ge, ALU.mult))
            setup.link(v.scalar_tensor_tensor(out=mmag, in0=gab, scalar=-1.0, in1=gab,
                                              op0=ALU.mult, op1=ALU.max))
            setup.link(v.tensor_scalar(mmag, mmag, 0.25, None, ALU.max))
            setup.inc(v.tensor_scalar(cb, cb, 1.0, None, ALU.add))
            setup.link(v.scalar_tensor_tensor(out=gab, in0=msgn, scalar=-1.0, in1=mmag,
                                              op0=ALU.add, op1=ALU.mult))
            v.tensor_copy(gve[:, :], ones[:, 0:FT]).then_inc(modrow_ready, 1)
            dve.wait_ge(small_in, SMALL)
            dve.wait_ge(const_ready, CONSTS)
            for h in range(H):
                setup.inc(v.tensor_tensor_scan(dmask[:, h, :], gam_bc[:, h:h + 1].to_broadcast([P, P]),
                                               ident[:, :], 0.0, ALU.mult, ALU.add))
            for ft in range(FT):
                setup.inc(v.memset(qdec[:, ft, 0:1], 1.0))
                setup.inc(v.tensor_tensor_scan(qdec[:, ft, 1:P + 1], gcol[:, ft:ft + 1].to_broadcast([P, P]),
                                               zeros, 1.0, ALU.mult, ALU.add))
            setup.wait()
            setup.inc(v.tensor_tensor(kdec[:, :], dmask[:, :, P - 1], gam_bc[:, :], ALU.mult))
            setup.inc(v.tensor_scalar(blkavg[:, :], blk[:, :], 1.0 / DH, None, ALU.mult))
            setup.inc(v.tensor_scalar(gnb_s[:, :], gnb_s[:, :], 0.5, None, ALU.mult))
            setup.inc(v.tensor_copy(erow[:, :], erow_i[:, :]))
            setup.inc(v.tensor_copy(ebase[:, :], ebase_i[:, :]))
            setup.inc(v.tensor_copy(ecol[:, :], ecol_i[:, :]))
            setup.inc(v.tensor_copy(tile_f[:, :], tile_i[:, :]))
            setup.wait()
            dve.sem_inc(front.drained["dve"], CREDIT)
            dve.sem_inc(tail.drained["dve"], CREDIT)
            dve.sem_inc(masked, 2)
            dve.sem_inc(setup_done, 1)
            dve.wait_ge(gsc_ready, 1 + 2 * B)
            dve.wait_ge(gb_out, 16)

            def norm_stats(chain, b, st, mv, ve, ready):
                for t in range(NC):
                    chain.inc(v.bn_stats(st[:, t, :], xs[:, bass.ds(NC * b + t, 1), :].rearrange("p a d -> p (a d)")))
                settle(dve, [chain.value()], dve_passed)
                for t in range(NC):
                    chain.inc(v.bn_aggr(mv[:, t, :], st[:, t, :]))
                chain.wait()
                v.tensor_scalar(ve[:, :], mv[:, :, 1], EPS, None, ALU.add).then_inc(ready, 1)

            def front_dve(b):
                fr.start(b)
                settle(dve, [(x_in, 16 * b + 16)], dve_passed)
                norm_stats(fr, b, st1, mv1, ve1, var1)
                dve.wait_ge(rstd1, b + 1)
                for t in range(NC):
                    v.tensor_scalar(xn[:, t, :], xs[:, bass.ds(NC * b + t, 1), :].rearrange("p a d -> p (a d)"),
                                    mv1[:, t, 0:1], rs1[:, t:t + 1], ALU.subtract, ALU.mult).then_inc(xn_ready, 1)
                fr.link(v.tensor_tensor(bog, gsc[:, bass.ds(b, 1), 0:D].rearrange("p a d -> p (a d)"),
                                        bo_bc[:, :], ALU.mult))
                xb = xs[:, bass.ds(NC * b, NC), :]
                fr.inc(v.tensor_tensor(xb, xb, bog.unsqueeze(1).broadcast_to([P, NC, D]), ALU.add))
                for ft in range(FT):
                    wait(dve, front.drains(b, f"q{ft}"))
                    v.tensor_tensor(qd[:, ft, :].rearrange("p (c n) -> p c n", c=NC),
                                    qT[:, ft, :].rearrange("p (c n) -> p c n", c=NC),
                                    qdec[:, ft, 0:P].unsqueeze(1).broadcast_to([P, NC, P]),
                                    ALU.mult).then_inc(qd_ready, 1)
                for ft in range(FT):
                    wait(dve, front.drains(b, f"g{ft}"))
                    zv = z[:, ft, :]
                    fr.inc(v.scalar_tensor_tensor(out=zv, in0=th[:, ft, :], scalar=1.0, in1=zv,
                                                  op0=ALU.add, op1=ALU.mult))
                for n, t0 in (("v01", 0), ("v23", 2)):
                    dve.wait_ge(front.full, front.filled(b, n))
                    for t in range(2):
                        ins = v.tensor_tensor(heads(vx[:, t0 + t, :], H // 2),
                                              front.bank(n)[:, t * D:(t + 1) * D].rearrange("p (j q d) -> p j q d", q=2, d=DH),
                                              bv_bc[:, :].rearrange("p (j q d) -> p j q d", q=2, d=DH), ALU.add)
                        if t:
                            ins.then_inc(front.drained["dve"], 1)
                        else:
                            fr.inc(ins)
                for n, c0, m in (("kd01", 0, 2), ("kd2", 2, 1)):
                    dve.wait_ge(front.full, front.filled(b, n))
                    v.tensor_tensor(kd[:, c0:c0 + m, :].rearrange("p c (h d) -> p c h d", d=DH),
                                    front.bank(n)[:, 0:m * D].rearrange("p (c h d) -> p c h d", c=m, d=DH),
                                    kdec[:, :].unsqueeze(1).unsqueeze(3).broadcast_to([P, m, H, DH]),
                                    ALU.mult).then_inc(front.drained["dve"], 1)
                fr.end()

            def chunks_dve(b):
                for c in range(NC):
                    if c < NC - 1:
                        n = f"st{c}"
                        dve.wait_ge(tail.full, tail.filled(b, n))
                        dst = stt if c else state
                        v.tensor_tensor(dst[:, :, :], tail.bank(n)[:, 0:D].rearrange("p (k n) -> p k n", k=FT),
                                        blk[:, :].unsqueeze(1).broadcast_to([P, FT, P]),
                                        ALU.mult).then_inc(tail.drained["dve"], 1)
                        if c:
                            wait(dve, tail.drains(b, n))
                            if c > 1:
                                dve.wait_ge(state_up, 4 * b + 2)
                            for ft in range(FT):
                                v.scalar_tensor_tensor(out=state[:, ft, :], in0=state[:, ft, :],
                                                       scalar=qdec[:, ft, P:P + 1], in1=stt[:, ft, :],
                                                       op0=ALU.mult, op1=ALU.add).then_inc(state_up, 1)
                    for g in range(4):
                        n = 4 * c + g
                        dve.wait_ge(scored, grp(b, n) + (4 + 1))
                        dve.wait_ge(pv_done, grp(b, n) + 1)
                        v.tensor_tensor(sm[:, g, :], sc[n % 2][:, :],
                                        dmask[:, 4 * g:4 * g + 4, :].rearrange("p h n -> p (h n)"),
                                        ALU.mult).then_inc(masked, 1)

            def tail_dve(b):
                tl.start(b)
                settle(dve, [(pv_done, grp(b, 4 * NC) + 4)], dve_passed)
                for ft in range(FT):
                    tl.inc(v.bn_stats(gst[:, ft, :], ret[ft][:, :]))
                settle(dve, [tl.value()], dve_passed)
                tl.inc(v.bn_aggr(gmv[:, 0, :], gst[:, 0, :]))
                v.bn_aggr(gmv[:, 1, :], gst[:, 1, :]).then_inc(gn_stat, 1)
                dve.wait_ge(gn_full, b + 1)
                gb_ = tail.bank("gn")
                tl.link(v.tensor_copy(gav[:, :, :], gb_[:, 0:2 * FT].rearrange("p (k m) -> p k m", k=FT)))
                tl.link(v.tensor_tensor(gd[:, :], gmv[:, :, 0], gav[:, :, 0], ALU.subtract))
                v.tensor_tensor(gd2[:, :], gd[:, :], gd[:, :], ALU.mult).then_inc(gn_dev, 1)
                dve.wait_ge(tail.full, tail.filled(b, "gn"))
                v.scalar_tensor_tensor(out=gve[:, :], in0=gb_[:, 8:8 + FT], scalar=EPS, in1=gav[:, :, 1],
                                       op0=ALU.add, op1=ALU.add).then_inc(tail.drained["dve"], 1)
                dve.wait_ge(grstd, b + 1)
                tl.link(v.scalar_tensor_tensor(out=gA[:, :], in0=grs[:, :], scalar=0.5, in1=gnw_s[:, :],
                                               op0=ALU.mult, op1=ALU.mult))
                tl.link(v.tensor_tensor(gt[:, :], gav[:, :, 0], gA[:, :], ALU.mult))
                v.tensor_tensor(gB[:, :], gnb_s[:, :], gt[:, :], ALU.subtract).then_inc(gn_ab, 1)
                for ft in range(FT):
                    dve.wait_ge(ro_ready, 2 * b + (2 + ft + 1))
                    v.tensor_tensor(ro[:, ft, :], ro[:, ft, :],
                                    z[:, ft, :],
                                    ALU.mult).then_inc(prod_ready, 1)
                for n, t0 in (("wo01", 0), ("wo23", 2)):
                    dve.wait_ge(tail.full, tail.filled(b, n))
                    v.tensor_tensor(xt[t0 // 2], tail.bank(n)[:, :].rearrange("p (t d) -> p t d", t=2),
                                    gsc[:, bass.ds(b, 1), 0:D].broadcast_to([P, 2, D]),
                                    ALU.mult).then_inc(tail.drained["dve"], 1)
                    wait(dve, tail.drains(b, n))
                    xv = xs[:, bass.ds(NC * b + t0, 2), :]
                    v.tensor_tensor(xv, xv, xt[t0 // 2], ALU.add).then_inc(x2_ready, 1)
                settle(dve, [(x2_ready, 2 * b + 2)], dve_passed)
                norm_stats(tl, b, st2, mv2, ve2, var2)
                dve.wait_ge(rstd2, b + 1)
                dve.wait_ge(h2_free, b + 1)
                for t in range(NC):
                    tl.inc(v.tensor_scalar(h2[:, t, 0:D], xs[:, bass.ds(NC * b + t, 1), :].rearrange("p a d -> p (a d)"),
                                           mv2[:, t, 0:1], rs2[:, t:t + 1], ALU.subtract, ALU.mult))
                tl.wait()
                hv = h2[:, :, 0:D]
                tl.link(v.tensor_tensor(hv, hv, gsc[:, bass.ds(b, 1), 2 * D:3 * D].broadcast_to([P, NC, D]), ALU.mult))
                v.tensor_tensor(hv, hv, gsc[:, bass.ds(b, 1), D:2 * D].broadcast_to([P, NC, D]),
                                ALU.add).then_inc(h2_ready, 1)
                dve.wait_ge(tail.full, tail.filled(b, "logits"))
                v.tensor_copy(lg[:, :, :], tail.bank("logits")[:, 0:NC * E].rearrange("p (t e) -> p t e", e=E))\
                    .then_inc(tail.drained["dve"], 1)
                settle(dve, [tail.drains(b, "logits")], dve_passed)
                for t in range(NC):
                    tl.inc(v.max(mx[:, t, :], lg[:, t, :]))
                tl.wait()
                v.tensor_tensor(vd[:, :], mx[:, :, 0], mx[:, :, 1], ALU.subtract).then_inc(vd_ready, 1)
                for t in range(NC):
                    tl.inc(v.max_index(ix[:, t, :], mx[:, t, :], lg[:, t, :]))
                tl.wait()
                tl.link(v.tensor_copy(ixf[:, :, :], ix[:, :, 0:TOPK]))
                for k in range(TOPK):
                    tl.inc(v.tensor_tensor(oh[:, k, :, :], erow[:, :].unsqueeze(1).broadcast_to([P, NC, E]),
                                           ixf[:, :, k:k + 1].broadcast_to([P, NC, E]), ALU.is_equal))
                tl.wait()
                v.tensor_tensor(msk[:, :, :], oh[:, 0, :, :], oh[:, 1, :, :], ALU.add).then_inc(msk_ready, 1)
                tl.inc(v.tensor_copy(h2[:, :, TOK:TOK + 1].rearrange("p t a -> p (t a)").bitcast(I32),
                                     tokid[:, bass.ds(NC * b, NC)]))
                tl.inc(v.tensor_copy(h2[:, :, BAT:BAT + 1].rearrange("p t a -> p (t a)").bitcast(I32),
                                     batid[:, bass.ds(NC * b, NC)]))
                dve.wait_ge(vt_ready, b + 1)
                for k, sg in ((0, 0.25), (1, -0.25)):
                    tl.inc(v.tensor_scalar(pk[:, k, :], vt[:, :], sg, 0.25, ALU.mult, ALU.add))
                tl.wait()
                for k in range(TOPK):
                    tl.inc(v.tensor_tensor(cmb[:, k, :, :], oh[:, k, :, :],
                                           pk[:, k, :].unsqueeze(2).broadcast_to([P, NC, E]), ALU.mult))
                tl.wait()
                v.tensor_tensor(h2[:, :, COMB:COMB + E], cmb[:, 0, :, :], cmb[:, 1, :, :],
                                ALU.add).then_inc(row_ready, 1)
                dve.wait_ge(tail.full, tail.filled(b, "rank"))
                rk = tail.bank("rank")
                for t in range(NC):
                    tl.link(v.tensor_tensor(carry[:, t + 1, :], carry[:, t, :],
                                            rk[:, 64 + E * t:64 + E * t + E], ALU.add))
                v.tensor_tensor(pos[:, :, :], rk[:, 0:NC * E].rearrange("p (t e) -> p t e", e=E),
                                carry[:, 0:NC, :], ALU.add).then_inc(tail.drained["dve"], 1)
                wait(dve, tail.drains(b, "rank"))
                tl.link(v.tensor_tensor(pos[:, :, :], pos[:, :, :], ebase[:, :].unsqueeze(1).broadcast_to([P, NC, E]), ALU.add))
                for k in range(TOPK):
                    tl.inc(v.tensor_tensor(posk[:, k, :, :], oh[:, k, :, :], pos[:, :, :], ALU.mult))
                tl.wait()
                tl.link(v.tensor_reduce(posf[:, :, :], posk[:, :, :, :], AX.X, ALU.add))
                v.tensor_copy(idx[:, :, :], posf[:, :, :]).then_inc(idx_ready, 1)
                tl.link(v.tensor_copy(carry[:, 0, :], carry[:, NC, :]))
                tl.end()

            with dve.Fori(0, B) as b:
                front_dve(b)
                chunks_dve(b)
                tail_dve(b)

            tb.start(0)
            tb.link(v.tensor_tensor(padr[:, :], carry[0:1, 0, :], ebase[0:1, :], ALU.add))
            v.tensor_copy(padi[:, :], padr[:, :]).then_inc(pad_ready, 1)
            tb.link(v.tensor_scalar(bas[:, :], ecol[:, :], float(REGION), float(-PAD_ROW), ALU.mult, ALU.add))
            dve.wait_ge(table_pe, 1)
            tb.link(v.tensor_scalar(cnti[:, :], ps[2][0:E, 0:1], float(P - 1), None, ALU.add))
            tb.link(v.tensor_scalar(cnti[:, :], cnti[:, :], 7, None, ALU.logical_shift_right))
            v.tensor_copy(tls[:, :], cnti[:, :]).then_inc(tls_ready, 1)
            dve.wait_ge(table_pe, 2)
            dve.wait_ge(tls_ready, 1)
            tb.inc(v.tensor_copy(stc[:, :], ps[3][0:E, 0:1]))
            tb.link(v.tensor_tensor(enc[:, :], ps[3][0:E, 0:1], tls[:, :], ALU.add))
            tb.inc(v.tensor_scalar(ge, tile_f[:, :], stc[:, 0:1], None, ALU.is_ge))
            tb.link(v.scalar_tensor_tensor(out=bas[:, :], in0=stc[:, :], scalar=float(-P), in1=bas[:, :],
                                           op0=ALU.mult, op1=ALU.add))
            tb.inc(v.scalar_tensor_tensor(out=ine, in0=tile_f[:, :], scalar=enc[:, 0:1], in1=ge,
                                          op0=ALU.is_lt, op1=ALU.mult))
            tb.link(v.tensor_scalar(row0, tile_f[:, :], float(P), bas[:, 0:1], ALU.mult, ALU.add))
            tb.inc(v.tensor_tensor(tab[:, 0, :], row0, ine, ALU.mult))
            v.tensor_scalar(tab[:, 1, :], ine, ecol[:, 0:1], None, ALU.mult).then_inc(tls_ready, 1)
            dve.wait_ge(table_pe, 3)
            v.tensor_scalar(tabi[:, 0, :], ps[3][0:1, 128:128 + N_TILES], float(PAD_ROW), None,
                            ALU.add).then_inc(tab_ready, 1)
            v.tensor_copy(tabi[:, 1, :], ps[3][0:1, 128 + N_TILES:128 + 2 * N_TILES]).then_inc(tab_ready, 1)
            dve.wait_ge(tab_ready, 2)

            dve.sem_inc(row_used, 2)
            dve.sem_inc(in_done, 4)
            dve.sem_inc(y_done, 2)

            def take_rows(i, s):
                dve.wait_ge(rt_full, i + 1)
                v.tensor_copy(rT[s % 2], ps[4][:, 0:D].rearrange("p (k n) -> p k n", k=FT)).then_inc(rt_dve, 1)
                dve.wait_ge(added_ok, i + 1)
                v.tensor_copy(meta[s % 4][:, :].bitcast(I32), rows[s % 2][:, D:ROW].bitcast(I32)).then_inc(row_used, 1)

            def silu_mul(i, s):
                dve.wait_ge(th_done, i + 1)
                v.scalar_tensor_tensor(out=eth[s % 2], in0=eth[s % 2], scalar=1.0, in1=ps[2 * (s % 2)][:, :],
                                       op0=ALU.add, op1=ALU.mult).then_inc(in_done, 1)

            def hidden(i, s):
                dve.wait_ge(up1_full, i + 1)
                dve.wait_ge(in_done, 2 * i + 5)
                dve.wait_ge(it_full, i + 1)
                v.tensor_tensor(ein[s % 2], eth[s % 2], ps[2 * (s % 2) + 1][:, :], ALU.mult).then_inc(in_done, 1)

            def weighted(i, s):
                e = dve.value_load(tabi[0:1, 1, bass.ds(i, 1)], min_val=0, max_val=E - 1)
                dve.wait_ge(dn_full, i + 3)
                wait(dve, gbr_value(i, s))
                dve.wait_ge(added_ok, i + 3)
                v.scalar_tensor_tensor(out=ey[s % 2], in0=ps[6 + s % 2][:, 0:D],
                                       scalar=meta[s % 4][:, bass.ds(e, 1)], in1=gbr[s % 2],
                                       op0=ALU.mult, op1=ALU.mult).then_inc(y_done, 1)

            def dve_step(i, s):
                const = isinstance(i, int)
                if not (const and not 0 <= i - 1 < N_TILES):
                    hidden(i - 1, s - 1)
                if not (const and not 0 <= i - 2 < N_TILES):
                    weighted(i - 2, s - 2)
                if not (const and not 0 <= i + 1 < N_TILES):
                    take_rows(i + 1, s + 1)
                if not (const and not 0 <= i < N_TILES):
                    silu_mul(i, s)

            take_rows(0, 0)
            run_steps(dve, dve_step)

        @block.tensor
        def _(pe):
            mm, tr = nc.tensor.matmul, nc.tensor.transpose

            pe.wait_ge(silu_ready, 1)
            pe.wait_ge(const_ready, CONSTS)
            for k in range(FT):
                last = tr(ps[4][:, k * B:(k + 1) * B], c_t[:, k * P:(k + 1) * P], ident[0:B, 0:B])
            last.then_inc(setup_pe, 1)
            pe.wait_ge(silu_ready, 2)
            pe.wait_ge(wmod_in, 16)
            for m in range(2 * FT):
                for k in range(FT):
                    last = mm(ps[5][:, m * B:(m + 1) * B], wmod_s[:, k, m * P:(m + 1) * P], siluT[:, k, :],
                              start=k == 0, stop=k == FT - 1)
            last.then_inc(setup_pe, 1)
            for m in range(2):
                for k in range(FT):
                    last = mm(ps[2 + m][0:B, :], siluT[:, k, :], wmod_s[:, k, 512 * (m + 1):512 * (m + 2)],
                              start=k == 0, stop=k == FT - 1)
            last.then_inc(setup_pe, 1)
            pe.wait_ge(modrow_ready, 1)
            pe.wait_ge(modT_ready, 2)
            for b in range(B):
                mm(BC_BANKS[b][:, :], sel[:, b, :], modrow[:, 0:512], start=True, stop=True)
                mm(BC_HALVES[b], sel[:, b, :], modrow[:, 512:3 * D], start=True, stop=True).then_inc(setup_pe, 1)
            pe.sem_inc(scored, 4)
            pe.sem_inc(pv_done, 4)
            pe.wait_ge(gsc_ready, 1 + 2 * B)
            pe.wait_ge(setup_done, 1)
            pe.wait_ge(w_in, 16 * 4)
            pe.wait_ge(wo_in, 16 * 2)

            def front_pe(b):
                for ft in range(FT):
                    n = f"hT{ft}"
                    if ft == 0:
                        pe.wait_ge(xn_ready, NC * b + NC)
                    wait(pe, front.free(b, n))
                    for t in range(NC):
                        last = tr(front.bank(n)[:, t * P:(t + 1) * P], xn[:, t, ft * P:(ft + 1) * P], ident[:, :])
                    last.then_inc(front.full, 1)
                wait(pe, front.drains(b, "hT1"))
                for w, s in (("q", wq_s), ("k", wk_s), ("g", wg_s)):
                    for ft in range(FT):
                        n = f"{w}{ft}"
                        wait(pe, front.free(b, n))
                        for k in range(FT):
                            last = mm(front.bank(n)[:, :], s[:, k, ft * P:(ft + 1) * P], hT[:, k, :],
                                      start=k == 0, stop=k == FT - 1)
                        last.then_inc(front.full, 1)
                for n, t0 in (("v01", 0), ("v23", 2)):
                    wait(pe, front.free(b, n))
                    for t in range(2):
                        for k in range(FT):
                            last = mm(front.bank(n)[:, t * D:(t + 1) * D], hT[:, k, (t0 + t) * P:(t0 + t + 1) * P],
                                      wv_s[:, k, :], start=k == 0, stop=k == FT - 1)
                    last.then_inc(front.full, 1)
                wait(pe, front.drains(b, "k1"))
                for n, c0, m in (("kd01", 0, 2), ("kd2", 2, 1)):
                    wait(pe, front.free(b, n))
                    for c in range(m):
                        for ft in range(FT):
                            last = tr(front.bank(n)[:, c * D + ft * P:c * D + (ft + 1) * P],
                                      kT[:, ft, (c0 + c) * P:(c0 + c + 1) * P], ident[:, :])
                    last.then_inc(front.full, 1)

            def chunk_pe(b, c):
                cs = slice(c * P, (c + 1) * P)
                if c == 0:
                    pe.wait_ge(ro_ready, 2 * b + 2)
                    pe.wait_ge(qd_ready, 2 * b + 2)
                    wait(pe, front.drains(b, "kd2"))
                else:
                    if c == 1:
                        wait(pe, tail.drains(b, "st0"))
                    else:
                        pe.wait_ge(state_up, 4 * b + 2 * (c - 1))
                    for ft in range(FT):
                        mm(ret[ft][:, cs], state[:, ft, :], qd[:, ft, cs], start=True, stop=False,
                           skip_group_check=True)
                if c < NC - 1:
                    n = f"st{c}"
                    wait(pe, tail.free(b, n))
                    for ft in range(FT):
                        last = mm(tail.bank(n)[:, ft * P:(ft + 1) * P], kd[:, c, ft * P:(ft + 1) * P],
                                  heads(vx[:, c, ft * D:(ft + 1) * D], HPT // 2), start=True, stop=True)
                    last.then_inc(tail.full, 1)
                for g in range(4):
                    n, ft = 4 * c + g, g // 2
                    if g % 2 == 0:
                        pe.wait_ge(qx_ready, 2 * NC * b + (2 * c + ft + 1))
                    pe.wait_ge(masked, grp(b, n) + 1)
                    mm(sc[n % 2][:, :], kT[:, ft, cs], qx[:, ft, (g % 2) * 512:(g % 2 + 1) * 512],
                       start=True, stop=True).then_inc(scored, 1)
                for g in range(4):
                    n, ft = 4 * c + g, g // 2
                    pe.wait_ge(masked, grp(b, n) + (1 + 2))
                    for i in range(4):
                        j, q = (4 * (g % 2) + i) // 2, i % 2
                        at = ft * D + j * 4 * DH + q * 2 * DH
                        last = mm(ret[ft][32 * j:32 * j + 32, cs], vx[:, c, at:at + 2 * DH],
                                  sm[:, g, i * P:(i + 1) * P], start=c == 0 and q == 0, stop=q == 1,
                                  skip_group_check=True)
                    last.then_inc(pv_done, 1)

            def tail_pe(b):
                pe.wait_ge(gn_stat, b + 1)
                wait(pe, tail.free(b, "gn"))
                mm(tail.bank("gn")[:, 0:2 * FT], blkavg[:, :], gmv[:, :, :].rearrange("p k m -> p (k m)"),
                   start=True, stop=True).then_inc(gn_full, 1)
                pe.wait_ge(gn_dev, b + 1)
                mm(tail.bank("gn")[:, 8:8 + FT], blkavg[:, :], gd2[:, :], start=True, stop=True)\
                    .then_inc(tail.full, 1)
                pe.wait_ge(prod_ready, 2 * b + 2)
                for n, t0 in (("wo01", 0), ("wo23", 2)):
                    wait(pe, tail.free(b, n))
                    for t in range(2):
                        for k in range(FT):
                            last = mm(tail.bank(n)[:, t * D:(t + 1) * D], ro[:, k, (t0 + t) * P:(t0 + t + 1) * P],
                                      wo_s[:, k, :], start=k == 0, stop=k == FT - 1)
                    last.then_inc(tail.full, 1)
                pe.wait_ge(h2_ready, b + 1)
                for ft in range(FT):
                    n = f"h2T{ft}"
                    wait(pe, tail.free(b, n))
                    for t in range(NC):
                        last = tr(tail.bank(n)[:, t * P:(t + 1) * P], h2[:, t, ft * P:(ft + 1) * P], ident[:, :])
                    last.then_inc(tail.full, 1)
                wait(pe, tail.free(b, "logits"))
                wait(pe, tail.drains(b, "h2T1"))
                for t in range(NC):
                    for k in range(FT):
                        last = mm(tail.bank("logits")[:, t * E:(t + 1) * E], h2T[:, k, t * P:(t + 1) * P],
                                  gate_s[:, k, :], start=k == 0, stop=k == FT - 1)
                last.then_inc(tail.full, 1)
                wait(pe, tail.free(b, "rank"))
                pe.wait_ge(msk_ready, b + 1)
                mv = msk[:, :, :].rearrange("p t e -> p (t e)")
                mm(tail.bank("rank")[:, 0:NC * E], tri[:, :], mv, start=True, stop=True)
                mm(tail.bank("rank")[:, 64:64 + NC * E], ones[:, :], mv, start=True, stop=True).then_inc(tail.full, 1)

            with pe.Fori(0, B) as b:
                front_pe(b)
                for c in range(NC):
                    chunk_pe(b, c)
                tail_pe(b)

            pe.wait_ge(pad_ready, 1)
            mm(ps[2][0:E, 0:1], carry[:, 0, :], ident[:, 0:1], start=True, stop=True).then_inc(table_pe, 1)
            pe.wait_ge(tls_ready, 1)
            mm(ps[3][0:E, 0:1], tri[0:E, 0:E], tls[:, :], start=True, stop=True).then_inc(table_pe, 1)
            pe.wait_ge(tls_ready, 2)
            mm(ps[3][0:1, 128:128 + 2 * N_TILES], ones[0:E, 0:1], tab[:, :, :].rearrange("e a n -> e (a n)"),
               start=True, stop=True).then_inc(table_pe, 1)
            pe.wait_ge(tab_ready, 2)
            wait(pe, tail.drains(B - 1, "rank"))
            pe.wait_ge(we_in, 16 * 3 * E)
            pe.sem_inc(it_full, 2)
            pe.sem_inc(dn_full, 2)

            def weights(e, o, n):
                return we[:, bass.ds(e, 1), o:o + n].rearrange("p a n -> p (a n)")

            def turn_rows(i, s, n):
                pe.wait_ge(row_in[s % 2], 16 * n)
                if not (isinstance(i, int) and i < 1):
                    pe.wait_ge(rt_dve, i)
                for k in range(FT):
                    last = tr(ps[4][:, k * P:(k + 1) * P], rows[s % 2][:, k * P:(k + 1) * P], ident[:, :])
                last.then_inc(rt_full, 1)

            def up(i, s, e, which, done):
                for k in range(FT):
                    last = mm(ps[2 * (s % 2) + which][:, :], rT[s % 2][:, k, :],
                              weights(e, (which * FT + k) * F, F), start=k == 0, stop=k == FT - 1)
                last.then_inc(done, 1)

            def turn_hidden(i, s):
                pe.wait_ge(in_done, 2 * i + 6)
                pe.wait_ge(it_act, i + 1)
                for k in range(KF):
                    last = tr(ps[5][:, k * P:(k + 1) * P], ein[s % 2][:, k * P:(k + 1) * P], ident[:, :])
                last.then_inc(it_full, 1)

            def down(i, s):
                e = pe.value_load(tabi[0:1, 1, bass.ds(i, 1)], min_val=0, max_val=E - 1)
                pe.wait_ge(it_act, i + 2)
                pe.wait_ge(y_done, i + 1)
                for k in range(KF):
                    last = mm(ps[6 + s % 2][:, 0:D], eit[s % 2][:, k, :], weights(e, 2 * FT * F + k * D, D),
                              start=k == 0, stop=k == KF - 1)
                last.then_inc(dn_full, 1)

            def pe_step(i, s):
                const = isinstance(i, int)
                here = not (const and i >= N_TILES)
                before = not (const and not 0 <= i - 1 < N_TILES)
                if here:
                    e = pe.value_load(tabi[0:1, 1, bass.ds(i, 1)], min_val=0, max_val=E - 1)
                    pe.wait_ge(rt_dve, i + 1)
                    pe.wait_ge(in_done, 2 * i + 2)
                    up(i, s, e, 0, up0_full)
                if before:
                    turn_hidden(i - 1, s - 1)
                if not (const and i + 1 >= N_TILES):
                    turn_rows(i + 1, s + 1, row_loads(i + 1, s + 1))
                if here:
                    up(i, s, e, 1, up1_full)
                if before:
                    down(i - 1, s - 1)

            turn_rows(0, 0, 1)
            run_steps(pe, pe_step)


_INS = ["attn_x", "attn_wq", "attn_bq", "attn_wk", "attn_bk", "attn_wv", "attn_bv", "attn_wg", "attn_bg", "attn_wo",
        "attn_bo", "attn_gn_w", "attn_gn_b", "attn_gamma", "ffn_gate_kernel", "ffn_w0_kernel", "ffn_w1_kernel",
        "ffn_wo_kernel", "c", "wmod"]


def kernel(**inputs):
    import numpy as _np
    import concourse.bacc as _bacc
    from concourse import mybir as _mybir
    from concourse.bass_utils import run_bass_kernel_spmd as _run

    nc = _bacc.Bacc("TRN2", target_bir_lowering=False, num_devices=1)
    arrays, args = {}, []
    for name in _INS:
        a = _np.ascontiguousarray(inputs[f"L0_{name}"])
        arrays[f"in_{name}_dram"] = a
        args.append(nc.dram_tensor(f"in_{name}_dram", a.shape, _mybir.dt.from_np(a.dtype), kind="ExternalInput").ap())
    o = nc.dram_tensor("out_0_dram", [NTOK + P, D], F32, kind="ExternalOutput").ap()
    adaln_block(nc, *args, o)
    r = _run(nc, [arrays], core_ids=[0])
    return r.results[0]["out_0_dram"][:NTOK].reshape(B, S, D)
```

```python
from contextlib import ExitStack

import concourse.bass as bass
from concourse import mybir

F32 = mybir.dt.float32
I32 = mybir.dt.int32
U32 = mybir.dt.uint32
ALU = mybir.AluOpType
ACT = mybir.ActivationFunctionType
AX = mybir.AxisListType

P = 128
B, S, D = 4, 512, 256
H, DH = 16, 16
FT = D // P
HPT = H // FT
NC = S // P
NTOK = B * S
E, F = 8, 512
KF = F // P
TOPK = 2
EPS = 1e-5
COMB, TOK, BAT, ROW = D, D + E, D + E + 1, D + E + 2
META = ROW - D
REGION = NTOK + P
PAD_ROW = E * REGION
N_TILES = (NTOK * TOPK + E * (P - 1)) // P
WE = FT * F * 2 + KF * D

FRONT = [("hT0", "act"), ("hT1", "act"), ("q0", "act"), ("q1", "act"), ("k0", "act"), ("k1", "act"),
         ("g0", "act"), ("g1", "act"), ("v01", "dve"), ("v23", "dve"), ("kd01", "dve"), ("kd2", "dve")]
TAIL = [("st0", "dve"), ("h2T0", "act"), ("h2T1", "act"), ("logits", "dve"), ("st1", "dve"), ("rank", "dve"),
        ("st2", "dve"), ("gn", "dve"), ("wo01", "dve"), ("wo23", "dve")]
LATER = ("h2T0", "h2T1", "logits", "rank")
CREDIT = 2


class Ring:

    def __init__(self, items, banks, full, drained, later=()):
        self.names = [n for n, _ in items]
        self.who = [w for _, w in items]
        self.banks, self.full, self.drained, self.later = banks, full, drained, later

    def round(self, b, name):
        return b + 1 if name in self.later else b

    def bank(self, name):
        return self.banks[self.names.index(name) % 2]

    def filled(self, b, name):
        return self.round(b, name) * len(self.names) + (self.names.index(name) + 1)

    def drains(self, b, name):
        return self.count(self.round(b, name), self.names.index(name))

    def count(self, r, i):
        w = self.who[i]
        return self.drained[w], r * self.who.count(w) + (CREDIT + self.who[:i + 1].count(w))

    def free(self, b, name):
        i, r = self.names.index(name), self.round(b, name)
        if i >= 2:
            return self.count(r, i - 2)
        w = self.who[i - 2]
        return self.drained[w], r * self.who.count(w) + (CREDIT - (1 - i))


def adaln_block(nc, x, wq, bq, wk, bk, wv, bv, wg, bg, wo, bo, gn_w, gn_b, gamma,
                gate_k, w0, w1, wo_e, c, wmod, out):
    ctx = ExitStack()
    with ctx:
        def sb(name, shape, dt=F32):
            return ctx.enter_context(nc.sbuf_tensor(name, shape, dt))

        def sem(name):
            return ctx.enter_context(nc.semaphore(name))

        ctx.enter_context(nc.allow_non_contiguous_dma(reason="small vectors"))

        routed = nc.dram_tensor("routed", [PAD_ROW + P, ROW], F32, kind="Internal").ap()
        gb_dram = nc.dram_tensor("gb_dram", [B, D], F32, kind="Internal").ap()
        gsc_dram = nc.dram_tensor("gsc_dram", [B, 3 * D], F32, kind="Internal").ap()

        xs = sb("xs", [P, B * NC, D])
        wq_s, wk_s, wv_s, wg_s, wo_s = (sb(n, [P, FT, D]) for n in ("wq_s", "wk_s", "wv_s", "wg_s", "wo_s"))
        gate_s = sb("gate_s", [P, FT, E])
        we = sb("we", [P, E, WE])
        wmod_s = we[:, E - 1, :].rearrange("p (k n) -> p k n", k=FT)
        siluT = sb("siluT", [P, FT, B])
        bq_s, bk_s, bg_s, bgh_s, gnw_s, gnb_s, gcol = (
            sb(n, [P, FT]) for n in ("bq_s", "bk_s", "bg_s", "bgh_s", "gnw_s", "gnb_s", "gcol"))
        bv_bc, bo_bc = sb("bv_bc", [P, D]), sb("bo_bc", [P, D])
        gam_bc = sb("gam_bc", [P, H])
        ident, tri, ones, blk, blkavg = (sb(n, [P, P]) for n in ("ident", "tri", "ones", "blk", "blkavg"))
        hmask = sb("hmask", [P, HPT])
        mhalf = sb("mhalf", [P, (B - 1) * NC])
        erow_i, erow = sb("erow_i", [P, E], I32), sb("erow", [P, E])
        ebase_i, ebase = sb("ebase_i", [P, E], I32), sb("ebase", [P, E])
        tokid = sb("tokid", [P, B * NC], I32)
        batid = sb("batid", [P, B * NC], I32)
        tmpl = sb("tmpl", [P, ROW])
        saT, ca1T = sb("saT", [P, FT, B]), sb("ca1T", [P, FT, B])
        gsc = sb("gsc", [P, B, 3 * D])
        dmask = sb("dmask", [P, H, P])
        qdec = sb("qdec", [P, FT, P + 1])
        kdec = sb("kdec", [P, H])
        st1, mv1 = sb("st1", [P, B * NC, 6]), sb("mv1", [P, B * NC, 2])
        ve1, rs1 = sb("ve1", [P, B * NC]), sb("rs1", [P, B * NC])
        xn = sb("xn", [P, NC, D])
        hT = sb("hT", [P, FT, S])
        qT, kT, qd = sb("qT", [P, FT, S]), sb("kT", [P, FT, S]), sb("qd", [P, FT, S])
        qx = sb("qx", [P, FT, HPT * P])
        vx = sb("vx", [P, NC, 2 * D])
        kd = xn
        z = sb("z", [P, FT, S])
        sm = sb("sm", [P, 4, 4 * P])
        th, ro = sm[:, 0:2, :], sm[:, 2:4, :]
        stt = xn[:, NC - 1, :].rearrange("p (k n) -> p k n", k=FT)
        state = sb("state", [P, FT, P])
        gst, gmv, gav, gd, gd2, gve, grs, gA, gt, gB = (
            sb("gst", [P, FT, 6]), sb("gmv", [P, FT, 2]), sb("gav", [P, FT, 2]), sb("gd", [P, FT]),
            sb("gd2", [P, FT]), sb("gve", [P, FT]), sb("grs", [P, FT]), sb("gA", [P, FT]),
            sb("gt", [P, FT]), sb("gB", [P, FT]))
        st2, mv2, ve2, rs2 = sb("st2", [P, NC, 6]), sb("mv2", [P, NC, 2]), sb("ve2", [P, NC]), sb("rs2", [P, NC])
        h2 = sb("h2", [P, NC, ROW])
        h2T = hT
        spare = we[0:B, E - 2, :]
        modrow = spare[:, 0:4 * D]
        msgn, mmag = (spare[:, (4 + 2 * u) * D:(6 + 2 * u) * D].rearrange("b (m d) -> b m d", m=2) for u in range(2))
        zeros = h2[:, 0, 0:P]
        c_s, c_t = kT[0:B, 0, 0:D], kT[0:B, 1, 0:D]
        lg, mx, ix = sb("lg", [P, NC, E]), sb("mx", [P, NC, 8]), sb("ix", [P, NC, 8], U32)
        ixf, oh, msk, cmb = (sb("ixf", [P, NC, 2]), sb("oh", [P, 2, NC, E]), sb("msk", [P, NC, E]),
                             sb("cmb", [P, 2, NC, E]))
        vd, vt, pk = sb("vd", [P, NC]), sb("vt", [P, NC]), sb("pk", [P, 2, NC])
        carry = sb("carry", [P, NC + 1, E])
        pos, posk, posf = sb("pos", [P, NC, E]), sb("posk", [P, 2, NC, E]), sb("posf", [P, 2, NC])
        idx = sb("idx", [P, 2, NC], I32)
        cnt, cnti, tls, stc, enc, bas = (sb("cnt", [E, 1]), sb("cnti", [E, 1], I32), sb("tls", [E, 1]),
                                         sb("stc", [E, 1]), sb("enc", [E, 1]), sb("bas", [E, 1]))
        ecol_i, ecol, tile_i, tile_f = (sb("ecol_i", [E, 1], I32), sb("ecol", [E, 1]),
                                        sb("tile_i", [E, N_TILES], I32), sb("tile_f", [E, N_TILES]))
        ge, ine, row0 = (z[0:E, 0, 64 * u:64 * u + N_TILES] for u in range(3))
        tab = z[0:E, 1, 0:2 * N_TILES].rearrange("e (a n) -> e a n", a=2)
        tabi = sb("tabi", [1, 2, N_TILES], I32)
        padr, padi = sb("padr", [1, E]), sb("padi", [1, E], I32)
        rows = [h2[:, 0, :], h2[:, 1, :]]
        rT = [xn[:, 2 * u, :].rearrange("p (k n) -> p k n", k=FT) for u in range(2)]
        eth = [sm[:, u, :] for u in range(2)]
        ein = [sm[:, 2 + u, :] for u in range(2)]
        eit = [qx[:, u, 0:F].rearrange("p (k n) -> p k n", k=KF) for u in range(2)]
        ey = [hT[:, u, 0:D] for u in range(2)]
        gbr = [hT[:, u, D:2 * D] for u in range(2)]
        meta = [sb(f"meta{u}", [P, META]) for u in range(4)]

        ps = [ctx.enter_context(nc.psum_tensor(f"ps{i}", [P, 512], F32)) for i in range(8)]
        ret = [ps[0], ps[1]]
        sc = [ps[2], ps[3]]
        front = Ring(FRONT, [ps[4], ps[5]], sem("front_full"), {"act": sem("front_act"), "dve": sem("front_dve")})
        tail = Ring(TAIL, [ps[6], ps[7]], sem("tail_full"), {"act": sem("tail_act"), "dve": sem("tail_dve")},
                    LATER)

        def sems(names):
            return [sem(n) for n in names.split()]

        c_in, wmod_in, small_in, w_in, wo_in, we_in, gsc_in = sems("c_in wmod_in small_in w_in wo_in we_in gsc_in")
        x_in = sems("x_in0 x_in1 x_in2 x_in3")
        const_zero, const_ready, tmpl_ready, dve_const = sems("const_zero const_ready tmpl_ready dve_const")
        setup_chain, ln1_chain, front_chain, tail_chain, table_chain = sems(
            "setup_chain ln1_chain front_chain tail_chain table_chain")
        tanh_c, silu_ready, setup_pe, modT_ready, modrow_ready, bgh_ready, setup_done = sems(
            "tanh_c silu_ready setup_pe modT_ready modrow_ready bgh_ready setup_done")
        gb_out, gsc_out, tmpl_out = sems("gb_out gsc_out tmpl_out")
        var1, rstd1, xn_ready, qd_ready, qx_pool, qx_act, z_ready = sems(
            "var1 rstd1 xn_ready qd_ready qx_pool qx_act z_ready")
        scored, masked, pv_done, state_up = sems("scored masked pv_done state_up")
        gn_stat, gn_full, gn_dev, grstd, gn_ab, ro_ready, prod_ready = sems(
            "gn_stat gn_full gn_dev grstd gn_ab ro_ready prod_ready")
        x2_out, var2, rstd2, h2n_ready, h2m_ready, h2_ready, row_ready = sems(
            "x2_out var2 rstd2 h2n_ready h2m_ready h2_ready row_ready")
        vd_ready, vt_ready, msk_ready, idx_ready, scattered, h2_free = sems(
            "vd_ready vt_ready msk_ready idx_ready scattered h2_free")
        pad_ready, pad_out, tls_ready, table_pe, tab_ready = sems("pad_ready pad_out tls_ready table_pe tab_ready")
        row_in, gbr_in = sems("row_in0 row_in1"), sems("gbr_in0 gbr_in1")
        rt_full, rt_dve, row_used, up0_full, up1_full, th_done, in_done, it_full, it_act, dn_full, y_done = sems(
            "rt_full rt_dve row_used up0_full up1_full th_done in_done it_full it_act dn_full y_done")
        added, added_ok, pool_passed, dve_passed = sems("added added_ok pool_passed dve_passed")
        SMALL, CONSTS = 16 * 10, 12
        N_FRONT_CHAIN, N_TAIL_CHAIN = 4, 45

        def row_loads(i, s):
            if isinstance(i, int):
                return i // 2 + 1
            return loop_loads[0] + s // 2 + 1

        def gbr_value(i, s):
            return gbr_in[s % 2], 16 * row_loads(i, s)

        loop_loads = [None]

        def run_steps(eng, step):
            lead = 2
            loops = (N_TILES - 1 - lead) // 4
            for i in range(lead):
                step(i, i)
            with eng.Fori(0, loops) as j:
                loop_loads[0] = 2 * j
                for s in range(lead, lead + 4):
                    step(4 * j + s, s)
            for i in range(lead + 4 * loops, N_TILES + 2):
                step(i, i)

        def heads(ap, pairs):
            base = [list(d) for d in ap.ap]
            return bass.AP(ap.tensor, ap.offset, [base[0], [4 * DH, pairs], [3 * DH, 2], [1, DH]])

        x_v = x.rearrange("b (t p) d -> b p t d", p=P)
        out_v = out[0:NTOK, :].rearrange("(b t p) d -> b p t d", p=P, t=NC)
        wk_v = lambda w: w.rearrange("(k p) n -> p k n", p=P)
        col = lambda v: v.rearrange("(k p) -> p k", p=P)
        wmod_v = wk_v(wmod)
        we_v = [(0, w0, FT, F), (FT * F, w1, FT, F), (2 * FT * F, wo_e, KF, D)]
        w0e = lambda e, k: we[:, e, k * F:(k + 1) * F]

        def wait(eng, pair):
            eng.wait_ge(pair[0], pair[1])

        def settle(eng, pairs, passed):
            for s, v in pairs:
                eng.wait_ge(s, v)
            eng.sem_inc(passed, 1)

        def tile_of_x(i):
            return xs[:, bass.ds(i, 1), :].rearrange("p a d -> p (a d)")

        def grp(b, n):
            return b * (4 * NC) + n

        block = ctx.enter_context(nc.Block())

        @block.sync
        def _(sp):
            def load_x(b):
                sp.dma_start(xs[:, b * NC:(b + 1) * NC, :], x_v[b]).then_inc(x_in[b], 16)

            def load_expert(e):
                for o, w, k, n in we_v:
                    sp.dma_start(we[:, e, o:o + k * n].rearrange("p (k n) -> p k n", k=k),
                                 w[e].rearrange("(k p) n -> p k n", p=P)).then_inc(we_in, 16)

            sp.dma_start(c_s, c).then_inc(c_in, 16)
            sp.dma_start(wmod_s, wmod_v).then_inc(wmod_in, 16)
            load_x(0)
            for s, d in ((wq_s, wq), (wk_s, wk), (wg_s, wg), (wv_s, wv)):
                sp.dma_start(s[:, :, :], wk_v(d)).then_inc(w_in, 16)
            for b in range(1, B):
                load_x(b)
            sp.dma_start(wo_s[:, :, :], wk_v(wo)).then_inc(wo_in, 16)
            sp.dma_start(gate_s[:, :, :], wk_v(gate_k)).then_inc(wo_in, 16)
            sp.wait_ge(modrow_ready, 1)
            sp.dma_start(gsc_dram, modrow[:, 0:3 * D]).then_inc(gsc_out, 16)
            sp.dma_start(gb_dram, modrow[:, 3 * D:4 * D]).then_inc(gb_out, 16)
            sp.wait_ge(gsc_out, 16)
            sp.dma_start(gsc[:, :, :].rearrange("p b n -> p (b n)"),
                         gsc_dram.rearrange("b n -> (b n)").partition_broadcast(P)).then_inc(gsc_in, 16)
            for e in range(E - 2):
                load_expert(e)
            sp.wait_ge(tmpl_ready, 1)
            sp.dma_start(routed[PAD_ROW:PAD_ROW + P, :], tmpl[:, :]).then_inc(tmpl_out, 16)
            sp.wait_ge(setup_pe, 3)
            sp.wait_ge(gb_out, 16)
            load_expert(E - 2)
            load_expert(E - 1)
            with sp.Fori(0, B) as b:
                wait(sp, tail.drains(b, "wo23"))
                sp.dma_start(out_v[bass.ds(b, 1)].rearrange("b p t d -> p (b t) d"),
                             xs[:, bass.ds(b * NC, NC), :]).then_inc(x2_out, 16)
            sp.wait_ge(pad_ready, 1)
            for e in range(E):
                r = sp.value_load(padi[0:1, e:e + 1], min_val=0, max_val=PAD_ROW - P)
                sp.dma_start(routed[bass.ds(r, P), :], tmpl[:, :]).then_inc(pad_out, 16)
            sp.wait_ge(tab_ready, 2)
            sp.wait_ge(tmpl_out, 16)
            sp.wait_ge(pad_out, 16 * E)
            sp.wait_ge(scattered, 16 * TOPK * NC * B)

            def load_rows(i, s, n):
                r = sp.value_load(tabi[0:1, 0, bass.ds(i, 1)], min_val=0, max_val=PAD_ROW)
                sp.wait_ge(row_used, i + 1)
                sp.dma_start(rows[s % 2], routed[bass.ds(r, P), :]).then_inc(row_in[s % 2], 16)

            with sp.Fori(0, N_TILES // 4) as j:
                for s in range(4):
                    load_rows(4 * j + s, s, 2 * j + s // 2)
            for i in range(N_TILES // 4 * 4, N_TILES):
                load_rows(i, i, i // 2)
            sp.wait_ge(x2_out, 16 * B)
            sp.wait_ge(gb_out, 16)
            sp.wait_ge(added, 16 * N_TILES)

        @block.gpsimd
        def _(pool):
            g = nc.gpsimd
            for t, value in ((ident[:, :], 0.0), (tri[:, :], 1.0), (blk[:, :], 1.0), (hmask[:, :], 1.0),
                             (tmpl[:, :], 0.0)):
                last = g.memset(t, value)
            last.then_inc(const_zero, 1)
            pool.wait_ge(const_zero, 1)
            g.affine_select(out=ident[:, :], in_=ident[:, :], compare_op=ALU.not_equal, fill=1.0, base=0,
                            pattern=[[-1, P]], channel_multiplier=1).then_inc(const_ready, 1)
            g.affine_select(out=tri[:, :], in_=tri[:, :], compare_op=ALU.is_gt, fill=0.0, base=0,
                            pattern=[[1, P]], channel_multiplier=-1).then_inc(const_ready, 1)
            blk3 = blk[:, :].rearrange("p (h d) -> p h d", d=DH)
            g.affine_select(out=blk3, in_=blk3, compare_op=ALU.is_ge, fill=0.0, base=0,
                            pattern=[[-DH, HPT], [0, DH]], channel_multiplier=1).then_inc(const_ready, 1)
            g.affine_select(out=hmask[:, :], in_=hmask[:, :], compare_op=ALU.is_ge, fill=0.0, base=0,
                            pattern=[[-DH, HPT]], channel_multiplier=1).then_inc(const_ready, 1)
            pool.wait_ge(const_ready, 4)
            g.affine_select(out=blk3, in_=blk3, compare_op=ALU.is_ge, fill=0.0, base=DH - 1,
                            pattern=[[DH, HPT], [0, DH]], channel_multiplier=-1).then_inc(const_ready, 1)
            g.affine_select(out=hmask[:, :], in_=hmask[:, :], compare_op=ALU.is_ge, fill=0.0, base=DH - 1,
                            pattern=[[DH, HPT]], channel_multiplier=-1).then_inc(const_ready, 1)
            g.iota(erow_i[:, :], [[1, E]], base=0, channel_multiplier=0).then_inc(const_ready, 1)
            g.iota(ebase_i[:, :], [[REGION, E]], base=0, channel_multiplier=0).then_inc(const_ready, 1)
            g.iota(tokid[:, :], [[P, B * NC]], base=0, channel_multiplier=1).then_inc(const_ready, 1)
            g.iota(batid[:, :].rearrange("p (b t) -> p b t", b=B), [[1, B], [0, NC]], base=0,
                   channel_multiplier=0).then_inc(const_ready, 1)
            g.iota(ecol_i[:, :], [[0, 1]], base=0, channel_multiplier=1).then_inc(const_ready, 1)
            g.iota(tile_i[:, :], [[1, N_TILES]], base=0, channel_multiplier=0).then_inc(const_ready, 1)
            g.iota(tmpl[:, TOK:TOK + 1].bitcast(I32), [[0, 1]], base=NTOK, channel_multiplier=1).then_inc(tmpl_ready, 1)

            def power(out_, in_, n, done):
                g.tensor_tensor(out_, in_, mhalf[:, 0:n], ALU.pow).then_inc(done, 1)

            def expand_q(b, c):
                if c == 0:
                    wait(pool, front.drains(b, "q0"))
                pool.wait_ge(scored, grp(b, 4 + 4 * (c - 1) + 2))
                q = qT[:, 0, c * P:(c + 1) * P].unsqueeze(1).broadcast_to([P, HPT, P])
                m = hmask[:, :].unsqueeze(2).broadcast_to([P, HPT, P])
                g.tensor_tensor(qx[:, 0, :].rearrange("p (h n) -> p h n", h=HPT), q, m, ALU.mult).then_inc(qx_pool, 1)

            def group_power(b):
                wait(pool, tail.drains(b, "gn"))
                power(grs[:, :], gve[:, :], FT, grstd)

            def modulate(b):
                pool.wait_ge(var2, b + 1)
                power(rs2[:, :], ve2[:, :], NC, rstd2)
                hv = h2[:, :, 0:D]
                pool.wait_ge(h2n_ready, NC * b + NC)
                g.tensor_tensor(hv, hv, gsc[:, bass.ds(b, 1), 2 * D:3 * D].broadcast_to([P, NC, D]),
                                ALU.mult).then_inc(h2m_ready, 1)
                pool.wait_ge(h2m_ready, b + 1)
                g.tensor_tensor(hv, hv, gsc[:, bass.ds(b, 1), D:2 * D].broadcast_to([P, NC, D]),
                                ALU.add).then_inc(h2_ready, 1)

            def scatter(b, tiles):
                if 0 in tiles:
                    settle(pool, [(idx_ready, b + 1), (row_ready, b + 1)], pool_passed)
                for t in tiles:
                    for k in range(TOPK):
                        g.indirect_dma_start(routed, bass.IndirectOffsetOnAxis(ap=idx[:, k, t:t + 1], axis=0),
                                             h2[:, t, :], None).then_inc(scattered, 16)

            def scatter_done(b):
                pool.wait_ge(scattered, 16 * (TOPK * NC) * b + 16 * (TOPK * NC))
                pool.sem_inc(h2_free, 1)

            pool.wait_ge(dve_const, 2)
            pool.wait_ge(var1, 1)
            power(rs1[:, 0:NC], ve1[:, 0:NC], NC, rstd1)
            pool.sem_inc(h2_free, 1)
            pool.wait_ge(const_ready, CONSTS)
            expand_q(0, 0)
            pool.wait_ge(var1, 2)
            power(rs1[:, NC:B * NC], ve1[:, NC:B * NC], (B - 1) * NC, rstd1)
            for c in range(1, NC):
                expand_q(0, c)
            pool.wait_ge(gsc_in, 16)
            with pool.Fori(0, B - 1) as b:
                group_power(b)
                expand_q(b + 1, 0)
                modulate(b)
                expand_q(b + 1, 1)
                expand_q(b + 1, 2)
                scatter(b, (0,))
                expand_q(b + 1, 3)
                scatter(b, (1, 2, 3))
                scatter_done(b)
            group_power(B - 1)
            modulate(B - 1)
            scatter(B - 1, range(NC))
            scatter_done(B - 1)

            def fetch_gb(i, s, n):
                settle(pool, [(row_used, i + 3), (y_done, i + 1)], pool_passed)
                g.indirect_dma_start(gbr[s % 2], None, gb_dram, bass.IndirectOffsetOnAxis(
                    ap=meta[s % 4][:, BAT - D:BAT - D + 1].bitcast(I32), axis=0)).then_inc(gbr_in[s % 2], 16)

            def add_rows(i, s, first=False, last=False):
                if not last:
                    fetch_gb(i + 1, s + 1, None)
                if not first:
                    pool.wait_ge(added, 16 * i)
                    pool.sem_inc(added_ok, 1)
                settle(pool, [(y_done, i + 3)], pool_passed)
                g.indirect_dma_start(out, bass.IndirectOffsetOnAxis(
                    ap=meta[s % 4][:, TOK - D:TOK - D + 1].bitcast(I32), axis=0), ey[s % 2], None,
                    compute_op=ALU.add).then_inc(added, 16)

            pool.sem_inc(added_ok, 4)
            pool.wait_ge(gb_out, 16)
            pool.wait_ge(x2_out, 16 * B)
            fetch_gb(0, 0, None)
            add_rows(0, 0, first=True)
            with pool.Fori(0, (N_TILES - 3) // 4) as j:
                for s in range(1, 5):
                    add_rows(4 * j + s, s)
            for i in range(N_TILES - 2, N_TILES):
                add_rows(i, i, last=i == N_TILES - 1)

        @block.scalar
        def _(act):
            a = nc.scalar
            act.wait_ge(c_in, 16)
            a.activation(c_t, c_s, ACT.Tanh, scale=0.5).then_inc(tanh_c, 1)
            for s, v in ((bq_s, bq), (bk_s, bk), (bg_s, bg), (gnw_s, gn_w), (gnb_s, gn_b)):
                act.dma_start(s[:, :], col(v)).then_inc(small_in, 16)
            act.dma_start(bv_bc[:, :], bv.partition_broadcast(P)).then_inc(small_in, 16)
            act.dma_start(bo_bc[:, :], bo.partition_broadcast(P)).then_inc(small_in, 16)
            act.dma_start(gam_bc[:, :], gamma.partition_broadcast(P)).then_inc(small_in, 16)
            for ft in range(FT):
                act.dma_start(gcol[:, ft:ft + 1], gamma[ft * HPT:(ft + 1) * HPT].unsqueeze(1).unsqueeze(2)
                              .broadcast_to([HPT, DH, 1])).then_inc(small_in, 16)
            act.wait_ge(modT_ready, 2)

            def features(b):
                for ft in range(FT):
                    act.wait_ge(front.full, front.filled(b, f"hT{ft}"))
                    a.activation(hT[:, ft, :], front.bank(f"hT{ft}")[:, :], ACT.Identity,
                                 scale=ca1T[:, ft, bass.ds(b, 1)], bias=saT[:, ft, bass.ds(b, 1)])\
                        .then_inc(front.drained["act"], 1)

            def bias(b, n, dst, vec):
                for ft in range(FT):
                    act.wait_ge(front.full, front.filled(b, f"{n}{ft}"))
                    a.activation(dst[:, ft, :], front.bank(f"{n}{ft}")[:, :], ACT.Identity,
                                 bias=vec[:, ft:ft + 1]).then_inc(front.drained["act"], 1)

            def gate(b):
                for ft in range(FT):
                    act.wait_ge(front.full, front.filled(b, f"g{ft}"))
                    a.activation(z[:, ft, :], front.bank(f"g{ft}")[:, :], ACT.Identity,
                                 bias=bg_s[:, ft:ft + 1]).then_inc(z_ready, 1)
                    a.activation(th[:, ft, :], front.bank(f"g{ft}")[:, :], ACT.Tanh, scale=0.5,
                                 bias=bgh_s[:, ft:ft + 1]).then_inc(front.drained["act"], 1)

            def expand_q(b, c):
                if c == 0:
                    wait(act, front.drains(b, "q1"))
                act.wait_ge(scored, grp(b, 4 + 4 * (c - 1) + 4))
                for h in range(HPT):
                    a.activation(qx[:, 1, h * P:(h + 1) * P], qT[:, 1, c * P:(c + 1) * P], ACT.Copy,
                                 scale=hmask[:, h:h + 1]).then_inc(qx_act, 1)

            def group_normed(b):
                act.wait_ge(gn_ab, b + 1)
                for ft in range(FT):
                    a.activation(ro[:, ft, :], ret[ft][:, :], ACT.Identity, scale=gA[:, ft:ft + 1],
                                 bias=gB[:, ft:ft + 1]).then_inc(ro_ready, 1)

            def h2_features(b):
                for ft in range(FT):
                    act.wait_ge(tail.full, tail.filled(b, f"h2T{ft}"))
                    a.copy(h2T[:, ft, :], tail.bank(f"h2T{ft}")[:, :]).then_inc(tail.drained["act"], 1)

            def top_tanh(b):
                act.wait_ge(vd_ready, b + 1)
                a.activation(vt[:, :], vd[:, :], ACT.Tanh, scale=0.5).then_inc(vt_ready, 1)

            act.sem_inc(tail.drained["act"], CREDIT + 2)
            act.sem_inc(front.drained["act"], CREDIT)
            act.sem_inc(ro_ready, 2)
            features(0)
            act.wait_ge(small_in, SMALL)
            a.mul(bgh_s[:, :], bg_s[:, :], 0.5).then_inc(bgh_ready, 1)
            bias(0, "q", qT, bq_s)
            bias(0, "k", kT, bk_s)
            act.wait_ge(bgh_ready, 1)
            gate(0)
            act.wait_ge(const_ready, CONSTS)
            expand_q(0, 0)
            expand_q(0, 1)
            with act.Fori(0, B - 1) as b:
                expand_q(b, 2)
                expand_q(b, 3)
                features(b + 1)
                bias(b + 1, "q", qT, bq_s)
                group_normed(b)
                bias(b + 1, "k", kT, bk_s)
                gate(b + 1)
                expand_q(b + 1, 0)
                expand_q(b + 1, 1)
                h2_features(b)
                top_tanh(b)
            b = B - 1
            expand_q(b, 2)
            expand_q(b, 3)
            group_normed(b)
            h2_features(b)
            top_tanh(b)

            act.sem_inc(it_act, 1)

            def turn_back(i, s):
                act.wait_ge(it_full, i + 3)
                act.wait_ge(dn_full, i + 1)
                a.copy(eit[s % 2], ps[5][:, :].rearrange("p (k n) -> p k n", k=KF)).then_inc(it_act, 1)

            def tanh_part(i, s):
                act.wait_ge(up0_full, i + 1)
                act.wait_ge(in_done, 2 * i + 2)
                a.activation(eth[s % 2], ps[2 * (s % 2)][:, :], ACT.Tanh, scale=0.5).then_inc(th_done, 1)

            def act_step(i, s):
                if not (isinstance(i, int) and not 0 <= i - 1 < N_TILES):
                    turn_back(i - 1, s - 1)
                if not (isinstance(i, int) and i >= N_TILES):
                    tanh_part(i, s)

            run_steps(act, act_step)

        @block.vector
        def _(dve):
            v = nc.vector

            class Chain:

                def __init__(self, s, per):
                    self.s, self.per, self.k = s, per, 0

                def start(self, b):
                    self.b, self.k = b, 0

                def inc(self, ins):
                    ins.then_inc(self.s, 1)
                    self.k += 1

                def value(self):
                    return self.s, self.b * self.per + self.k

                def wait(self):
                    dve.wait_ge(*self.value())

                def link(self, ins):
                    self.inc(ins)
                    self.wait()

                def end(self):
                    assert self.k == self.per, (self.s, self.k)

            setup, ln1, fr, tl, tb = (Chain(setup_chain, 0), Chain(ln1_chain, 0), Chain(front_chain, N_FRONT_CHAIN),
                                      Chain(tail_chain, N_TAIL_CHAIN), Chain(table_chain, 0))
            setup.start(0)
            ln1.start(0)
            v.memset(ones[:, :], 1.0).then_inc(dve_const, 1)
            setup.inc(v.memset(zeros, 0.0))
            v.memset(mhalf[:, :], -0.5).then_inc(dve_const, 1)
            setup.inc(v.memset(vx[:, :, :], 0.0))
            setup.inc(v.memset(carry[:, 0, :], 0.0))
            setup.inc(v.memset(h2[:, :, COMB:ROW], 0.0))
            dve.wait_ge(tanh_c, 1)
            setup.link(v.scalar_tensor_tensor(out=c_t, in0=c_t, scalar=1.0, in1=c_s,
                                              op0=ALU.add, op1=ALU.mult))
            v.tensor_scalar(c_t, c_t, 0.5, None, ALU.mult).then_inc(silu_ready, 1)
            dve.wait_ge(setup_pe, 1)
            v.tensor_copy(siluT[:, :, :], ps[4][:, 0:FT * B].rearrange("p (k b) -> p k b", k=FT))\
                .then_inc(silu_ready, 1)

            def norm_stats(chain, first, n, tiles, st, mv, ve, ready):
                for t in range(n):
                    chain.inc(v.bn_stats(st[:, tiles + t, :], tile_of_x(first + t)))
                if isinstance(first, int):
                    chain.wait()
                else:
                    settle(dve, [chain.value()], dve_passed)
                for t in range(n):
                    chain.inc(v.bn_aggr(mv[:, tiles + t, :], st[:, tiles + t, :]))
                chain.wait()
                v.tensor_scalar(ve[:, tiles:tiles + n], mv[:, tiles:tiles + n, 1], EPS, None, ALU.add)\
                    .then_inc(ready, 1)

            dve.wait_ge(x_in[0], 16)
            norm_stats(ln1, 0, NC, 0, st1, mv1, ve1, var1)

            def normed(b):
                for t in range(NC):
                    v.tensor_scalar(xn[:, t, :], tile_of_x(NC * b + t), mv1[:, bass.ds(NC * b + t, 1), 0],
                                    rs1[:, bass.ds(NC * b + t, 1)], ALU.subtract, ALU.mult).then_inc(xn_ready, 1)

            dve.wait_ge(rstd1, 1)
            normed(0)
            dve.wait_ge(setup_pe, 2)
            modT = ps[5][:, 0:2 * FT * B].rearrange("p (k b) -> p k b", b=B)
            v.tensor_copy(saT[:, :, :], modT[:, 0:FT, :]).then_inc(modT_ready, 1)
            v.tensor_scalar(ca1T[:, :, :], modT[:, FT:2 * FT, :], 1.0, None, ALU.add).then_inc(modT_ready, 1)
            dve.wait_ge(setup_pe, 3)
            setup.inc(v.tensor_copy(modrow[:, 0:512], ps[2][0:B, :]))
            setup.link(v.tensor_copy(modrow[:, 512:1024], ps[3][0:B, :]))
            gab = modrow.rearrange("b (m d) -> b m d", m=4)[:, 0:4:3, :]
            cb = modrow[:, 2 * D:3 * D]
            setup.inc(v.tensor_scalar(msgn, gab, 0.0, 2.0, ALU.is_ge, ALU.mult))
            setup.link(v.scalar_tensor_tensor(out=mmag, in0=gab, scalar=-1.0, in1=gab,
                                              op0=ALU.mult, op1=ALU.max))
            setup.link(v.tensor_scalar(mmag, mmag, 0.25, None, ALU.max))
            setup.inc(v.tensor_scalar(cb, cb, 1.0, None, ALU.add))
            setup.link(v.scalar_tensor_tensor(out=gab, in0=msgn, scalar=-1.0, in1=mmag,
                                              op0=ALU.add, op1=ALU.mult))
            v.tensor_copy(gve[:, :], ones[:, 0:FT]).then_inc(modrow_ready, 1)
            dve.wait_ge(small_in, SMALL)
            dve.wait_ge(const_ready, CONSTS)
            for h in range(H):
                setup.inc(v.tensor_tensor_scan(dmask[:, h, :], gam_bc[:, h:h + 1].to_broadcast([P, P]),
                                               ident[:, :], 0.0, ALU.mult, ALU.add))
            for ft in range(FT):
                setup.inc(v.memset(qdec[:, ft, 0:1], 1.0))
                setup.inc(v.tensor_tensor_scan(qdec[:, ft, 1:P + 1], gcol[:, ft:ft + 1].to_broadcast([P, P]),
                                               zeros, 1.0, ALU.mult, ALU.add))
            setup.wait()
            setup.inc(v.tensor_tensor(kdec[:, :], dmask[:, :, P - 1], gam_bc[:, :], ALU.mult))
            setup.inc(v.tensor_scalar(blkavg[:, :], blk[:, :], 1.0 / DH, None, ALU.mult))
            setup.inc(v.tensor_scalar(gnb_s[:, :], gnb_s[:, :], 0.5, None, ALU.mult))
            setup.inc(v.tensor_copy(erow[:, :], erow_i[:, :]))
            setup.inc(v.tensor_copy(ebase[:, :], ebase_i[:, :]))
            setup.inc(v.tensor_copy(ecol[:, :], ecol_i[:, :]))
            setup.inc(v.tensor_copy(tile_f[:, :], tile_i[:, :]))
            setup.wait()
            dve.sem_inc(front.drained["dve"], CREDIT)
            dve.sem_inc(tail.drained["dve"], CREDIT)
            dve.sem_inc(masked, 2)
            dve.sem_inc(setup_done, 1)
            for b in range(1, B):
                dve.wait_ge(x_in[b], 16)

            norm_stats(ln1, NC, (B - 1) * NC, NC, st1, mv1, ve1, var1)

            def decay_q(b):
                for ft in range(FT):
                    wait(dve, front.drains(b, f"q{ft}"))
                    v.tensor_tensor(qd[:, ft, :].rearrange("p (c n) -> p c n", c=NC),
                                    qT[:, ft, :].rearrange("p (c n) -> p c n", c=NC),
                                    qdec[:, ft, 0:P].unsqueeze(1).broadcast_to([P, NC, P]),
                                    ALU.mult).then_inc(qd_ready, 1)

            def gates_and_rows(b):
                fr.start(b)
                for ft in range(FT):
                    wait(dve, front.drains(b, f"g{ft}"))
                    zv = z[:, ft, :]
                    fr.inc(v.scalar_tensor_tensor(out=zv, in0=th[:, ft, :], scalar=1.0, in1=zv,
                                                  op0=ALU.add, op1=ALU.mult))
                for n, t0 in (("v01", 0), ("v23", 2)):
                    dve.wait_ge(front.full, front.filled(b, n))
                    for t in range(2):
                        ins = v.tensor_tensor(heads(vx[:, t0 + t, :], H // 2),
                                              front.bank(n)[:, t * D:(t + 1) * D].rearrange("p (j q d) -> p j q d", q=2, d=DH),
                                              bv_bc[:, :].rearrange("p (j q d) -> p j q d", q=2, d=DH), ALU.add)
                        if t:
                            ins.then_inc(front.drained["dve"], 1)
                        else:
                            fr.inc(ins)
                for n, c0, m in (("kd01", 0, 2), ("kd2", 2, 1)):
                    dve.wait_ge(front.full, front.filled(b, n))
                    v.tensor_tensor(kd[:, c0:c0 + m, :].rearrange("p c (h d) -> p c h d", d=DH),
                                    front.bank(n)[:, 0:m * D].rearrange("p (c h d) -> p c h d", c=m, d=DH),
                                    kdec[:, :].unsqueeze(1).unsqueeze(3).broadcast_to([P, m, H, DH]),
                                    ALU.mult).then_inc(front.drained["dve"], 1)
                fr.end()

            def chunk_dve(b, c, between=None):
                if c < NC - 1:
                    n = f"st{c}"
                    dve.wait_ge(tail.full, tail.filled(b, n))
                    if c == 1 and isinstance(b, int) and b == 0:
                        dve.sem_inc(tail.drained["dve"], 1)
                    dst = stt if c else state
                    v.tensor_tensor(dst[:, :, :], tail.bank(n)[:, 0:D].rearrange("p (k n) -> p k n", k=FT),
                                    blk[:, :].unsqueeze(1).broadcast_to([P, FT, P]),
                                    ALU.mult).then_inc(tail.drained["dve"], 1)
                    if c:
                        wait(dve, tail.drains(b, n))
                        if c > 1:
                            dve.wait_ge(state_up, 4 * b + 2)
                        for ft in range(FT):
                            v.scalar_tensor_tensor(out=state[:, ft, :], in0=state[:, ft, :],
                                                   scalar=qdec[:, ft, P:P + 1], in1=stt[:, ft, :],
                                                   op0=ALU.mult, op1=ALU.add).then_inc(state_up, 1)
                for g in range(4):
                    n = 4 * c + g
                    dve.wait_ge(scored, grp(b, n) + (4 + 1))
                    dve.wait_ge(pv_done, grp(b, n) + 1)
                    v.tensor_tensor(sm[:, g, :], sc[n % 2][:, :],
                                    dmask[:, 4 * g:4 * g + 4, :].rearrange("p h n -> p (h n)"),
                                    ALU.mult).then_inc(masked, 1)
                    if g == 1 and between is not None:
                        between()

            def group_norm(b):
                tl.start(b)
                settle(dve, [(pv_done, grp(b, 4 * NC) + 4)], dve_passed)
                for ft in range(FT):
                    tl.inc(v.bn_stats(gst[:, ft, :], ret[ft][:, :]))
                settle(dve, [tl.value()], dve_passed)
                tl.inc(v.bn_aggr(gmv[:, 0, :], gst[:, 0, :]))
                v.bn_aggr(gmv[:, 1, :], gst[:, 1, :]).then_inc(gn_stat, 1)
                dve.wait_ge(gn_full, b + 1)
                gb_ = tail.bank("gn")
                tl.link(v.tensor_copy(gav[:, :, :], gb_[:, 0:2 * FT].rearrange("p (k m) -> p k m", k=FT)))
                tl.link(v.tensor_tensor(gd[:, :], gmv[:, :, 0], gav[:, :, 0], ALU.subtract))
                v.tensor_tensor(gd2[:, :], gd[:, :], gd[:, :], ALU.mult).then_inc(gn_dev, 1)
                dve.wait_ge(tail.full, tail.filled(b, "gn"))
                v.scalar_tensor_tensor(out=gve[:, :], in0=gb_[:, 8:8 + FT], scalar=EPS, in1=gav[:, :, 1],
                                       op0=ALU.add, op1=ALU.add).then_inc(tail.drained["dve"], 1)
                dve.wait_ge(grstd, b + 1)
                tl.link(v.scalar_tensor_tensor(out=gA[:, :], in0=grs[:, :], scalar=0.5, in1=gnw_s[:, :],
                                               op0=ALU.mult, op1=ALU.mult))
                tl.link(v.tensor_tensor(gt[:, :], gav[:, :, 0], gA[:, :], ALU.mult))
                v.tensor_tensor(gB[:, :], gnb_s[:, :], gt[:, :], ALU.subtract).then_inc(gn_ab, 1)

            def attention_out(b):
                for ft in range(FT):
                    dve.wait_ge(ro_ready, 2 * b + (2 + ft + 1))
                    v.tensor_tensor(ro[:, ft, :], ro[:, ft, :],
                                    z[:, ft, :],
                                    ALU.mult).then_inc(prod_ready, 1)
                for n, t0 in (("wo01", 0), ("wo23", 2)):
                    dve.wait_ge(tail.full, tail.filled(b, n))
                    att = tail.bank(n)[:, :].rearrange("p (t d) -> p t d", t=2)
                    tl.link(v.tensor_tensor(att, att, bo_bc[:, :].unsqueeze(1).broadcast_to([P, 2, D]), ALU.add))
                    tl.link(v.tensor_tensor(att, att, gsc[:, bass.ds(b, 1), 0:D].broadcast_to([P, 2, D]), ALU.mult))
                    xv = xs[:, bass.ds(NC * b + t0, 2), :]
                    v.tensor_tensor(xv, xv, att, ALU.add).then_inc(tail.drained["dve"], 1)
                settle(dve, [tail.drains(b, "wo23")], dve_passed)
                norm_stats(tl, NC * b, NC, 0, st2, mv2, ve2, var2)

            def second_norm(b):
                dve.wait_ge(rstd2, b + 1)
                dve.wait_ge(h2_free, b + 1)
                for t in range(NC):
                    v.tensor_scalar(h2[:, t, 0:D], tile_of_x(NC * b + t), mv2[:, t, 0:1], rs2[:, t:t + 1],
                                    ALU.subtract, ALU.mult).then_inc(h2n_ready, 1)

            def choose(b):
                dve.wait_ge(tail.full, tail.filled(b, "logits"))
                v.tensor_copy(lg[:, :, :], tail.bank("logits")[:, 0:NC * E].rearrange("p (t e) -> p t e", e=E))\
                    .then_inc(tail.drained["dve"], 1)
                settle(dve, [tail.drains(b, "logits")], dve_passed)
                for t in range(NC):
                    tl.inc(v.max(mx[:, t, :], lg[:, t, :]))
                tl.wait()
                v.tensor_tensor(vd[:, :], mx[:, :, 0], mx[:, :, 1], ALU.subtract).then_inc(vd_ready, 1)
                for t in range(NC):
                    tl.inc(v.max_index(ix[:, t, :], mx[:, t, :], lg[:, t, :]))
                tl.wait()
                tl.link(v.tensor_copy(ixf[:, :, :], ix[:, :, 0:TOPK]))
                for k in range(TOPK):
                    tl.inc(v.tensor_tensor(oh[:, k, :, :], erow[:, :].unsqueeze(1).broadcast_to([P, NC, E]),
                                           ixf[:, :, k:k + 1].broadcast_to([P, NC, E]), ALU.is_equal))
                tl.wait()
                v.tensor_tensor(msk[:, :, :], oh[:, 0, :, :], oh[:, 1, :, :], ALU.add).then_inc(msk_ready, 1)
                tl.inc(v.tensor_copy(h2[:, :, TOK:TOK + 1].rearrange("p t a -> p (t a)").bitcast(I32),
                                     tokid[:, bass.ds(NC * b, NC)]))
                tl.inc(v.tensor_copy(h2[:, :, BAT:BAT + 1].rearrange("p t a -> p (t a)").bitcast(I32),
                                     batid[:, bass.ds(NC * b, NC)]))
                dve.wait_ge(vt_ready, b + 1)
                for k, sg in ((0, 0.25), (1, -0.25)):
                    tl.inc(v.tensor_scalar(pk[:, k, :], vt[:, :], sg, 0.25, ALU.mult, ALU.add))
                tl.wait()
                for k in range(TOPK):
                    tl.inc(v.tensor_tensor(cmb[:, k, :, :], oh[:, k, :, :],
                                           pk[:, k, :].unsqueeze(2).broadcast_to([P, NC, E]), ALU.mult))
                tl.wait()
                v.tensor_tensor(h2[:, :, COMB:COMB + E], cmb[:, 0, :, :], cmb[:, 1, :, :],
                                ALU.add).then_inc(row_ready, 1)

            def places(b):
                dve.wait_ge(tail.full, tail.filled(b, "rank"))
                rk = tail.bank("rank")
                for t in range(NC):
                    tl.link(v.tensor_tensor(carry[:, t + 1, :], carry[:, t, :],
                                            rk[:, 64 + E * t:64 + E * t + E], ALU.add))
                v.tensor_tensor(pos[:, :, :], rk[:, 0:NC * E].rearrange("p (t e) -> p t e", e=E),
                                carry[:, 0:NC, :], ALU.add).then_inc(tail.drained["dve"], 1)
                wait(dve, tail.drains(b, "rank"))
                tl.link(v.tensor_tensor(pos[:, :, :], pos[:, :, :], ebase[:, :].unsqueeze(1).broadcast_to([P, NC, E]), ALU.add))
                for k in range(TOPK):
                    tl.inc(v.tensor_tensor(posk[:, k, :, :], oh[:, k, :, :], pos[:, :, :], ALU.mult))
                tl.wait()
                tl.link(v.tensor_reduce(posf[:, :, :], posk[:, :, :, :], AX.X, ALU.add))
                v.tensor_copy(idx[:, :, :], posf[:, :, :]).then_inc(idx_ready, 1)
                tl.link(v.tensor_copy(carry[:, 0, :], carry[:, NC, :]))
                tl.end()

            decay_q(0)
            gates_and_rows(0)
            chunk_dve(0, 0)
            chunk_dve(0, 1)
            dve.sem_inc(tail.drained["dve"], 1)
            dve.wait_ge(rstd1, 2)
            dve.wait_ge(gsc_in, 16)
            with dve.Fori(0, B - 1) as b:
                chunk_dve(b, 2)
                chunk_dve(b, 3, between=lambda: normed(b + 1))
                group_norm(b)
                decay_q(b + 1)
                attention_out(b)
                gates_and_rows(b + 1)
                second_norm(b)
                chunk_dve(b + 1, 0)
                choose(b)
                chunk_dve(b + 1, 1)
                places(b)
            b = B - 1
            chunk_dve(b, 2)
            chunk_dve(b, 3)
            group_norm(b)
            attention_out(b)
            dve.sem_inc(tail.drained["dve"], 1)
            second_norm(b)
            choose(b)
            dve.sem_inc(tail.drained["dve"], 1)
            places(b)

            tb.start(0)
            tb.link(v.tensor_tensor(padr[:, :], carry[0:1, 0, :], ebase[0:1, :], ALU.add))
            v.tensor_copy(padi[:, :], padr[:, :]).then_inc(pad_ready, 1)
            tb.link(v.tensor_scalar(bas[:, :], ecol[:, :], float(REGION), float(-PAD_ROW), ALU.mult, ALU.add))
            dve.wait_ge(table_pe, 1)
            tb.link(v.tensor_scalar(cnti[:, :], ps[2][0:E, 0:1], float(P - 1), None, ALU.add))
            tb.link(v.tensor_scalar(cnti[:, :], cnti[:, :], 7, None, ALU.logical_shift_right))
            v.tensor_copy(tls[:, :], cnti[:, :]).then_inc(tls_ready, 1)
            dve.wait_ge(table_pe, 2)
            dve.wait_ge(tls_ready, 1)
            tb.inc(v.tensor_copy(stc[:, :], ps[3][0:E, 0:1]))
            tb.link(v.tensor_tensor(enc[:, :], ps[3][0:E, 0:1], tls[:, :], ALU.add))
            tb.inc(v.tensor_scalar(ge, tile_f[:, :], stc[:, 0:1], None, ALU.is_ge))
            tb.link(v.scalar_tensor_tensor(out=bas[:, :], in0=stc[:, :], scalar=float(-P), in1=bas[:, :],
                                           op0=ALU.mult, op1=ALU.add))
            tb.inc(v.scalar_tensor_tensor(out=ine, in0=tile_f[:, :], scalar=enc[:, 0:1], in1=ge,
                                          op0=ALU.is_lt, op1=ALU.mult))
            tb.link(v.tensor_scalar(row0, tile_f[:, :], float(P), bas[:, 0:1], ALU.mult, ALU.add))
            tb.inc(v.tensor_tensor(tab[:, 0, :], row0, ine, ALU.mult))
            v.tensor_scalar(tab[:, 1, :], ine, ecol[:, 0:1], None, ALU.mult).then_inc(tls_ready, 1)
            dve.wait_ge(table_pe, 3)
            v.tensor_scalar(tabi[:, 0, :], ps[3][0:1, 128:128 + N_TILES], float(PAD_ROW), None,
                            ALU.add).then_inc(tab_ready, 1)
            v.tensor_copy(tabi[:, 1, :], ps[3][0:1, 128 + N_TILES:128 + 2 * N_TILES]).then_inc(tab_ready, 1)
            dve.wait_ge(tab_ready, 2)

            dve.sem_inc(row_used, 2)
            dve.sem_inc(in_done, 4)
            dve.sem_inc(y_done, 2)

            def take_rows(i, s):
                dve.wait_ge(rt_full, i + 1)
                v.tensor_copy(rT[s % 2], ps[4][:, 0:D].rearrange("p (k n) -> p k n", k=FT)).then_inc(rt_dve, 1)
                dve.wait_ge(added_ok, i + 1)
                v.tensor_copy(meta[s % 4][:, :].bitcast(I32), rows[s % 2][:, D:ROW].bitcast(I32)).then_inc(row_used, 1)

            def silu_mul(i, s):
                dve.wait_ge(th_done, i + 1)
                v.scalar_tensor_tensor(out=eth[s % 2], in0=eth[s % 2], scalar=1.0, in1=ps[2 * (s % 2)][:, :],
                                       op0=ALU.add, op1=ALU.mult).then_inc(in_done, 1)

            def hidden(i, s):
                dve.wait_ge(up1_full, i + 1)
                dve.wait_ge(in_done, 2 * i + 5)
                dve.wait_ge(it_full, i + 1)
                v.tensor_tensor(ein[s % 2], eth[s % 2], ps[2 * (s % 2) + 1][:, :], ALU.mult).then_inc(in_done, 1)

            def weighted(i, s):
                e = dve.value_load(tabi[0:1, 1, bass.ds(i, 1)], min_val=0, max_val=E - 1)
                dve.wait_ge(dn_full, i + 3)
                wait(dve, gbr_value(i, s))
                dve.wait_ge(added_ok, i + 3)
                v.scalar_tensor_tensor(out=ey[s % 2], in0=ps[6 + s % 2][:, 0:D],
                                       scalar=meta[s % 4][:, bass.ds(e, 1)], in1=gbr[s % 2],
                                       op0=ALU.mult, op1=ALU.mult).then_inc(y_done, 1)

            def dve_step(i, s):
                const = isinstance(i, int)
                if not (const and not 0 <= i - 1 < N_TILES):
                    hidden(i - 1, s - 1)
                if not (const and not 0 <= i - 2 < N_TILES):
                    weighted(i - 2, s - 2)
                if not (const and not 0 <= i + 1 < N_TILES):
                    take_rows(i + 1, s + 1)
                if not (const and not 0 <= i < N_TILES):
                    silu_mul(i, s)

            take_rows(0, 0)
            run_steps(dve, dve_step)

        @block.tensor
        def _(pe):
            mm, tr = nc.tensor.matmul, nc.tensor.transpose

            pe.wait_ge(silu_ready, 1)
            pe.wait_ge(const_ready, CONSTS)
            for k in range(FT):
                last = tr(ps[4][:, k * B:(k + 1) * B], c_t[:, k * P:(k + 1) * P], ident[0:B, 0:B])
            last.then_inc(setup_pe, 1)
            pe.wait_ge(silu_ready, 2)
            pe.wait_ge(wmod_in, 16)
            for m in range(2 * FT):
                for k in range(FT):
                    last = mm(ps[5][:, m * B:(m + 1) * B], wmod_s[:, k, m * P:(m + 1) * P], siluT[:, k, :],
                              start=k == 0, stop=k == FT - 1)
            last.then_inc(setup_pe, 1)
            for m in range(2):
                for k in range(FT):
                    last = mm(ps[2 + m][0:B, :], siluT[:, k, :], wmod_s[:, k, 512 * (m + 1):512 * (m + 2)],
                              start=k == 0, stop=k == FT - 1)
            last.then_inc(setup_pe, 1)
            pe.sem_inc(scored, 4)
            pe.sem_inc(pv_done, 4)
            pe.wait_ge(modT_ready, 2)

            def turn_x(b):
                for ft in range(FT):
                    n = f"hT{ft}"
                    if ft == 0:
                        pe.wait_ge(xn_ready, NC * b + NC)
                    wait(pe, front.free(b, n))
                    for t in range(NC):
                        last = tr(front.bank(n)[:, t * P:(t + 1) * P], xn[:, t, ft * P:(ft + 1) * P], ident[:, :])
                    last.then_inc(front.full, 1)

            def project(b, w, s, tiles=range(FT)):
                for ft in tiles:
                    n = f"{w}{ft}"
                    wait(pe, front.free(b, n))
                    for k in range(FT):
                        last = mm(front.bank(n)[:, :], s[:, k, ft * P:(ft + 1) * P], hT[:, k, :],
                                  start=k == 0, stop=k == FT - 1)
                    last.then_inc(front.full, 1)

            def rows_v_k(b):
                for n, t0 in (("v01", 0), ("v23", 2)):
                    wait(pe, front.free(b, n))
                    for t in range(2):
                        for k in range(FT):
                            last = mm(front.bank(n)[:, t * D:(t + 1) * D], hT[:, k, (t0 + t) * P:(t0 + t + 1) * P],
                                      wv_s[:, k, :], start=k == 0, stop=k == FT - 1)
                    last.then_inc(front.full, 1)
                wait(pe, front.drains(b, "k1"))
                for n, c0, m in (("kd01", 0, 2), ("kd2", 2, 1)):
                    wait(pe, front.free(b, n))
                    for c in range(m):
                        for ft in range(FT):
                            last = tr(front.bank(n)[:, c * D + ft * P:c * D + (ft + 1) * P],
                                      kT[:, ft, (c0 + c) * P:(c0 + c + 1) * P], ident[:, :])
                    last.then_inc(front.full, 1)

            def chunk_pe(b, c):
                cs = slice(c * P, (c + 1) * P)
                if c == 0:
                    pe.wait_ge(ro_ready, 2 * b + 2)
                    pe.wait_ge(qd_ready, 2 * b + 2)
                    wait(pe, front.drains(b, "kd2"))
                else:
                    if c == 1:
                        wait(pe, tail.drains(b, "st0"))
                        if isinstance(b, int) and b == 0:
                            pe.sem_inc(tail.full, 3)
                    else:
                        pe.wait_ge(state_up, 4 * b + 2 * (c - 1))
                    for ft in range(FT):
                        mm(ret[ft][:, cs], state[:, ft, :], qd[:, ft, cs], start=True, stop=False,
                           skip_group_check=True)
                if c < NC - 1:
                    n = f"st{c}"
                    wait(pe, tail.free(b, n))
                    for ft in range(FT):
                        last = mm(tail.bank(n)[:, ft * P:(ft + 1) * P], kd[:, c, ft * P:(ft + 1) * P],
                                  heads(vx[:, c, ft * D:(ft + 1) * D], HPT // 2), start=True, stop=True)
                    last.then_inc(tail.full, 1)
                for g in range(4):
                    n, ft = 4 * c + g, g // 2
                    if g == 0:
                        pe.wait_ge(qx_pool, NC * b + (c + 1))
                    elif g == 2:
                        pe.wait_ge(qx_act, NC * HPT * b + HPT * (c + 1))
                    pe.wait_ge(masked, grp(b, n) + 1)
                    mm(sc[n % 2][:, :], kT[:, ft, cs], qx[:, ft, (g % 2) * 512:(g % 2 + 1) * 512],
                       start=True, stop=True).then_inc(scored, 1)
                for g in range(4):
                    n, ft = 4 * c + g, g // 2
                    pe.wait_ge(masked, grp(b, n) + (1 + 2))
                    for i in range(4):
                        j, q = (4 * (g % 2) + i) // 2, i % 2
                        at = ft * D + j * 4 * DH + q * 2 * DH
                        last = mm(ret[ft][32 * j:32 * j + 32, cs], vx[:, c, at:at + 2 * DH],
                                  sm[:, g, i * P:(i + 1) * P], start=c == 0 and q == 0, stop=q == 1,
                                  skip_group_check=True)
                    last.then_inc(pv_done, 1)

            def average(b):
                pe.wait_ge(gn_stat, b + 1)
                wait(pe, tail.free(b, "gn"))
                mm(tail.bank("gn")[:, 0:2 * FT], blkavg[:, :], gmv[:, :, :].rearrange("p k m -> p (k m)"),
                   start=True, stop=True).then_inc(gn_full, 1)

            def average_dev(b):
                pe.wait_ge(gn_dev, b + 1)
                mm(tail.bank("gn")[:, 8:8 + FT], blkavg[:, :], gd2[:, :], start=True, stop=True)\
                    .then_inc(tail.full, 1)

            def out_rows(b):
                pe.wait_ge(prod_ready, 2 * b + 2)
                for n, t0 in (("wo01", 0), ("wo23", 2)):
                    wait(pe, tail.free(b, n))
                    for t in range(2):
                        for k in range(FT):
                            last = mm(tail.bank(n)[:, t * D:(t + 1) * D], ro[:, k, (t0 + t) * P:(t0 + t + 1) * P],
                                      wo_s[:, k, :], start=k == 0, stop=k == FT - 1)
                    last.then_inc(tail.full, 1)

            def router(b):
                pe.wait_ge(h2_ready, b + 1)
                for ft in range(FT):
                    n = f"h2T{ft}"
                    wait(pe, tail.free(b, n))
                    for t in range(NC):
                        last = tr(tail.bank(n)[:, t * P:(t + 1) * P], h2[:, t, ft * P:(ft + 1) * P], ident[:, :])
                    last.then_inc(tail.full, 1)
                wait(pe, tail.free(b, "logits"))
                wait(pe, tail.drains(b, "h2T1"))
                for t in range(NC):
                    for k in range(FT):
                        last = mm(tail.bank("logits")[:, t * E:(t + 1) * E], h2T[:, k, t * P:(t + 1) * P],
                                  gate_s[:, k, :], start=k == 0, stop=k == FT - 1)
                last.then_inc(tail.full, 1)

            def rank(b):
                wait(pe, tail.free(b, "rank"))
                pe.wait_ge(msk_ready, b + 1)
                mv = msk[:, :, :].rearrange("p t e -> p (t e)")
                mm(tail.bank("rank")[:, 0:NC * E], tri[:, :], mv, start=True, stop=True)
                mm(tail.bank("rank")[:, 64:64 + NC * E], ones[:, :], mv, start=True, stop=True).then_inc(tail.full, 1)

            turn_x(0)
            wait(pe, front.drains(0, "hT1"))
            pe.wait_ge(w_in, 16 * 4)
            for w, s in (("q", wq_s), ("k", wk_s), ("g", wg_s)):
                project(0, w, s)
            rows_v_k(0)
            pe.wait_ge(setup_done, 1)
            chunk_pe(0, 0)
            chunk_pe(0, 1)
            wait(pe, tail.drains(0, "st1"))
            pe.sem_inc(tail.full, 1)
            pe.wait_ge(wo_in, 16 * 2)
            with pe.Fori(0, B - 1) as b:
                chunk_pe(b, 2)
                chunk_pe(b, 3)
                turn_x(b + 1)
                average(b)
                wait(pe, front.drains(b + 1, "hT1"))
                project(b + 1, "q", wq_s)
                average_dev(b)
                project(b + 1, "k", wk_s, [0])
                out_rows(b)
                project(b + 1, "k", wk_s, [1])
                project(b + 1, "g", wg_s)
                rows_v_k(b + 1)
                chunk_pe(b + 1, 0)
                router(b)
                chunk_pe(b + 1, 1)
                rank(b)
            b = B - 1
            chunk_pe(b, 2)
            chunk_pe(b, 3)
            average(b)
            average_dev(b)
            out_rows(b)
            wait(pe, tail.drains(b, "wo23"))
            pe.sem_inc(tail.full, 1)
            router(b)
            wait(pe, tail.drains(b, "logits"))
            pe.sem_inc(tail.full, 1)
            rank(b)

            pe.wait_ge(pad_ready, 1)
            mm(ps[2][0:E, 0:1], carry[:, 0, :], ident[:, 0:1], start=True, stop=True).then_inc(table_pe, 1)
            pe.wait_ge(tls_ready, 1)
            mm(ps[3][0:E, 0:1], tri[0:E, 0:E], tls[:, :], start=True, stop=True).then_inc(table_pe, 1)
            pe.wait_ge(tls_ready, 2)
            mm(ps[3][0:1, 128:128 + 2 * N_TILES], ones[0:E, 0:1], tab[:, :, :].rearrange("e a n -> e (a n)"),
               start=True, stop=True).then_inc(table_pe, 1)
            pe.wait_ge(tab_ready, 2)
            wait(pe, tail.drains(B - 1, "rank"))
            pe.wait_ge(we_in, 16 * 3 * E)
            pe.sem_inc(it_full, 2)
            pe.sem_inc(dn_full, 2)

            def weights(e, o, n):
                return we[:, bass.ds(e, 1), o:o + n].rearrange("p a n -> p (a n)")

            def turn_rows(i, s, n):
                pe.wait_ge(row_in[s % 2], 16 * n)
                if not (isinstance(i, int) and i < 1):
                    pe.wait_ge(rt_dve, i)
                for k in range(FT):
                    last = tr(ps[4][:, k * P:(k + 1) * P], rows[s % 2][:, k * P:(k + 1) * P], ident[:, :])
                last.then_inc(rt_full, 1)

            def up(i, s, e, which, done):
                for k in range(FT):
                    last = mm(ps[2 * (s % 2) + which][:, :], rT[s % 2][:, k, :],
                              weights(e, (which * FT + k) * F, F), start=k == 0, stop=k == FT - 1)
                last.then_inc(done, 1)

            def turn_hidden(i, s):
                pe.wait_ge(in_done, 2 * i + 6)
                pe.wait_ge(it_act, i + 1)
                for k in range(KF):
                    last = tr(ps[5][:, k * P:(k + 1) * P], ein[s % 2][:, k * P:(k + 1) * P], ident[:, :])
                last.then_inc(it_full, 1)

            def down(i, s):
                e = pe.value_load(tabi[0:1, 1, bass.ds(i, 1)], min_val=0, max_val=E - 1)
                pe.wait_ge(it_act, i + 2)
                pe.wait_ge(y_done, i + 1)
                for k in range(KF):
                    last = mm(ps[6 + s % 2][:, 0:D], eit[s % 2][:, k, :], weights(e, 2 * FT * F + k * D, D),
                              start=k == 0, stop=k == KF - 1)
                last.then_inc(dn_full, 1)

            def pe_step(i, s):
                const = isinstance(i, int)
                here = not (const and i >= N_TILES)
                before = not (const and not 0 <= i - 1 < N_TILES)
                if here:
                    e = pe.value_load(tabi[0:1, 1, bass.ds(i, 1)], min_val=0, max_val=E - 1)
                    pe.wait_ge(rt_dve, i + 1)
                    pe.wait_ge(in_done, 2 * i + 2)
                    up(i, s, e, 0, up0_full)
                if before:
                    turn_hidden(i - 1, s - 1)
                if not (const and i + 1 >= N_TILES):
                    turn_rows(i + 1, s + 1, row_loads(i + 1, s + 1))
                if here:
                    up(i, s, e, 1, up1_full)
                if before:
                    down(i - 1, s - 1)

            turn_rows(0, 0, 1)
            run_steps(pe, pe_step)


_INS = ["attn_x", "attn_wq", "attn_bq", "attn_wk", "attn_bk", "attn_wv", "attn_bv", "attn_wg", "attn_bg", "attn_wo",
        "attn_bo", "attn_gn_w", "attn_gn_b", "attn_gamma", "ffn_gate_kernel", "ffn_w0_kernel", "ffn_w1_kernel",
        "ffn_wo_kernel", "c", "wmod"]


def kernel(**inputs):
    import numpy as _np
    import concourse.bacc as _bacc
    from concourse import mybir as _mybir
    from concourse.bass_utils import run_bass_kernel_spmd as _run

    nc = _bacc.Bacc("TRN2", target_bir_lowering=False, num_devices=1)
    arrays, args = {}, []
    for name in _INS:
        a = _np.ascontiguousarray(inputs[f"L0_{name}"])
        arrays[f"in_{name}_dram"] = a
        args.append(nc.dram_tensor(f"in_{name}_dram", a.shape, _mybir.dt.from_np(a.dtype), kind="ExternalInput").ap())
    o = nc.dram_tensor("out_0_dram", [NTOK + P, D], F32, kind="ExternalOutput").ap()
    adaln_block(nc, *args, o)
    r = _run(nc, [arrays], core_ids=[0])
    return r.results[0]["out_0_dram"][:NTOK].reshape(B, S, D)
```

```python
from contextlib import ExitStack

import concourse.bass as bass
from concourse import mybir

F32 = mybir.dt.float32
F32R = mybir.dt.float32r
I32 = mybir.dt.int32
U32 = mybir.dt.uint32
ALU = mybir.AluOpType
ACT = mybir.ActivationFunctionType
AX = mybir.AxisListType

P = 128
B, S, D = 4, 512, 256
H, DH = 16, 16
FT = D // P
HPT = H // FT
NC = S // P
NTOK = B * S
E, F = 8, 512
KF = F // P
TOPK = 2
EPS = 1e-5
COMB, TOK, BAT, ROW = D, D + E, D + E + 1, D + E + 2
META = ROW - D
REGION = NTOK + P
PAD_ROW = E * REGION
N_TILES = (NTOK * TOPK + E * (P - 1)) // P
EARLY = 9
assert EARLY <= -(-((B - 2) * S * TOPK - E * (P - 1)) // P)
WE = FT * F * 2 + KF * D

FRONT = [("hT0", "act"), ("hT1", "act"), ("q0", "act"), ("q1", "act"), ("k0", "act"), ("k1", "act"),
         ("g0", "act"), ("g1", "act"), ("v01", "dve"), ("kd01", "dve"), ("kd2", "dve"), ("v23", "dve")]
TAIL = [("st0", "dve"), ("h2T0", "act"), ("h2T1", "act"), ("st1", "dve"), ("logits", "dve"), ("st2", "dve"),
        ("rank", "dve"), ("gn", "dve"), ("wo01", "dve"), ("wo23", "dve")]
LATER = ("h2T0", "h2T1", "logits", "rank")
CREDIT = 2


class Ring:

    def __init__(self, items, banks, full, drained, later=()):
        self.names = [n for n, _ in items]
        self.who = [w for _, w in items]
        self.banks, self.full, self.drained, self.later = banks, full, drained, later

    def round(self, b, name):
        return b + 1 if name in self.later else b

    def bank(self, name):
        return self.banks[self.names.index(name) % 2]

    def filled(self, b, name):
        return self.round(b, name) * len(self.names) + (self.names.index(name) + 1)

    def drains(self, b, name):
        return self.count(self.round(b, name), self.names.index(name))

    def count(self, r, i):
        w = self.who[i]
        return self.drained[w], r * self.who.count(w) + (CREDIT + self.who[:i + 1].count(w))

    def free(self, b, name):
        i, r = self.names.index(name), self.round(b, name)
        if i >= 2:
            return self.count(r, i - 2)
        w = self.who[i - 2]
        return self.drained[w], r * self.who.count(w) + (CREDIT - (1 - i))


def adaln_block(nc, x, wq, bq, wk, bk, wv, bv, wg, bg, wo, bo, gn_w, gn_b, gamma,
                gate_k, w0, w1, wo_e, c, wmod, out):
    ctx = ExitStack()
    with ctx:
        offset = {}

        def sb(name, shape, dt=F32):
            offset[name] = nc.sbuf_base
            return ctx.enter_context(nc.sbuf_tensor(name, shape, dt))

        def sem(name):
            return ctx.enter_context(nc.semaphore(name))

        ctx.enter_context(nc.allow_non_contiguous_dma(reason="small vectors"))

        routed = nc.dram_tensor("routed", [PAD_ROW + P, ROW], F32, kind="Internal").ap()
        gb_dram = nc.dram_tensor("gb_dram", [B, D], F32, kind="Internal").ap()
        gsc_dram = nc.dram_tensor("gsc_dram", [B, 3 * D], F32, kind="Internal").ap()

        xs = sb("xs", [P, B * NC, D])
        wq_s, wk_s, wv_s, wg_s, wo_s = (sb(n, [P, FT, D]) for n in ("wq_s", "wk_s", "wv_s", "wg_s", "wo_s"))
        gate_s = sb("gate_s", [P, FT, E])
        we = sb("we", [P, E, WE])
        wmod_s = we[:, E - 1, :].rearrange("p (k n) -> p k n", k=FT)
        siluT = sb("siluT", [P, FT, B])
        bq_s, bk_s, bg_s, bgh_s, gnw_s, gnb_s, gcol = (
            sb(n, [P, FT]) for n in ("bq_s", "bk_s", "bg_s", "bgh_s", "gnw_s", "gnb_s", "gcol"))
        bv_bc, bo_bc = sb("bv_bc", [P, D]), sb("bo_bc", [P, D])
        gam_bc = sb("gam_bc", [P, H])
        ident, tri, ones, blk, blkavg = (sb(n, [P, P]) for n in ("ident", "tri", "ones", "blk", "blkavg"))
        hmask = sb("hmask", [P, HPT])
        mhalf = sb("mhalf", [P, 2 * NC])
        erow_i, erow = sb("erow_i", [P, E], I32), sb("erow", [P, E])
        ebase_i, ebase = sb("ebase_i", [P, E], I32), sb("ebase", [P, E])
        tokid = sb("tokid", [P, B * NC], I32)
        batid = sb("batid", [P, B * NC], I32)
        saT, ca1T = sb("saT", [P, FT, B]), sb("ca1T", [P, FT, B])
        gsc = sb("gsc", [P, B, 3 * D])
        dmask = sb("dmask", [P, H, P])
        qdec = sb("qdec", [P, FT, P + 1])
        kdec = sb("kdec", [P, H])
        mv1 = sb("mv1", [P, B * NC, 2])
        ve1, rs1, nmr1 = sb("ve1", [P, B * NC]), sb("rs1", [P, B * NC]), sb("nmr1", [P, B * NC])
        xn = sb("xn", [P, NC, D])
        hT = sb("hT", [P, FT, S])
        qT, kT, qd = sb("qT", [P, FT, S]), sb("kT", [P, FT, S]), sb("qd", [P, FT, S])
        qx = sb("qx", [P, FT, HPT * P])
        vx = sb("vx", [P, NC, 2 * D])
        kd = xn
        z = sb("z", [P, FT, S])
        sm = sb("sm", [P, 4, 4 * P])
        th, ro = sm[:, 0:2, :], sm[:, 2:4, :]
        stt = xn[:, NC - 1, :].rearrange("p (k n) -> p k n", k=FT)
        state = sb("state", [P, FT, P])
        gst, gmv, gav, gd, gd2, gve, grs, gA, gt, gB = (
            sb("gst", [P, FT, 6]), sb("gmv", [P, FT, 2]), sb("gav", [P, FT, 2]), sb("gd", [P, FT]),
            sb("gd2", [P, FT]), sb("gve", [P, FT]), sb("grs", [P, FT]), sb("gA", [P, FT]),
            sb("gt", [P, FT]), sb("gB", [P, FT]))
        st2, mv2, ve2, rs2 = sb("st2", [P, NC, 6]), sb("mv2", [P, NC, 2]), sb("ve2", [P, NC]), sb("rs2", [P, NC])
        h2 = sb("h2", [P, NC, ROW])
        h2T = hT
        wob = sb("wob", [P, FT, D])
        st1 = h2[:, 1, 0:B * NC * 6].rearrange("p (t k) -> p t k", k=6)
        tmpl = z[:, 0, 0:ROW]
        spare = we[0:B, E - 2, :]
        modrow = spare[:, 0:4 * D]
        msgn, mmag = (spare[:, (4 + 2 * u) * D:(6 + 2 * u) * D].rearrange("b (m d) -> b m d", m=2) for u in range(2))
        zeros = h2[:, 0, 0:P]
        c_s, c_t = kT[0:B, 0, 0:D], kT[0:B, 1, 0:D]
        lg, mx, ix = sb("lg", [P, NC, E]), sb("mx", [P, NC, 8]), sb("ix", [P, NC, 8], U32)
        ixf, oh, msk, cmb = (sb("ixf", [P, NC, 2]), sb("oh", [P, 2, NC, E]), sb("msk", [P, NC, E]),
                             sb("cmb", [P, 2, NC, E]))
        vd, vt, pk = sb("vd", [P, NC]), sb("vt", [P, NC]), sb("pk", [P, 2, NC])
        carry = sb("carry", [P, NC + 1, E])
        carry_early = sb("carry_early", [P, E])
        pos, posk, posf = sb("pos", [P, NC, E]), sb("posk", [P, 2, NC, E]), sb("posf", [P, 2, NC])
        idx = sb("idx", [P, 2, NC], I32)
        cnt, cnti, tls, stc, enc, bas = (sb("cnt", [E, 1]), sb("cnti", [E, 1], I32), sb("tls", [E, 1]),
                                         sb("stc", [E, 1]), sb("enc", [E, 1]), sb("bas", [E, 1]))
        ecol_i, ecol, tile_i, tile_f = (sb("ecol_i", [E, 1], I32), sb("ecol", [E, 1]),
                                        sb("tile_i", [E, N_TILES], I32), sb("tile_f", [E, N_TILES]))
        ge, ine, row0 = (hT[0:E, 0, 64 * u:64 * u + N_TILES] for u in range(3))
        tab = hT[0:E, 1, 0:2 * N_TILES].rearrange("e (a n) -> e a n", a=2)
        tabi = [sb(f"tabi{u}", [1, 2, N_TILES], I32) for u in range(2)]
        base0, tlf, done = sb("base0", [E, 1]), sb("tlf", [E, 1]), sb("done", [E, 1])
        padr, padi = sb("padr", [1, E]), sb("padi", [1, E], I32)
        rows = [w[:, :, :].rearrange("p k n -> p (k n)")[:, 0:ROW] for w in (wq_s, wk_s)]
        rT = [xn[:, 2 * u, :].rearrange("p (k n) -> p k n", k=FT) for u in range(2)]
        def half(name, shape, place, of):
            return nc.alloc_sbuf_tensor_at(name, shape, F32R, offset=offset[place] + 4 * of)

        rT_halves = half("rT_halves", [P, 2, 2, FT, P], "xn", 0)
        rT_hi, rT_lo = ([rT_halves[:, u, v, :, :] for u in range(2)] for v in range(2))
        w0_halves = half("w0_halves", [P, 2, FT * F], "vx", 0)
        w1_hi, w1_lo = half("w1_hi", [P, FT * F], "qT", 0), half("w1_lo", [P, FT * F], "kT", 0)
        w_hi, w_lo = [w0_halves[:, 0, :], w1_hi[:, :]], [w0_halves[:, 1, :], w1_lo[:, :]]
        eth = [sm[:, u, :] for u in range(2)]
        ein = [dmask[:, 4 * u:4 * u + 4, :].rearrange("p h n -> p (h n)") for u in range(2)]
        eit = [qx[:, u, 0:F].rearrange("p (k n) -> p k n", k=KF) for u in range(2)]
        ey = [wg_s[:, u, :] for u in range(2)]
        gbr = [wv_s[:, u, :] for u in range(2)]
        meta = [sb(f"meta{u}", [P, META]) for u in range(4)]

        ps = [ctx.enter_context(nc.psum_tensor(f"ps{i}", [P, 512], F32)) for i in range(8)]
        ret = [ps[0], ps[1]]
        sc = [ps[2], ps[3]]
        up_ps = [[ps[2], ps[3]], [ps[0], ps[1]]]
        down_ps = ps[6][:, 0:D]
        table_ps = ps[7][:, D:2 * D]
        front = Ring(FRONT, [ps[4], ps[5]], sem("front_full"), {"act": sem("front_act"), "dve": sem("front_dve")})
        tail = Ring(TAIL, [ps[6], ps[7]], sem("tail_full"), {"act": sem("tail_act"), "dve": sem("tail_dve")},
                    LATER)

        def sems(names):
            return [sem(n) for n in names.split()]

        c_in, wmod_in, small_in, w_in, wo_in, we_in, gsc_in = sems("c_in wmod_in small_in w_in wo_in we_in gsc_in")
        x_in = sems("x_in0 x_in1 x_in2 x_in3")
        const_zero, const_ready, tmpl_ready, dve_const = sems("const_zero const_ready tmpl_ready dve_const")
        setup_chain, ln1_chain, front_chain, tail_chain, table_chain = sems(
            "setup_chain ln1_chain front_chain tail_chain table_chain")
        tanh_c, silu_ready, setup_pe, modT_ready, modrow_ready, bgh_ready, setup_done = sems(
            "tanh_c silu_ready setup_pe modT_ready modrow_ready bgh_ready setup_done")
        gb_out, gsc_out, tmpl_out, tmpl_zero = sems("gb_out gsc_out tmpl_out tmpl_zero")
        wob_ready, bog_ready, x1_ready = sems("wob_ready bog_ready x1_ready")
        var1, rstd1, shift1, xn_ready, qd_ready, qx_pool, qx_act, z_ready = sems(
            "var1 rstd1 shift1 xn_ready qd_ready qx_pool qx_act z_ready")
        scored, masked, pv_done, state_up = sems("scored masked pv_done state_up")
        gn_stat, gn_full, gn_dev, grstd, gn_ab, ro_ready, prod_ready = sems(
            "gn_stat gn_full gn_dev grstd gn_ab ro_ready prod_ready")
        x2_out, x2_last, var2, rstd2, h2n_ready, h2m_ready, h2_ready, row_ready = sems(
            "x2_out x2_last var2 rstd2 h2n_ready h2m_ready h2_ready row_ready")
        vd_ready, vt_ready, msk_ready, idx_ready, scattered, h2_free = sems(
            "vd_ready vt_ready msk_ready idx_ready scattered h2_free")
        pad_ready, pad_early, pad_out, tls_ready, table_pe, tab_ready = sems(
            "pad_ready pad_early pad_out tls_ready table_pe tab_ready")
        row_in, gbr_in = sems("row_in0 row_in1"), sems("gbr_in0 gbr_in1")
        rt_full, rt_dve, row_used, up0_full, up1_full, th_done, in_done, it_full, it_act, dn_full, y_done = sems(
            "rt_full rt_dve row_used up0_full up1_full th_done in_done it_full it_act dn_full y_done")
        added, added_ok, pool_passed, dve_passed, act_passed = sems("added added_ok pool_passed dve_passed act_passed")
        rt_hi, w_hi_ready, w_lo_ready = sem("rt_hi"), sems("w0_hi_ready w1_hi_ready"), sems("w0_lo_ready w1_lo_ready")
        SMALL, CONSTS = 16 * 10, 12
        N_FRONT_CHAIN, N_TAIL_CHAIN = 4, 42

        def row_loads(i, s):
            if isinstance(i, int):
                return i // 2 + 1
            return loop_loads[0] + s // 2 + 1

        def gbr_value(i, s):
            return gbr_in[s % 2], 16 * row_loads(i, s)

        loop_loads = [None]

        def run_steps(eng, step, first=0):
            loops = (N_TILES - 1 - EARLY) // 4
            for i in range(first, EARLY):
                step(i, i)
            eng.wait_ge(tab_ready, 4)
            with eng.Fori(0, loops) as j:
                loop_loads[0] = 2 * j
                for s in range(EARLY, EARLY + 4):
                    step(4 * j + s, s)
            for i in range(EARLY + 4 * loops, N_TILES + 2):
                step(i, i)

        def expert_up(e, which):
            return we[:, bass.ds(e, 1), which * FT * F:(which + 1) * FT * F].rearrange("p a n -> p (a n)")

        def early(i):
            return isinstance(i, int) and i < EARLY

        def table(i):
            return tabi[0] if early(i) else tabi[1]

        def heads(ap, pairs):
            base = [list(d) for d in ap.ap]
            return bass.AP(ap.tensor, ap.offset, [base[0], [4 * DH, pairs], [3 * DH, 2], [1, DH]])

        x_v = x.rearrange("b (t p) d -> b p t d", p=P)
        out_v = out[0:NTOK, :].rearrange("(b t p) d -> b p t d", p=P, t=NC)
        wk_v = lambda w: w.rearrange("(k p) n -> p k n", p=P)
        col = lambda v: v.rearrange("(k p) -> p k", p=P)
        wmod_v = wk_v(wmod)
        we_v = [(0, w0, FT, F), (FT * F, w1, FT, F), (2 * FT * F, wo_e, KF, D)]
        w0e = lambda e, k: we[:, e, k * F:(k + 1) * F]

        def tail_bank(b, name):
            return ps[7] if isinstance(b, int) and b == B - 1 and name in LATER else tail.bank(name)

        def wait(eng, pair):
            eng.wait_ge(pair[0], pair[1])

        def settle(eng, pairs, passed):
            for s, v in pairs:
                eng.wait_ge(s, v)
            eng.sem_inc(passed, 1)

        def tile_of_x(i):
            return xs[:, bass.ds(i, 1), :].rearrange("p a d -> p (a d)")

        def grp(b, n):
            return b * (4 * NC) + n

        block = ctx.enter_context(nc.Block())

        @block.sync
        def _(sp):
            def load_x(b):
                sp.dma_start(xs[:, b * NC:(b + 1) * NC, :], x_v[b]).then_inc(x_in[b], 16)

            def load_expert(e):
                for o, w, k, n in we_v:
                    sp.dma_start(we[:, e, o:o + k * n].rearrange("p (k n) -> p k n", k=k),
                                 w[e].rearrange("(k p) n -> p k n", p=P)).then_inc(we_in, 16)

            sp.dma_start(c_s, c).then_inc(c_in, 16)
            load_x(0)
            sp.dma_start(wmod_s, wmod_v).then_inc(wmod_in, 16)
            for s, d in ((wq_s, wq), (wk_s, wk), (wg_s, wg), (wv_s, wv)):
                sp.dma_start(s[:, :, :], wk_v(d)).then_inc(w_in, 16)
            for b in range(1, B):
                load_x(b)
            sp.dma_start(wo_s[:, :, :], wk_v(wo)).then_inc(wo_in, 16)
            sp.dma_start(gate_s[:, :, :], wk_v(gate_k)).then_inc(wo_in, 16)
            sp.wait_ge(modrow_ready, 1)
            sp.dma_start(gsc_dram, modrow[:, 0:3 * D]).then_inc(gsc_out, 16)
            sp.dma_start(gb_dram, modrow[:, 3 * D:4 * D]).then_inc(gb_out, 16)
            sp.wait_ge(gsc_out, 16)
            sp.dma_start(gsc[:, :, :].rearrange("p b n -> p (b n)"),
                         gsc_dram.rearrange("b n -> (b n)").partition_broadcast(P)).then_inc(gsc_in, 16)
            for e in range(E - 2):
                load_expert(e)
            sp.wait_ge(setup_pe, 3)
            sp.wait_ge(gb_out, 16)
            load_expert(E - 2)
            load_expert(E - 1)
            def store_x(b, done_sem):
                wait(sp, tail.drains(b, "wo23"))
                sp.dma_start(out_v[bass.ds(b, 1)].rearrange("b p t d -> p (b t) d"),
                             xs[:, bass.ds(b * NC, NC), :]).then_inc(done_sem, 16)

            with sp.Fori(0, B - 1) as b:
                store_x(b, x2_out)

            def load_rows(i, s):
                r = sp.value_load(table(i)[0:1, 0, bass.ds(i, 1)], min_val=0, max_val=PAD_ROW)
                sp.wait_ge(row_used, i + 1)
                sp.dma_start(rows[s % 2], routed[bass.ds(r, P), :]).then_inc(row_in[s % 2], 16)

            sp.wait_ge(tab_ready, 2)
            sp.wait_ge(h2_free, B - 1)
            for i in range(EARLY):
                load_rows(i, i)
                if i == 2:
                    store_x(B - 1, x2_last)
                if i == 7:
                    sp.wait_ge(tmpl_ready, 1)
                    sp.dma_start(routed[PAD_ROW:PAD_ROW + P, :], tmpl).then_inc(tmpl_out, 16)
                    sp.wait_ge(pad_ready, 1)
                    for e in range(E):
                        r = sp.value_load(padi[0:1, e:e + 1], min_val=0, max_val=PAD_ROW - P)
                        sp.dma_start(routed[bass.ds(r, P), :], tmpl).then_inc(pad_out, 16)
            sp.wait_ge(tab_ready, 4)
            sp.wait_ge(tmpl_out, 16)
            sp.wait_ge(pad_out, 16 * E)
            sp.wait_ge(scattered, 16 * TOPK * NC * B)
            loads = (N_TILES - EARLY) // 4
            with sp.Fori(0, loads) as j:
                for s in range(EARLY, EARLY + 4):
                    load_rows(4 * j + s, s)
            for i in range(EARLY + 4 * loads, N_TILES):
                load_rows(i, i)
            sp.wait_ge(x2_last, 16)
            sp.wait_ge(x2_out, 16 * (B - 1))
            sp.wait_ge(gb_out, 16)
            sp.wait_ge(added, 16 * N_TILES)

        @block.gpsimd
        def _(pool):
            g = nc.gpsimd
            for t, value in ((ident[:, :], 0.0), (tri[:, :], 1.0), (blk[:, :], 1.0), (hmask[:, :], 1.0)):
                last = g.memset(t, value)
            last.then_inc(const_zero, 1)
            pool.wait_ge(const_zero, 1)
            g.affine_select(out=ident[:, :], in_=ident[:, :], compare_op=ALU.not_equal, fill=1.0, base=0,
                            pattern=[[-1, P]], channel_multiplier=1).then_inc(const_ready, 1)
            g.affine_select(out=tri[:, :], in_=tri[:, :], compare_op=ALU.is_gt, fill=0.0, base=0,
                            pattern=[[1, P]], channel_multiplier=-1).then_inc(const_ready, 1)
            blk3 = blk[:, :].rearrange("p (h d) -> p h d", d=DH)
            g.affine_select(out=blk3, in_=blk3, compare_op=ALU.is_ge, fill=0.0, base=0,
                            pattern=[[-DH, HPT], [0, DH]], channel_multiplier=1).then_inc(const_ready, 1)
            g.affine_select(out=hmask[:, :], in_=hmask[:, :], compare_op=ALU.is_ge, fill=0.0, base=0,
                            pattern=[[-DH, HPT]], channel_multiplier=1).then_inc(const_ready, 1)
            pool.wait_ge(const_ready, 4)
            g.affine_select(out=blk3, in_=blk3, compare_op=ALU.is_ge, fill=0.0, base=DH - 1,
                            pattern=[[DH, HPT], [0, DH]], channel_multiplier=-1).then_inc(const_ready, 1)
            g.affine_select(out=hmask[:, :], in_=hmask[:, :], compare_op=ALU.is_ge, fill=0.0, base=DH - 1,
                            pattern=[[DH, HPT]], channel_multiplier=-1).then_inc(const_ready, 1)
            g.iota(erow_i[:, :], [[1, E]], base=0, channel_multiplier=0).then_inc(const_ready, 1)
            g.iota(ebase_i[:, :], [[REGION, E]], base=0, channel_multiplier=0).then_inc(const_ready, 1)
            g.iota(tokid[:, :], [[P, B * NC]], base=0, channel_multiplier=1).then_inc(const_ready, 1)
            g.iota(batid[:, :].rearrange("p (b t) -> p b t", b=B), [[1, B], [0, NC]], base=0,
                   channel_multiplier=0).then_inc(const_ready, 1)
            g.iota(ecol_i[:, :], [[0, 1]], base=0, channel_multiplier=1).then_inc(const_ready, 1)
            g.iota(tile_i[:, :], [[1, N_TILES]], base=0, channel_multiplier=0).then_inc(const_ready, 1)

            def power(out_, in_, n, done):
                g.tensor_tensor(out_, in_, mhalf[:, 0:n], ALU.pow).then_inc(done, 1)

            def expand_q(b, c):
                if c == 0:
                    wait(pool, front.drains(b, "q0"))
                pool.wait_ge(scored, grp(b, 4 + 4 * (c - 1) + 2))
                q = qT[:, 0, c * P:(c + 1) * P].unsqueeze(1).broadcast_to([P, HPT, P])
                m = hmask[:, :].unsqueeze(2).broadcast_to([P, HPT, P])
                g.tensor_tensor(qx[:, 0, :].rearrange("p (h n) -> p h n", h=HPT), q, m, ALU.mult).then_inc(qx_pool, 1)

            def group_power(b):
                wait(pool, tail.drains(b, "gn"))
                power(grs[:, :], gve[:, :], FT, grstd)

            def modulate(b):
                pool.wait_ge(var2, b + 1)
                power(rs2[:, :], ve2[:, :], NC, rstd2)
                hv = h2[:, :, 0:D]
                pool.wait_ge(h2n_ready, NC * b + NC)
                g.tensor_tensor(hv, hv, gsc[:, bass.ds(b, 1), 2 * D:3 * D].broadcast_to([P, NC, D]),
                                ALU.mult).then_inc(h2m_ready, 1)
                pool.wait_ge(h2m_ready, b + 1)
                g.tensor_tensor(hv, hv, gsc[:, bass.ds(b, 1), D:2 * D].broadcast_to([P, NC, D]),
                                ALU.add).then_inc(h2_ready, 1)

            def scale_wo(b):
                if not (isinstance(b, int) and b == 0):
                    settle(pool, [(tail.full, tail.filled(b - 1, "wo23"))], pool_passed)
                g.tensor_tensor(wob[:, :, :], wo_s[:, :, :], gsc[:, bass.ds(b, 1), 0:D].broadcast_to([P, FT, D]),
                                ALU.mult).then_inc(wob_ready, 1)

            def add_bias(b):
                bog = gsc[:, bass.ds(b, 1), 0:D]
                settle(pool, [(wob_ready, b + 1)], pool_passed)
                g.tensor_tensor(bog, bog, bo_bc[:, :].unsqueeze(1), ALU.mult).then_inc(bog_ready, 1)
                xb = xs[:, bass.ds(NC * b, NC), :]
                settle(pool, [(bog_ready, b + 1)], pool_passed)
                g.tensor_tensor(xb, xb, bog.broadcast_to([P, NC, D]), ALU.add).then_inc(x1_ready, 1)

            def scatter(b, tiles):
                if 0 in tiles:
                    settle(pool, [(idx_ready, b + 1), (row_ready, b + 1)], pool_passed)
                for t in tiles:
                    for k in range(TOPK):
                        g.indirect_dma_start(routed, bass.IndirectOffsetOnAxis(ap=idx[:, k, t:t + 1], axis=0),
                                             h2[:, t, :], None).then_inc(scattered, 16)

            def scatter_done(b):
                pool.wait_ge(scattered, 16 * (TOPK * NC) * b + 16 * (TOPK * NC))
                pool.sem_inc(h2_free, 1)

            pool.wait_ge(dve_const, 2)
            pool.wait_ge(var1, 1)
            power(rs1[:, 0:NC], ve1[:, 0:NC], NC, rstd1)
            pool.sem_inc(h2_free, 1)
            pool.wait_ge(const_ready, CONSTS)
            expand_q(0, 0)
            pool.wait_ge(var1, 2)
            power(rs1[:, NC:2 * NC], ve1[:, NC:2 * NC], NC, rstd1)
            expand_q(0, 1)
            pool.wait_ge(gsc_in, 16)
            pool.wait_ge(wo_in, 16 * 2)
            scale_wo(0)
            expand_q(0, 2)
            pool.wait_ge(var1, 4)
            power(rs1[:, 2 * NC:B * NC], ve1[:, 2 * NC:B * NC], 2 * NC, rstd1)
            expand_q(0, 3)
            add_bias(0)
            with pool.Fori(0, B - 1) as b:
                group_power(b)
                expand_q(b + 1, 0)
                modulate(b)
                expand_q(b + 1, 1)
                scale_wo(b + 1)
                expand_q(b + 1, 2)
                add_bias(b + 1)
                expand_q(b + 1, 3)
                scatter(b, range(NC))
                scatter_done(b)

            def fetch_gb(i, s):
                settle(pool, [(row_used, i + 3), (y_done, i + 1)], pool_passed)
                g.indirect_dma_start(gbr[s % 2], None, gb_dram, bass.IndirectOffsetOnAxis(
                    ap=meta[s % 4][:, BAT - D:BAT - D + 1].bitcast(I32), axis=0)).then_inc(gbr_in[s % 2], 16)

            def weights_lo(i, s):
                e = pool.value_load(table(i)[0:1, 1, bass.ds(i, 1)], min_val=0, max_val=E - 1)
                pool.wait_ge(w_hi_ready[1], i + (1 - EARLY))
                g.tensor_tensor(w_lo[1], expert_up(e, 1), w_hi[1].bitcast(F32), ALU.subtract)\
                    .then_inc(w_lo_ready[1], 1)

            def add_rows(i, s, first=False, last=False):
                if not last:
                    fetch_gb(i + 1, s + 1)
                if not first:
                    pool.wait_ge(added, 16 * i)
                    pool.sem_inc(added_ok, 1)
                settle(pool, [(y_done, i + 3)], pool_passed)
                g.indirect_dma_start(out, bass.IndirectOffsetOnAxis(
                    ap=meta[s % 4][:, TOK - D:TOK - D + 1].bitcast(I32), axis=0), ey[s % 2], None,
                    compute_op=ALU.add).then_inc(added, 16)
                if not (isinstance(i, int) and not EARLY <= i + 3 < N_TILES):
                    weights_lo(i + 3, s + 3)

            pool.sem_inc(added_ok, 4)
            group_power(B - 1)
            pool.wait_ge(gb_out, 16)
            pool.wait_ge(x2_out, 16 * (B - 1))
            fetch_gb(0, 0)
            pool.wait_ge(prod_ready, 2 * B)
            g.memset(tmpl, 0.0).then_inc(tmpl_zero, 1)
            pool.wait_ge(tmpl_zero, 1)
            g.iota(tmpl[:, TOK:TOK + 1].bitcast(I32), [[0, 1]], base=NTOK, channel_multiplier=1).then_inc(tmpl_ready, 1)
            modulate(B - 1)
            for i in range(EARLY):
                add_rows(i, i, first=i == 0)
                if 2 <= i < 2 + NC:
                    scatter(B - 1, (i - 2,))
                if i == EARLY - 4:
                    pool.wait_ge(tab_ready, 4)
            pool.wait_ge(x2_last, 16)
            loops = (N_TILES - 3 - EARLY) // 4
            with pool.Fori(0, loops) as j:
                for s in range(EARLY, EARLY + 4):
                    add_rows(4 * j + s, s)
            for i in range(EARLY + 4 * loops, N_TILES):
                add_rows(i, i, last=i == N_TILES - 1)

        @block.scalar
        def _(act):
            a = nc.scalar
            act.wait_ge(c_in, 16)
            a.activation(c_t, c_s, ACT.Tanh, scale=0.5).then_inc(tanh_c, 1)
            for s, v in ((bq_s, bq), (bk_s, bk), (bg_s, bg), (gnw_s, gn_w), (gnb_s, gn_b)):
                act.dma_start(s[:, :], col(v)).then_inc(small_in, 16)
            act.dma_start(bv_bc[:, :], bv.partition_broadcast(P)).then_inc(small_in, 16)
            act.dma_start(bo_bc[:, :], bo.partition_broadcast(P)).then_inc(small_in, 16)
            act.dma_start(gam_bc[:, :], gamma.partition_broadcast(P)).then_inc(small_in, 16)
            for ft in range(FT):
                act.dma_start(gcol[:, ft:ft + 1], gamma[ft * HPT:(ft + 1) * HPT].unsqueeze(1).unsqueeze(2)
                              .broadcast_to([HPT, DH, 1])).then_inc(small_in, 16)

            def normed(b):
                for t in range(NC):
                    i = NC * b + t
                    a.activation(xn[:, t, :], tile_of_x(i), ACT.Identity, scale=rs1[:, bass.ds(i, 1)],
                                 bias=nmr1[:, bass.ds(i, 1)]).then_inc(xn_ready, 1)

            def features(b):
                for ft in range(FT):
                    act.wait_ge(front.full, front.filled(b, f"hT{ft}"))
                    a.activation(hT[:, ft, :], front.bank(f"hT{ft}")[:, :], ACT.Identity,
                                 scale=ca1T[:, ft, bass.ds(b, 1)], bias=saT[:, ft, bass.ds(b, 1)])\
                        .then_inc(front.drained["act"], 1)

            def bias(b, n, dst, vec, tiles=range(FT)):
                for ft in tiles:
                    act.wait_ge(front.full, front.filled(b, f"{n}{ft}"))
                    a.activation(dst[:, ft, :], front.bank(f"{n}{ft}")[:, :], ACT.Identity,
                                 bias=vec[:, ft:ft + 1]).then_inc(front.drained["act"], 1)

            def gate(b):
                for ft in range(FT):
                    act.wait_ge(front.full, front.filled(b, f"g{ft}"))
                    a.activation(z[:, ft, :], front.bank(f"g{ft}")[:, :], ACT.Identity,
                                 bias=bg_s[:, ft:ft + 1]).then_inc(z_ready, 1)
                    a.activation(th[:, ft, :], front.bank(f"g{ft}")[:, :], ACT.Tanh, scale=0.5,
                                 bias=bgh_s[:, ft:ft + 1]).then_inc(front.drained["act"], 1)

            def expand_q(b, c):
                if c == 0:
                    wait(act, front.drains(b, "q1"))
                act.wait_ge(scored, grp(b, 4 + 4 * (c - 1) + 4))
                for h in range(HPT):
                    a.activation(qx[:, 1, h * P:(h + 1) * P], qT[:, 1, c * P:(c + 1) * P], ACT.Copy,
                                 scale=hmask[:, h:h + 1]).then_inc(qx_act, 1)

            def group_normed(b):
                act.wait_ge(gn_ab, b + 1)
                for ft in range(FT):
                    a.activation(ro[:, ft, :], ret[ft][:, :], ACT.Identity, scale=gA[:, ft:ft + 1],
                                 bias=gB[:, ft:ft + 1]).then_inc(ro_ready, 1)

            def h2_features(b, tiles=range(FT)):
                for ft in tiles:
                    act.wait_ge(tail.full, tail.filled(b, f"h2T{ft}"))
                    a.copy(h2T[:, ft, :], tail_bank(b, f"h2T{ft}")[:, :]).then_inc(tail.drained["act"], 1)

            def top_tanh(b):
                act.wait_ge(vd_ready, b + 1)
                a.activation(vt[:, :], vd[:, :], ACT.Tanh, scale=0.5).then_inc(vt_ready, 1)

            act.sem_inc(tail.drained["act"], CREDIT + 2)
            act.sem_inc(front.drained["act"], CREDIT)
            act.sem_inc(ro_ready, 2)
            act.wait_ge(shift1, 1)
            normed(0)
            act.wait_ge(modT_ready, 2)
            features(0)
            act.wait_ge(small_in, SMALL)
            a.mul(bgh_s[:, :], bg_s[:, :], 0.5).then_inc(bgh_ready, 1)
            bias(0, "q", qT, bq_s)
            bias(0, "k", kT, bk_s)
            act.wait_ge(bgh_ready, 1)
            gate(0)
            act.wait_ge(const_ready, CONSTS)
            expand_q(0, 0)
            expand_q(0, 1)
            expand_q(0, 2)
            act.wait_ge(shift1, 3)
            with act.Fori(0, B - 1) as b:
                expand_q(b, 3)
                act.wait_ge(state_up, 4 * b + 4)
                normed(b + 1)
                features(b + 1)
                bias(b + 1, "q", qT, bq_s)
                bias(b + 1, "k", kT, bk_s, [0])
                group_normed(b)
                bias(b + 1, "k", kT, bk_s, [1])
                act.wait_ge(prod_ready, 2 * b + 2)
                gate(b + 1)
                expand_q(b + 1, 0)
                expand_q(b + 1, 1)
                h2_features(b)
                top_tanh(b)
                expand_q(b + 1, 2)
            b = B - 1
            expand_q(b, 3)
            act.sem_inc(it_act, 1)

            def turn_back(i, s):
                act.wait_ge(it_full, i + 3)
                act.wait_ge(dn_full, i + 1)
                a.copy(eit[s % 2], ps[5][:, :].rearrange("p (k n) -> p k n", k=KF)).then_inc(it_act, 1)

            def tanh_part(i, s):
                act.wait_ge(up0_full, i + 1)
                act.wait_ge(in_done, 2 * i + 2)
                a.activation(eth[s % 2], up_ps[s % 2][0][:, :], ACT.Tanh, scale=0.5).then_inc(th_done, 1)

            def weights_hi(i, s, which):
                if isinstance(i, int) and i == EARLY:
                    act.wait_ge(tab_ready, 4)
                    act.wait_ge(we_in, 16 * 3 * E)
                e = act.value_load(table(i)[0:1, 1, bass.ds(i, 1)], min_val=0, max_val=E - 1)
                if not (isinstance(i, int) and i == EARLY):
                    settle(act, [((up0_full, up1_full)[which], i)], act_passed)
                a.copy(w_hi[which], expert_up(e, which)).then_inc(w_hi_ready[which], 1)

            def act_step(i, s, between=None):
                if not (isinstance(i, int) and not 0 <= i - 1 < N_TILES):
                    turn_back(i - 1, s - 1)
                if between is not None:
                    between()
                if not (isinstance(i, int) and i >= N_TILES):
                    tanh_part(i, s)
                if not (isinstance(i, int) and not EARLY <= i + 1 < N_TILES):
                    for which in range(2):
                        weights_hi(i + 1, s + 1, which)

            group_normed(b)
            for i in range(3):
                act_step(i, i)
            h2_features(b, [0])
            act_step(3, 3, between=lambda: h2_features(b, [1]))
            top_tanh(b)
            run_steps(act, act_step, first=4)

        @block.vector
        def _(dve):
            v = nc.vector

            class Chain:

                def __init__(self, s, per):
                    self.s, self.per, self.k = s, per, 0

                def start(self, b):
                    self.b, self.k = b, 0

                def inc(self, ins):
                    ins.then_inc(self.s, 1)
                    self.k += 1

                def value(self):
                    return self.s, self.b * self.per + self.k

                def wait(self):
                    dve.wait_ge(*self.value())

                def link(self, ins):
                    self.inc(ins)
                    self.wait()

                def end(self):
                    assert self.k == self.per, (self.s, self.k)

            setup, ln1, fr, tl, tb = (Chain(setup_chain, 0), Chain(ln1_chain, 0), Chain(front_chain, N_FRONT_CHAIN),
                                      Chain(tail_chain, N_TAIL_CHAIN), Chain(table_chain, 0))
            setup.start(0)
            ln1.start(0)
            v.memset(ones[:, :], 1.0).then_inc(dve_const, 1)
            setup.inc(v.memset(zeros, 0.0))
            v.memset(mhalf[:, :], -0.5).then_inc(dve_const, 1)
            setup.inc(v.memset(vx[:, :, :], 0.0))
            setup.inc(v.memset(carry[:, 0, :], 0.0))
            setup.inc(v.memset(h2[:, :, COMB:ROW], 0.0))
            dve.wait_ge(tanh_c, 1)
            setup.link(v.scalar_tensor_tensor(out=c_t, in0=c_t, scalar=1.0, in1=c_s,
                                              op0=ALU.add, op1=ALU.mult))
            v.tensor_scalar(c_t, c_t, 0.5, None, ALU.mult).then_inc(silu_ready, 1)
            dve.wait_ge(setup_pe, 1)
            v.tensor_copy(siluT[:, :, :], ps[4][:, 0:FT * B].rearrange("p (k b) -> p k b", k=FT))\
                .then_inc(silu_ready, 1)

            def norm_stats(chain, first, n, tiles, st, mv, ve, ready, between=None):
                for t in range(n):
                    chain.inc(v.bn_stats(st[:, tiles + t, :], tile_of_x(first + t)))
                if between is not None:
                    between()
                if isinstance(first, int):
                    chain.wait()
                else:
                    settle(dve, [chain.value()], dve_passed)
                for t in range(n):
                    chain.inc(v.bn_aggr(mv[:, tiles + t, :], st[:, tiles + t, :]))
                chain.wait()
                v.tensor_scalar(ve[:, tiles:tiles + n], mv[:, tiles:tiles + n, 1], EPS, None, ALU.add)\
                    .then_inc(ready, 1)

            dve.wait_ge(x_in[0], 16)
            norm_stats(ln1, 0, NC, 0, st1, mv1, ve1, var1)

            def shift(tiles, n):
                v.scalar_tensor_tensor(out=nmr1[:, tiles:tiles + n], in0=mv1[:, tiles:tiles + n, 0], scalar=-1.0,
                                       in1=rs1[:, tiles:tiles + n], op0=ALU.mult, op1=ALU.mult).then_inc(shift1, 1)

            dve.wait_ge(rstd1, 1)
            shift(0, NC)
            dve.wait_ge(setup_pe, 2)
            modT = ps[5][:, 0:2 * FT * B].rearrange("p (k b) -> p k b", b=B)
            v.tensor_copy(saT[:, :, :], modT[:, 0:FT, :]).then_inc(modT_ready, 1)
            v.tensor_scalar(ca1T[:, :, :], modT[:, FT:2 * FT, :], 1.0, None, ALU.add).then_inc(modT_ready, 1)
            dve.wait_ge(modT_ready, 2)
            dve.sem_inc(front.drained["dve"], CREDIT)
            dve.wait_ge(setup_pe, 3)
            setup.inc(v.tensor_copy(modrow[:, 0:512], ps[2][0:B, :]))
            setup.link(v.tensor_copy(modrow[:, 512:1024], ps[3][0:B, :]))
            gab = modrow.rearrange("b (m d) -> b m d", m=4)[:, 0:4:3, :]
            cb = modrow[:, 2 * D:3 * D]
            setup.inc(v.tensor_scalar(msgn, gab, 0.0, 2.0, ALU.is_ge, ALU.mult))
            setup.link(v.scalar_tensor_tensor(out=mmag, in0=gab, scalar=-1.0, in1=gab,
                                              op0=ALU.mult, op1=ALU.max))
            setup.link(v.tensor_scalar(mmag, mmag, 0.25, None, ALU.max))
            setup.inc(v.tensor_scalar(cb, cb, 1.0, None, ALU.add))
            setup.link(v.scalar_tensor_tensor(out=gab, in0=msgn, scalar=-1.0, in1=mmag,
                                              op0=ALU.add, op1=ALU.mult))
            v.tensor_copy(gve[:, :], ones[:, 0:FT]).then_inc(modrow_ready, 1)
            dve.wait_ge(small_in, SMALL)
            dve.wait_ge(const_ready, CONSTS)
            for h in range(H):
                setup.inc(v.tensor_tensor_scan(dmask[:, h, :], gam_bc[:, h:h + 1].to_broadcast([P, P]),
                                               ident[:, :], 0.0, ALU.mult, ALU.add))
            for ft in range(FT):
                setup.inc(v.memset(qdec[:, ft, 0:1], 1.0))
                setup.inc(v.tensor_tensor_scan(qdec[:, ft, 1:P + 1], gcol[:, ft:ft + 1].to_broadcast([P, P]),
                                               zeros, 1.0, ALU.mult, ALU.add))
            setup.wait()
            setup.inc(v.tensor_tensor(kdec[:, :], dmask[:, :, P - 1], gam_bc[:, :], ALU.mult))
            setup.inc(v.tensor_scalar(blkavg[:, :], blk[:, :], 1.0 / DH, None, ALU.mult))
            setup.inc(v.tensor_scalar(gnb_s[:, :], gnb_s[:, :], 0.5, None, ALU.mult))
            setup.inc(v.tensor_copy(erow[:, :], erow_i[:, :]))
            setup.inc(v.tensor_copy(ebase[:, :], ebase_i[:, :]))
            setup.inc(v.tensor_copy(ecol[:, :], ecol_i[:, :]))
            setup.inc(v.tensor_copy(tile_f[:, :], tile_i[:, :]))
            setup.wait()
            dve.sem_inc(tail.drained["dve"], CREDIT)
            dve.sem_inc(masked, 2)
            dve.sem_inc(setup_done, 1)

            def first_stats(b):
                dve.wait_ge(x_in[b], 16)
                norm_stats(ln1, b * NC, NC, b * NC, st1, mv1, ve1, var1)

            def decay_q(b):
                for ft in range(FT):
                    wait(dve, front.drains(b, f"q{ft}"))
                    v.tensor_tensor(qd[:, ft, :].rearrange("p (c n) -> p c n", c=NC),
                                    qT[:, ft, :].rearrange("p (c n) -> p c n", c=NC),
                                    qdec[:, ft, 0:P].unsqueeze(1).broadcast_to([P, NC, P]),
                                    ALU.mult).then_inc(qd_ready, 1)

            def gates(b):
                for ft in range(FT):
                    wait(dve, front.drains(b, f"g{ft}"))
                    zv = z[:, ft, :]
                    fr.inc(v.scalar_tensor_tensor(out=zv, in0=th[:, ft, :], scalar=1.0, in1=zv,
                                                  op0=ALU.add, op1=ALU.mult))

            def rows_v(b, n, t0):
                dve.wait_ge(front.full, front.filled(b, n))
                for t in range(2):
                    ins = v.tensor_tensor(heads(vx[:, t0 + t, :], H // 2),
                                          front.bank(n)[:, t * D:(t + 1) * D].rearrange("p (j q d) -> p j q d", q=2, d=DH),
                                          bv_bc[:, :].rearrange("p (j q d) -> p j q d", q=2, d=DH), ALU.add)
                    if t:
                        ins.then_inc(front.drained["dve"], 1)
                    else:
                        fr.inc(ins)

            def rows_k(b):
                for n, c0, m in (("kd01", 0, 2), ("kd2", 2, 1)):
                    dve.wait_ge(front.full, front.filled(b, n))
                    v.tensor_tensor(kd[:, c0:c0 + m, :].rearrange("p c (h d) -> p c h d", d=DH),
                                    front.bank(n)[:, 0:m * D].rearrange("p (c h d) -> p c h d", c=m, d=DH),
                                    kdec[:, :].unsqueeze(1).unsqueeze(3).broadcast_to([P, m, H, DH]),
                                    ALU.mult).then_inc(front.drained["dve"], 1)

            def chunk_dve(b, c, between={}):
                if c < NC - 1:
                    n = f"st{c}"
                    dve.wait_ge(tail.full, tail.filled(b, n))
                    if c == 2 and isinstance(b, int) and b == 0:
                        dve.sem_inc(tail.drained["dve"], 1)
                    dst = stt if c else state
                    v.tensor_tensor(dst[:, :, :], tail.bank(n)[:, 0:D].rearrange("p (k n) -> p k n", k=FT),
                                    blk[:, :].unsqueeze(1).broadcast_to([P, FT, P]),
                                    ALU.mult).then_inc(tail.drained["dve"], 1)
                    if c:
                        wait(dve, tail.drains(b, n))
                        if c > 1:
                            dve.wait_ge(state_up, 4 * b + 2)
                        for ft in range(FT):
                            v.scalar_tensor_tensor(out=state[:, ft, :], in0=state[:, ft, :],
                                                   scalar=qdec[:, ft, P:P + 1], in1=stt[:, ft, :],
                                                   op0=ALU.mult, op1=ALU.add).then_inc(state_up, 1)
                for g in range(4):
                    n = 4 * c + g
                    dve.wait_ge(scored, grp(b, n) + (4 + 1))
                    dve.wait_ge(pv_done, grp(b, n) + 1)
                    v.tensor_tensor(sm[:, g, :], sc[n % 2][:, :],
                                    dmask[:, 4 * g:4 * g + 4, :].rearrange("p h n -> p (h n)"),
                                    ALU.mult).then_inc(masked, 1)
                    for step in between.get(g, ()):
                        step()

            def group_norm(b, between=None):
                tl.start(b)
                settle(dve, [(pv_done, grp(b, 4 * NC) + 4)], dve_passed)
                for ft in range(FT):
                    tl.inc(v.bn_stats(gst[:, ft, :], ret[ft][:, :]))
                settle(dve, [tl.value()], dve_passed)
                tl.inc(v.bn_aggr(gmv[:, 0, :], gst[:, 0, :]))
                v.bn_aggr(gmv[:, 1, :], gst[:, 1, :]).then_inc(gn_stat, 1)
                dve.wait_ge(gn_full, b + 1)
                gb_ = tail.bank("gn")
                tl.link(v.tensor_copy(gav[:, :, :], gb_[:, 0:2 * FT].rearrange("p (k m) -> p k m", k=FT)))
                tl.link(v.tensor_tensor(gd[:, :], gmv[:, :, 0], gav[:, :, 0], ALU.subtract))
                v.tensor_tensor(gd2[:, :], gd[:, :], gd[:, :], ALU.mult).then_inc(gn_dev, 1)
                if between is not None:
                    between()
                dve.wait_ge(tail.full, tail.filled(b, "gn"))
                v.scalar_tensor_tensor(out=gve[:, :], in0=gb_[:, 8:8 + FT], scalar=EPS, in1=gav[:, :, 1],
                                       op0=ALU.add, op1=ALU.add).then_inc(tail.drained["dve"], 1)
                dve.wait_ge(grstd, b + 1)
                tl.link(v.scalar_tensor_tensor(out=gA[:, :], in0=grs[:, :], scalar=0.5, in1=gnw_s[:, :],
                                               op0=ALU.mult, op1=ALU.mult))
                tl.link(v.tensor_tensor(gt[:, :], gav[:, :, 0], gA[:, :], ALU.mult))
                v.tensor_tensor(gB[:, :], gnb_s[:, :], gt[:, :], ALU.subtract).then_inc(gn_ab, 1)

            def gated(b):
                for ft in range(FT):
                    dve.wait_ge(ro_ready, 2 * b + (2 + ft + 1))
                    v.tensor_tensor(ro[:, ft, :], ro[:, ft, :],
                                    z[:, ft, :],
                                    ALU.mult).then_inc(prod_ready, 1)

            def attention_out(b):
                dve.wait_ge(x1_ready, b + 1)
                for n, t0 in (("wo01", 0), ("wo23", 2)):
                    dve.wait_ge(tail.full, tail.filled(b, n))
                    att = tail.bank(n)[:, :].rearrange("p (t d) -> p t d", t=2)
                    xv = xs[:, bass.ds(NC * b + t0, 2), :]
                    v.tensor_tensor(xv, xv, att, ALU.add).then_inc(tail.drained["dve"], 1)

            def second_stats(b, between=None):
                settle(dve, [tail.drains(b, "wo23")], dve_passed)
                norm_stats(tl, NC * b, NC, 0, st2, mv2, ve2, var2, between)

            def second_norm(b):
                dve.wait_ge(rstd2, b + 1)
                dve.wait_ge(h2_free, b + 1)
                for t in range(NC):
                    v.tensor_scalar(h2[:, t, 0:D], tile_of_x(NC * b + t), mv2[:, t, 0:1], rs2[:, t:t + 1],
                                    ALU.subtract, ALU.mult).then_inc(h2n_ready, 1)

            def take_logits(b):
                dve.wait_ge(tail.full, tail.filled(b, "logits"))
                v.tensor_copy(lg[:, :, :], tail_bank(b, "logits")[:, 0:NC * E].rearrange("p (t e) -> p t e", e=E))\
                    .then_inc(tail.drained["dve"], 1)

            def choose_top(b):
                settle(dve, [tail.drains(b, "logits")], dve_passed)
                for t in range(NC):
                    tl.inc(v.max(mx[:, t, :], lg[:, t, :]))
                tl.wait()
                v.tensor_tensor(vd[:, :], mx[:, :, 0], mx[:, :, 1], ALU.subtract).then_inc(vd_ready, 1)

            def choose_places(b):
                for t in range(NC):
                    tl.inc(v.max_index(ix[:, t, :], mx[:, t, :], lg[:, t, :]))
                tl.wait()
                tl.link(v.tensor_copy(ixf[:, :, :], ix[:, :, 0:TOPK]))
                for k in range(TOPK):
                    tl.inc(v.tensor_tensor(oh[:, k, :, :], erow[:, :].unsqueeze(1).broadcast_to([P, NC, E]),
                                           ixf[:, :, k:k + 1].broadcast_to([P, NC, E]), ALU.is_equal))
                tl.wait()
                v.tensor_tensor(msk[:, :, :], oh[:, 0, :, :], oh[:, 1, :, :], ALU.add).then_inc(msk_ready, 1)

            def choose_weights(b):
                tl.inc(v.tensor_copy(h2[:, :, TOK:TOK + 1].rearrange("p t a -> p (t a)").bitcast(I32),
                                     tokid[:, bass.ds(NC * b, NC)]))
                tl.inc(v.tensor_copy(h2[:, :, BAT:BAT + 1].rearrange("p t a -> p (t a)").bitcast(I32),
                                     batid[:, bass.ds(NC * b, NC)]))
                dve.wait_ge(vt_ready, b + 1)
                for k, sg in ((0, 0.25), (1, -0.25)):
                    tl.inc(v.tensor_scalar(pk[:, k, :], vt[:, :], sg, 0.25, ALU.mult, ALU.add))
                tl.wait()
                for k in range(TOPK):
                    tl.inc(v.tensor_tensor(cmb[:, k, :, :], oh[:, k, :, :],
                                           pk[:, k, :].unsqueeze(2).broadcast_to([P, NC, E]), ALU.mult))
                tl.wait()
                v.tensor_tensor(h2[:, :, COMB:COMB + E], cmb[:, 0, :, :], cmb[:, 1, :, :],
                                ALU.add).then_inc(row_ready, 1)

            def places(b):
                dve.wait_ge(tail.full, tail.filled(b, "rank"))
                rk = tail_bank(b, "rank")
                tl.inc(v.tensor_copy(carry_early[:, :], carry[:, 0, :]))
                for t in range(NC):
                    tl.link(v.tensor_tensor(carry[:, t + 1, :], carry[:, t, :],
                                            rk[:, 64 + E * t:64 + E * t + E], ALU.add))
                v.tensor_tensor(pos[:, :, :], rk[:, 0:NC * E].rearrange("p (t e) -> p t e", e=E),
                                carry[:, 0:NC, :], ALU.add).then_inc(tail.drained["dve"], 1)

            def rows_of_tokens(b):
                wait(dve, tail.drains(b, "rank"))
                tl.link(v.tensor_tensor(pos[:, :, :], pos[:, :, :], ebase[:, :].unsqueeze(1).broadcast_to([P, NC, E]), ALU.add))
                for k in range(TOPK):
                    tl.inc(v.tensor_tensor(posk[:, k, :, :], oh[:, k, :, :], pos[:, :, :], ALU.mult))
                tl.wait()
                tl.link(v.tensor_reduce(posf[:, :, :], posk[:, :, :, :], AX.X, ALU.add))
                v.tensor_copy(idx[:, :, :], posf[:, :, :]).then_inc(idx_ready, 1)
                tl.link(v.tensor_copy(carry[:, 0, :], carry[:, NC, :]))
                tl.end()

            def chunks_0_to_2(b, before=None):
                if before is None:
                    chunk_dve(b, 0, {3: [lambda: first_stats(2)]})
                    chunk_dve(b, 1, {3: [lambda: first_stats(3)]})
                    chunk_dve(b, 2)
                    dve.wait_ge(rstd1, 3)
                    shift(2 * NC, 2 * NC)
                    return
                chunk_dve(b, 0, {1: [lambda: rows_v(b, "v23", 2)]})
                fr.end()
                chunk_dve(b, 1, {3: [lambda: take_logits(before), lambda: choose_top(before),
                                     lambda: choose_places(before)]})
                chunk_dve(b, 2, {1: [lambda: choose_weights(before)],
                                 3: [lambda: places(before), lambda: rows_of_tokens(before)]})

            decay_q(0)
            fr.start(0)
            rows_v(0, "v01", 0)
            rows_k(0)
            gates(0)
            fr.wait()
            first_stats(1)
            rows_v(0, "v23", 2)
            fr.end()
            dve.wait_ge(rstd1, 2)
            shift(NC, NC)
            chunks_0_to_2(0)
            dve.sem_inc(tail.drained["dve"], 1)
            dve.wait_ge(gsc_in, 16)
            with dve.Fori(0, B - 1) as b:
                chunk_dve(b, 3)
                group_norm(b)
                gated(b)
                decay_q(b + 1)
                attention_out(b)
                second_stats(b)
                fr.start(b + 1)
                rows_v(b + 1, "v01", 0)
                rows_k(b + 1)
                gates(b + 1)
                second_norm(b)
                fr.wait()
                chunks_0_to_2(b + 1, b)

            tb.start(0)

            def tiles_of_experts(rnd):
                if rnd:
                    tb.link(v.tensor_tensor(padr[:, :], carry[0:1, 0, :], ebase[0:1, :], ALU.add))
                    v.tensor_copy(padi[:, :], padr[:, :]).then_inc(pad_ready, 1)
                else:
                    tb.link(v.memset(done[:, :], 0.0))
                    v.tensor_scalar(base0[:, :], ecol[:, :], float(REGION), float(-PAD_ROW), ALU.mult, ALU.add)\
                        .then_inc(pad_early, 1)

            def tiles_before(rnd):
                dve.wait_ge(table_pe, 3 * rnd + 1)
                tb.link(v.tensor_scalar(cnti[:, :], table_ps[0:E, 0:1], float(P - 1) * rnd, None, ALU.add))
                tb.link(v.tensor_scalar(cnti[:, :], cnti[:, :], 7, None, ALU.logical_shift_right))
                tb.link(v.tensor_copy(tlf[:, :], cnti[:, :]))
                v.tensor_tensor(tls[:, :], tlf[:, :], done[:, :], ALU.subtract).then_inc(tls_ready, 1)

            def tile_columns(rnd):
                dve.wait_ge(table_pe, 3 * rnd + 2)
                dve.wait_ge(tls_ready, 2 * rnd + 1)
                tb.link(v.tensor_scalar(stc[:, :], table_ps[0:E, 1:2], float(EARLY * rnd), None, ALU.add))
                tb.inc(v.tensor_tensor(enc[:, :], stc[:, :], tls[:, :], ALU.add))
                tb.link(v.scalar_tensor_tensor(out=bas[:, :], in0=stc[:, :], scalar=float(-P), in1=base0[:, :],
                                               op0=ALU.mult, op1=ALU.add))
                tb.inc(v.tensor_scalar(ge, tile_f[:, :], stc[:, 0:1], None, ALU.is_ge))
                tb.link(v.scalar_tensor_tensor(out=bas[:, :], in0=done[:, :], scalar=float(P), in1=bas[:, :],
                                               op0=ALU.mult, op1=ALU.add))
                tb.inc(v.scalar_tensor_tensor(out=ine, in0=tile_f[:, :], scalar=enc[:, 0:1], in1=ge,
                                              op0=ALU.is_lt, op1=ALU.mult))
                tb.link(v.tensor_scalar(row0, tile_f[:, :], float(P), bas[:, 0:1], ALU.mult, ALU.add))
                tb.link(v.tensor_tensor(tab[:, 0, :], row0, ine, ALU.mult))
                v.tensor_scalar(tab[:, 1, :], ine, ecol[:, 0:1], None, ALU.mult).then_inc(tls_ready, 1)
                if not rnd:
                    tb.link(v.tensor_scalar(done[:, :], stc[:, :], -1.0, float(EARLY), ALU.mult, ALU.add))
                    tb.link(v.scalar_tensor_tensor(out=done[:, :], in0=done[:, :], scalar=0.0, in1=tls[:, :],
                                                   op0=ALU.max, op1=ALU.min))

            def table_rows(rnd):
                dve.wait_ge(table_pe, 3 * rnd + 3)
                if rnd:
                    tb.link(v.tensor_copy(tabi[1][:, :, 0:EARLY], tabi[0][:, :, 0:EARLY]))
                lo, hi = (EARLY, N_TILES) if rnd else (0, EARLY)
                v.tensor_scalar(tabi[rnd][:, 0, lo:hi], table_ps[0:1, 128 + lo:128 + hi], float(PAD_ROW), None,
                                ALU.add).then_inc(tab_ready, 1)
                v.tensor_copy(tabi[rnd][:, 1, lo:hi], table_ps[0:1, 128 + N_TILES + lo:128 + N_TILES + hi])\
                    .then_inc(tab_ready, 1)
                dve.wait_ge(tab_ready, 2 * rnd + 2)

            def take_rows(i, s):
                dve.wait_ge(rt_full, i + 1)
                turned = ps[4][:, 0:D].rearrange("p (k n) -> p k n", k=FT)
                if early(i):
                    v.tensor_copy(rT[s % 2], turned).then_inc(rt_dve, 1)
                else:
                    v.tensor_copy(rT_hi[s % 2], turned).then_inc(rt_hi, 1)
                    dve.wait_ge(rt_hi, i + (1 - EARLY))
                    v.tensor_tensor(rT_lo[s % 2], turned, rT_hi[s % 2].bitcast(F32), ALU.subtract).then_inc(rt_dve, 1)
                dve.wait_ge(added_ok, i + 1)
                v.tensor_copy(meta[s % 4][:, :].bitcast(I32), rows[s % 2][:, D:ROW].bitcast(I32)).then_inc(row_used, 1)

            def silu_mul(i, s):
                dve.wait_ge(th_done, i + 1)
                v.scalar_tensor_tensor(out=eth[s % 2], in0=eth[s % 2], scalar=1.0, in1=up_ps[s % 2][0][:, :],
                                       op0=ALU.add, op1=ALU.mult).then_inc(in_done, 1)

            def hidden(i, s):
                dve.wait_ge(up1_full, i + 1)
                dve.wait_ge(in_done, 2 * i + 5)
                dve.wait_ge(it_full, i + 1)
                v.tensor_tensor(ein[s % 2], eth[s % 2], up_ps[s % 2][1][:, :], ALU.mult).then_inc(in_done, 1)

            def weighted(i, s):
                e = dve.value_load(table(i)[0:1, 1, bass.ds(i, 1)], min_val=0, max_val=E - 1)
                dve.wait_ge(dn_full, i + 3)
                wait(dve, gbr_value(i, s))
                dve.wait_ge(added_ok, i + 3)
                v.scalar_tensor_tensor(out=ey[s % 2], in0=down_ps,
                                       scalar=meta[s % 4][:, bass.ds(e, 1)], in1=gbr[s % 2],
                                       op0=ALU.mult, op1=ALU.mult).then_inc(y_done, 1)

            def weights_lo(i, s):
                e = dve.value_load(table(i)[0:1, 1, bass.ds(i, 1)], min_val=0, max_val=E - 1)
                dve.wait_ge(w_hi_ready[0], i + (1 - EARLY))
                v.tensor_tensor(w_lo[0], expert_up(e, 0), w_hi[0].bitcast(F32), ALU.subtract)\
                    .then_inc(w_lo_ready[0], 1)

            def dve_step(i, s, hidden_made=False):
                const = isinstance(i, int)
                if not hidden_made and not (const and not 0 <= i - 1 < N_TILES):
                    hidden(i - 1, s - 1)
                if not (const and not 0 <= i - 2 < N_TILES):
                    weighted(i - 2, s - 2)
                if not (const and not 0 <= i + 1 < N_TILES):
                    take_rows(i + 1, s + 1)
                if not (const and not 0 <= i < N_TILES):
                    silu_mul(i, s)
                if not (const and not EARLY <= i + 1 < N_TILES):
                    weights_lo(i + 1, s + 1)

            b = B - 1
            dve.sem_inc(row_used, 2)
            dve.sem_inc(in_done, 4)
            dve.sem_inc(y_done, 2)
            tiles_of_experts(0)
            chunk_dve(b, 3, {0: [lambda: tiles_before(0)], 2: [lambda: tile_columns(0)]})
            table_rows(0)
            group_norm(b, between=lambda: take_rows(0, 0))
            take_rows(1, 1)
            gated(b)
            silu_mul(0, 0)
            hidden(0, 0)
            attention_out(b)
            wait(dve, tail.drains(b, "wo23"))
            dve.sem_inc(tail.drained["dve"], 2)
            silu_mul(1, 1)
            take_rows(2, 2)
            second_stats(b)
            hidden(1, 1)
            second_norm(b)
            for i in range(2, 8):
                dve_step(i, i, hidden_made=i == 2)
                if i == 3:
                    take_logits(b)
                    choose_top(b)
                    choose_places(b)
                    choose_weights(b)
                    dve.sem_inc(tail.drained["dve"], 1)
                elif i == 4:
                    places(b)
                    rows_of_tokens(b)
                    tiles_of_experts(1)
                elif i == 5:
                    tiles_before(1)
                elif i == 6:
                    tile_columns(1)
                elif i == 7:
                    table_rows(1)
            run_steps(dve, dve_step, first=8)

        @block.tensor
        def _(pe):
            mm, tr = nc.tensor.matmul, nc.tensor.transpose

            pe.wait_ge(silu_ready, 1)
            pe.wait_ge(const_ready, CONSTS)
            for k in range(FT):
                last = tr(ps[4][:, k * B:(k + 1) * B], c_t[:, k * P:(k + 1) * P], ident[0:B, 0:B])
            last.then_inc(setup_pe, 1)
            pe.wait_ge(silu_ready, 2)
            pe.wait_ge(wmod_in, 16)
            for m in range(2 * FT):
                for k in range(FT):
                    last = mm(ps[5][:, m * B:(m + 1) * B], wmod_s[:, k, m * P:(m + 1) * P], siluT[:, k, :],
                              start=k == 0, stop=k == FT - 1)
            last.then_inc(setup_pe, 1)
            pe.sem_inc(scored, 4)
            pe.sem_inc(pv_done, 4)
            pe.wait_ge(modT_ready, 2)

            def turn_x(b):
                for ft in range(FT):
                    n = f"hT{ft}"
                    if ft == 0:
                        pe.wait_ge(xn_ready, NC * b + NC)
                    wait(pe, front.free(b, n))
                    for t in range(NC):
                        last = tr(front.bank(n)[:, t * P:(t + 1) * P], xn[:, t, ft * P:(ft + 1) * P], ident[:, :])
                    last.then_inc(front.full, 1)

            def project(b, w, s, tiles=range(FT), between=None):
                for ft in tiles:
                    n = f"{w}{ft}"
                    wait(pe, front.free(b, n))
                    for k in range(FT):
                        if k and between is not None:
                            between()
                        last = mm(front.bank(n)[:, :], s[:, k, ft * P:(ft + 1) * P], hT[:, k, :],
                                  start=k == 0, stop=k == FT - 1)
                    last.then_inc(front.full, 1)

            def rows_k(b):
                wait(pe, front.drains(b, "k1"))
                for n, c0, m in (("kd01", 0, 2), ("kd2", 2, 1)):
                    wait(pe, front.free(b, n))
                    for c in range(m):
                        for ft in range(FT):
                            last = tr(front.bank(n)[:, c * D + ft * P:c * D + (ft + 1) * P],
                                      kT[:, ft, (c0 + c) * P:(c0 + c + 1) * P], ident[:, :])
                    last.then_inc(front.full, 1)

            def rows_v(b, n, t0):
                wait(pe, front.free(b, n))
                for t in range(2):
                    for k in range(FT):
                        last = mm(front.bank(n)[:, t * D:(t + 1) * D], hT[:, k, (t0 + t) * P:(t0 + t + 1) * P],
                                  wv_s[:, k, :], start=k == 0, stop=k == FT - 1)
                last.then_inc(front.full, 1)

            def chunk_pe(b, c, between=None, before_scores={}, before_values={}):
                cs = slice(c * P, (c + 1) * P)
                if c == 0:
                    pe.wait_ge(ro_ready, 2 * b + 2)
                    pe.wait_ge(qd_ready, 2 * b + 2)
                    wait(pe, front.drains(b, "kd2"))
                else:
                    if c == 1:
                        wait(pe, tail.drains(b, "st0"))
                        if isinstance(b, int) and b == 0:
                            pe.sem_inc(tail.full, 2)
                    else:
                        pe.wait_ge(state_up, 4 * b + 2 * (c - 1))
                    if c == 2:
                        wait(pe, front.drains(b, "v23"))
                        if isinstance(b, int) and b == 0:
                            pe.sem_inc(tail.full, 1)
                    for ft in range(FT):
                        mm(ret[ft][:, cs], state[:, ft, :], qd[:, ft, cs], start=True, stop=False,
                           skip_group_check=True)
                if c < NC - 1:
                    n = f"st{c}"
                    wait(pe, tail.free(b, n))
                    for ft in range(FT):
                        last = mm(tail.bank(n)[:, ft * P:(ft + 1) * P], kd[:, c, ft * P:(ft + 1) * P],
                                  heads(vx[:, c, ft * D:(ft + 1) * D], HPT // 2), start=True, stop=True)
                    last.then_inc(tail.full, 1)
                for g in range(4):
                    n, ft = 4 * c + g, g // 2
                    if g == 0:
                        pe.wait_ge(qx_pool, NC * b + (c + 1))
                    elif g == 2:
                        pe.wait_ge(qx_act, NC * HPT * b + HPT * (c + 1))
                    if g in before_scores:
                        before_scores[g]()
                    pe.wait_ge(masked, grp(b, n) + 1)
                    mm(sc[n % 2][:, :], kT[:, ft, cs], qx[:, ft, (g % 2) * 512:(g % 2 + 1) * 512],
                       start=True, stop=True).then_inc(scored, 1)
                if between is not None:
                    between()
                for g in range(4):
                    n, ft = 4 * c + g, g // 2
                    if g in before_values:
                        before_values[g]()
                    pe.wait_ge(masked, grp(b, n) + (1 + 2))
                    for i in range(4):
                        j, q = (4 * (g % 2) + i) // 2, i % 2
                        at = ft * D + j * 4 * DH + q * 2 * DH
                        last = mm(ret[ft][32 * j:32 * j + 32, cs], vx[:, c, at:at + 2 * DH],
                                  sm[:, g, i * P:(i + 1) * P], start=c == 0 and q == 0, stop=q == 1,
                                  skip_group_check=True)
                    last.then_inc(pv_done, 1)

            def average(b):
                pe.wait_ge(gn_stat, b + 1)
                wait(pe, tail.free(b, "gn"))
                mm(tail.bank("gn")[:, 0:2 * FT], blkavg[:, :], gmv[:, :, :].rearrange("p k m -> p (k m)"),
                   start=True, stop=True).then_inc(gn_full, 1)

            def average_dev(b):
                pe.wait_ge(gn_dev, b + 1)
                mm(tail.bank("gn")[:, 8:8 + FT], blkavg[:, :], gd2[:, :], start=True, stop=True)\
                    .then_inc(tail.full, 1)

            def out_rows(b):
                pe.wait_ge(wob_ready, b + 1)
                pe.wait_ge(prod_ready, 2 * b + 2)
                for n, t0 in (("wo01", 0), ("wo23", 2)):
                    wait(pe, tail.free(b, n))
                    for t in range(2):
                        for k in range(FT):
                            last = mm(tail.bank(n)[:, t * D:(t + 1) * D], ro[:, k, (t0 + t) * P:(t0 + t + 1) * P],
                                      wob[:, k, :], start=k == 0, stop=k == FT - 1)
                    last.then_inc(tail.full, 1)

            def turn_h2(b, tiles=range(FT)):
                pe.wait_ge(h2_ready, b + 1)
                for ft in tiles:
                    n = f"h2T{ft}"
                    wait(pe, tail.free(b, n))
                    if isinstance(b, int) and b == B - 1 and ft:
                        wait(pe, tail.drains(b, "h2T0"))
                    for t in range(NC):
                        last = tr(tail_bank(b, f"h2T{ft}")[:, t * P:(t + 1) * P], h2[:, t, ft * P:(ft + 1) * P], ident[:, :])
                    last.then_inc(tail.full, 1)

            def router(b):
                wait(pe, tail.free(b, "logits"))
                wait(pe, tail.drains(b, "h2T1"))
                for t in range(NC):
                    for k in range(FT):
                        last = mm(tail_bank(b, "logits")[:, t * E:(t + 1) * E], h2T[:, k, t * P:(t + 1) * P],
                                  gate_s[:, k, :], start=k == 0, stop=k == FT - 1)
                last.then_inc(tail.full, 1)

            def rank(b):
                wait(pe, tail.free(b, "rank"))
                pe.wait_ge(msk_ready, b + 1)
                mv = msk[:, :, :].rearrange("p t e -> p (t e)")
                mm(tail_bank(b, "rank")[:, 0:NC * E], tri[:, :], mv, start=True, stop=True)
                mm(tail_bank(b, "rank")[:, 64:64 + NC * E], ones[:, :], mv, start=True, stop=True).then_inc(tail.full, 1)

            turn_x(0)
            for m in range(2):
                for k in range(FT):
                    last = mm(ps[2 + m][0:B, :], siluT[:, k, :], wmod_s[:, k, 512 * (m + 1):512 * (m + 2)],
                              start=k == 0, stop=k == FT - 1)
            last.then_inc(setup_pe, 1)
            wait(pe, front.drains(0, "hT1"))
            pe.wait_ge(w_in, 16 * 4)
            project(0, "q", wq_s)
            project(0, "k", wk_s)
            project(0, "g", wg_s)
            rows_v(0, "v01", 0)
            rows_k(0)
            rows_v(0, "v23", 2)
            pe.wait_ge(setup_done, 1)
            for c in range(3):
                chunk_pe(0, c)
            wait(pe, tail.drains(0, "st2"))
            pe.sem_inc(tail.full, 1)
            pe.wait_ge(wo_in, 16 * 2)
            with pe.Fori(0, B - 1) as b:
                chunk_pe(b, 3, between=lambda: turn_x(b + 1))
                wait(pe, front.drains(b + 1, "hT1"))
                project(b + 1, "q", wq_s, [0])
                average(b)
                project(b + 1, "q", wq_s, [1], between=lambda: average_dev(b))
                project(b + 1, "k", wk_s)
                project(b + 1, "g", wg_s, [0])
                out_rows(b)
                project(b + 1, "g", wg_s, [1])
                rows_v(b + 1, "v01", 0)
                rows_k(b + 1)
                rows_v(b + 1, "v23", 2)
                chunk_pe(b + 1, 0)
                turn_h2(b)
                chunk_pe(b + 1, 1, between=lambda: router(b))
                chunk_pe(b + 1, 2, between=lambda: rank(b))

            def counts(rnd):
                if rnd:
                    pe.wait_ge(pad_ready, 1)
                else:
                    pe.wait_ge(pad_early, 1)
                rows_so_far = carry[:, 0, :] if rnd else carry_early[:, :]
                mm(table_ps[0:E, 0:1], rows_so_far, ident[:, 0:1], start=True, stop=True).then_inc(table_pe, 1)

            def firsts(rnd):
                pe.wait_ge(tls_ready, 2 * rnd + 1)
                mm(table_ps[0:E, 1:2], tri[0:E, 0:E], tls[:, :], start=True, stop=True).then_inc(table_pe, 1)

            def fold(rnd):
                pe.wait_ge(tls_ready, 2 * rnd + 2)
                mm(table_ps[0:1, 128:128 + 2 * N_TILES], ones[0:E, 0:1], tab[:, :, :].rearrange("e a n -> e (a n)"),
                   start=True, stop=True).then_inc(table_pe, 1)

            def weights(e, o, n):
                return we[:, bass.ds(e, 1), o:o + n].rearrange("p a n -> p (a n)")

            def turn_rows(i, s):
                pe.wait_ge(row_in[s % 2], 16 * row_loads(i, s))
                if not (isinstance(i, int) and i < 1):
                    pe.wait_ge(rt_dve, i)
                for k in range(FT):
                    last = tr(ps[4][:, k * P:(k + 1) * P], rows[s % 2][:, k * P:(k + 1) * P], ident[:, :])
                last.then_inc(rt_full, 1)

            def up_early(i, s, e, which, done):
                for k in range(FT):
                    last = mm(up_ps[s % 2][which][:, :], rT[s % 2][:, k, :],
                              weights(e, (which * FT + k) * F, F), start=k == 0, stop=k == FT - 1)
                last.then_inc(done, 1)

            def up(i, s, which, done):
                dst = up_ps[s % 2][which][:, :]
                pe.wait_ge(w_hi_ready[which], i + (1 - EARLY))
                for k in range(FT):
                    mm(dst, rT_hi[s % 2][:, k, :], w_hi[which][:, k * F:(k + 1) * F], start=k == 0, stop=False)
                    mm(dst, rT_lo[s % 2][:, k, :], w_hi[which][:, k * F:(k + 1) * F], start=False, stop=False)
                pe.wait_ge(w_lo_ready[which], i + (1 - EARLY))
                for k in range(FT):
                    last = mm(dst, rT_hi[s % 2][:, k, :], w_lo[which][:, k * F:(k + 1) * F],
                              start=False, stop=k == FT - 1)
                last.then_inc(done, 1)

            def turn_hidden(i, s):
                pe.wait_ge(in_done, 2 * i + 6)
                pe.wait_ge(it_act, i + 1)
                for k in range(KF):
                    last = tr(ps[5][:, k * P:(k + 1) * P], ein[s % 2][:, k * P:(k + 1) * P], ident[:, :])
                last.then_inc(it_full, 1)

            def down(i, s):
                e = pe.value_load(table(i)[0:1, 1, bass.ds(i, 1)], min_val=0, max_val=E - 1)
                pe.wait_ge(it_act, i + 2)
                pe.wait_ge(y_done, i + 2)
                for k in range(KF):
                    last = mm(down_ps, eit[s % 2][:, k, :], weights(e, 2 * FT * F + k * D, D),
                              start=k == 0, stop=k == KF - 1)
                last.then_inc(dn_full, 1)

            def upward(i, s, e, which, full):
                if early(i):
                    up_early(i, s, e, which, full)
                else:
                    up(i, s, which, full)

            def pe_step(i, s, between=None, before_second=None, before_down=None):
                e = None
                const = isinstance(i, int)
                here = not (const and i >= N_TILES)
                before = not (const and not 0 <= i - 1 < N_TILES)
                if here:
                    if early(i):
                        e = pe.value_load(table(i)[0:1, 1, bass.ds(i, 1)], min_val=0, max_val=E - 1)
                    pe.wait_ge(rt_dve, i + 1)
                    pe.wait_ge(in_done, 2 * i + 2)
                    upward(i, s, e, 0, up0_full)
                if between is not None:
                    between()
                if before:
                    turn_hidden(i - 1, s - 1)
                if not (const and i + 1 >= N_TILES):
                    turn_rows(i + 1, s + 1)
                if before_second is not None:
                    before_second()
                if here:
                    upward(i, s, e, 1, up1_full)
                if before_down is not None:
                    before_down()
                if before:
                    down(i - 1, s - 1)

            b = B - 1
            chunk_pe(b, 3, before_scores={2: lambda: counts(0), 3: lambda: firsts(0)},
                     before_values={2: lambda: fold(0)})
            pe.wait_ge(tab_ready, 2)
            pe.wait_ge(we_in, 16 * 3 * E)
            pe.sem_inc(it_full, 2)
            pe.sem_inc(dn_full, 2)
            average(b)
            turn_rows(0, 0)
            average_dev(b)
            pe_step(0, 0)
            out_rows(b)

            def out_drained():
                wait(pe, tail.drains(b, "wo23"))
                pe.sem_inc(tail.full, 1)

            pe_step(1, 1, before_down=out_drained)
            pe_step(2, 2)

            def last_router():
                wait(pe, tail.drains(b, "h2T1"))
                pe.sem_inc(tail.full, 1)
                router(b)

            pe_step(3, 3, between=lambda: turn_h2(b, [0]), before_second=lambda: turn_h2(b, [1]),
                    before_down=last_router)

            def last_rank():
                wait(pe, tail.drains(b, "logits"))
                pe.sem_inc(tail.full, 1)
                rank(b)

            pe_step(4, 4, between=last_rank)
            pe_step(5, 5, between=lambda: counts(1))
            pe_step(6, 6, between=lambda: firsts(1))
            pe_step(7, 7, between=lambda: fold(1))
            run_steps(pe, pe_step, first=8)


_INS = ["attn_x", "attn_wq", "attn_bq", "attn_wk", "attn_bk", "attn_wv", "attn_bv", "attn_wg", "attn_bg", "attn_wo",
        "attn_bo", "attn_gn_w", "attn_gn_b", "attn_gamma", "ffn_gate_kernel", "ffn_w0_kernel", "ffn_w1_kernel",
        "ffn_wo_kernel", "c", "wmod"]


def kernel(**inputs):
    import numpy as _np
    import concourse.bacc as _bacc
    from concourse import mybir as _mybir
    from concourse.bass_utils import run_bass_kernel_spmd as _run

    nc = _bacc.Bacc("TRN2", target_bir_lowering=False, num_devices=1)
    arrays, args = {}, []
    for name in _INS:
        a = _np.ascontiguousarray(inputs[f"L0_{name}"])
        arrays[f"in_{name}_dram"] = a
        args.append(nc.dram_tensor(f"in_{name}_dram", a.shape, _mybir.dt.from_np(a.dtype), kind="ExternalInput").ap())
    o = nc.dram_tensor("out_0_dram", [NTOK + P, D], F32, kind="ExternalOutput").ap()
    adaln_block(nc, *args, o)
    r = _run(nc, [arrays], core_ids=[0])
    return r.results[0]["out_0_dram"][:NTOK].reshape(B, S, D)
```
